# Optimizing a Trainium2 kernel written in Bass

```python
import numpy as np
import jax
import jax.numpy as jnp

def _softmax(x, axis=-1):
    return jax.nn.softmax(x, axis=axis)

def _gelu(x):
    return jax.nn.gelu(x, approximate=True)

def _silu(x):
    return jax.nn.silu(x)

def _sigmoid(x):
    return jax.nn.sigmoid(x)

def _layernorm(x, axis=-1, eps=1e-05):
    m = jnp.mean(x, axis=axis, keepdims=True)
    v = jnp.var(x, axis=axis, keepdims=True)
    return (x - m) / jnp.sqrt(v + eps)

def _scatter_add(tgt, idx, src, axis=0):
    return tgt.at[idx].add(src)

def _segment_sum(src, seg, n):
    return jax.ops.segment_sum(src, seg, n)
kernel_name = 'mk_adaln_d1_jaxref_r4_b06c38'

def setup_inputs(seed: int=0):
    np.random.seed(seed)
    _w = jnp.asarray

    def _L0_attn_setup():
        import jax, jax.numpy as jnp
        import numpy as np
        B, S, D = (2, 512, 512)
        H = 16
        HD = D // H
        key = jax.random.key(seed)
        k1, k2, k3 = jax.random.split(key, 3)
        x = jax.random.normal(k1, (B, S, D), dtype=jnp.float32)
        w_qkv = jax.random.normal(k2, (D, 3 * D), dtype=jnp.float32) * (1.0 / np.sqrt(D))
        b_qkv = jnp.zeros((3 * D,), dtype=jnp.float32)
        w_out = jax.random.normal(k3, (D, D), dtype=jnp.float32) * (1.0 / np.sqrt(D))
        b_out = jnp.zeros((D,), dtype=jnp.float32)
        return {'x': x, 'w_qkv': w_qkv, 'b_qkv': b_qkv, 'w_out': w_out, 'b_out': b_out}
    _L0_attn_in = _L0_attn_setup()

    def _L0_ffn_setup():
        import jax, jax.numpy as jnp
        import numpy as np
        _FP4_LUT = jnp.array([0.0, 0.5, 1.0, 1.5, 2.0, 3.0, 4.0, 6.0, -0.0, -0.5, -1.0, -1.5, -2.0, -3.0, -4.0, -6.0], dtype=jnp.float32)
        GROUP_SIZE = 128
        EPS = 1e-06

        def _dequant_fp4(packed_i32, scales_f16, group_size):
            out_f, in_p = packed_i32.shape
            w = packed_i32.astype(jnp.uint32)
            shifts = jnp.arange(8, dtype=jnp.uint32) * 4
            nib = w[:, :, None] >> shifts & jnp.uint32(15)
            vals = _FP4_LUT[nib.astype(jnp.int32)].reshape(out_f, in_p * 8)
            s = scales_f16.astype(jnp.float32).T
            s_full = jnp.repeat(s, group_size, axis=1)
            return vals * s_full
        key = jax.random.key(seed)
        k1, k2, k3, k4, k5 = jax.random.split(key, 5)
        B, S, H, I = (4, 512, 512, 1408)
        x = jax.random.normal(k1, (B, S, H), dtype=jnp.float32)
        gate_up_packed = jax.random.randint(k2, (2 * I, H // 8), 0, 2147483647, dtype=jnp.int32)
        gate_up_scales = jax.random.uniform(k3, (H // GROUP_SIZE, 2 * I), dtype=jnp.float32).astype(jnp.float16)
        down_packed = jax.random.randint(k4, (H, I // 8), 0, 2147483647, dtype=jnp.int32)
        down_scales = jax.random.uniform(k5, (I // GROUP_SIZE, H), dtype=jnp.float32).astype(jnp.float16)
        return {'x': x, 'gate_up_packed': gate_up_packed, 'gate_up_scales': gate_up_scales, 'down_packed': down_packed, 'down_scales': down_scales}
    _L0_ffn_in = _L0_ffn_setup()
    _L0_c = _w((lambda *s: np.random.randn(*s).astype(np.float32) * 0.05)(1, 512))
    _L0_wmod = _w((lambda *s: np.random.randn(*s).astype(np.float32) * 0.05)(512, 6 * 512) * 512 ** (-0.5))
    _d = {'L0_attn_x': _L0_attn_in['x'], 'L0_attn_w_qkv': _L0_attn_in['w_qkv'], 'L0_attn_b_qkv': _L0_attn_in['b_qkv'], 'L0_attn_w_out': _L0_attn_in['w_out'], 'L0_attn_b_out': _L0_attn_in['b_out'], 'L0_ffn_gate_up_packed': _L0_ffn_in['gate_up_packed'], 'L0_ffn_gate_up_scales': _L0_ffn_in['gate_up_scales'], 'L0_ffn_down_packed': _L0_ffn_in['down_packed'], 'L0_ffn_down_scales': _L0_ffn_in['down_scales'], 'L0_c': _L0_c, 'L0_wmod': _L0_wmod}
    _x0 = _d['L0_attn_x']
    _d['L0_attn_x'] = jax.random.normal(jax.random.fold_in(jax.random.key(seed), 1), (1, 2048, 512), dtype=_x0.dtype)
    del _x0
    return _d

def reference(L0_attn_x, L0_attn_w_qkv, L0_attn_b_qkv, L0_attn_w_out, L0_attn_b_out, L0_ffn_gate_up_packed, L0_ffn_gate_up_scales, L0_ffn_down_packed, L0_ffn_down_scales, L0_c, L0_wmod):

    def _L0_attn_ref(x, w_qkv, b_qkv, w_out, b_out):
        import jax, jax.numpy as jnp
        import numpy as np
        B, S, D = (2, 512, 512)
        H = 16
        HD = D // H
        batch, seq_len, channels = x.shape
        qkv = x @ w_qkv + b_qkv
        q, k, v = jnp.split(qkv, 3, axis=-1)

        def heads(t):
            return t.reshape(batch, seq_len, H, HD).transpose(0, 2, 1, 3)
        q, k, v = (heads(q), heads(k), heads(v))
        scale = 1.0 / np.sqrt(HD).astype(np.float32)
        attn = jnp.einsum('bhqd,bhkd->bhqk', q, k) * scale
        causal = jnp.tril(jnp.ones((seq_len, seq_len), dtype=bool))
        attn = jnp.where(causal, attn, -jnp.inf)
        attn = jax.nn.softmax(attn, axis=-1)
        y = jnp.einsum('bhqk,bhkd->bhqd', attn, v)
        y = y.transpose(0, 2, 1, 3).reshape(batch, seq_len, channels)
        return y @ w_out + b_out

    def _L0_ffn_ref(x, gate_up_packed, gate_up_scales, down_packed, down_scales):
        import jax, jax.numpy as jnp
        import numpy as np
        _FP4_LUT = jnp.array([0.0, 0.5, 1.0, 1.5, 2.0, 3.0, 4.0, 6.0, -0.0, -0.5, -1.0, -1.5, -2.0, -3.0, -4.0, -6.0], dtype=jnp.float32)
        GROUP_SIZE = 128
        EPS = 1e-06

        def _dequant_fp4(packed_i32, scales_f16, group_size):
            out_f, in_p = packed_i32.shape
            w = packed_i32.astype(jnp.uint32)
            shifts = jnp.arange(8, dtype=jnp.uint32) * 4
            nib = w[:, :, None] >> shifts & jnp.uint32(15)
            vals = _FP4_LUT[nib.astype(jnp.int32)].reshape(out_f, in_p * 8)
            s = scales_f16.astype(jnp.float32).T
            s_full = jnp.repeat(s, group_size, axis=1)
            return vals * s_full
        I = gate_up_packed.shape[0] // 2
        w_gu = _dequant_fp4(gate_up_packed, gate_up_scales, GROUP_SIZE)
        w_down = _dequant_fp4(down_packed, down_scales, GROUP_SIZE)
        gate_up = jnp.einsum('bsh,oh->bso', x, w_gu)
        gate, up = (gate_up[..., :I], gate_up[..., I:])
        h = jax.nn.silu(gate) * up
        y = jnp.einsum('bsi,hi->bsh', h, w_down)
        rms = jnp.sqrt(jnp.mean(y * y, axis=-1, keepdims=True) + EPS)
        return y / rms
    x = L0_attn_x
    mod = (_silu(L0_c) @ L0_wmod).reshape(L0_c.shape[0], 6, 1, -1)
    sa, ca, ga, sb, cb, gb = (mod[:, 0], mod[:, 1], mod[:, 2], mod[:, 3], mod[:, 4], mod[:, 5])
    ga = (2 * (ga >= 0) - 1) * jnp.maximum(jnp.abs(ga), 0.25)
    gb = (2 * (gb >= 0) - 1) * jnp.maximum(jnp.abs(gb), 0.25)
    h = _layernorm(x, axis=-1) * (1 + ca) + sa
    x = x + ga * _L0_attn_ref(h, L0_attn_w_qkv, L0_attn_b_qkv, L0_attn_w_out, L0_attn_b_out)
    h = _layernorm(x, axis=-1) * (1 + cb) + sb
    x = x + gb * _L0_ffn_ref(h, L0_ffn_gate_up_packed, L0_ffn_gate_up_scales, L0_ffn_down_packed, L0_ffn_down_scales)
    return x

_drawn_inputs = setup_inputs


def setup_inputs(seed=0):
    import zlib

    import numpy as np

    out = dict(_drawn_inputs(seed))
    spreads = {'L0_attn_b_qkv': (0.0, 0.3), 'L0_attn_b_out': (0.0, 0.327)}
    factors = {}
    for name, (base, spread) in spreads.items():
        noise = np.random.default_rng([zlib.crc32(name.encode()), seed]).standard_normal(out[name].shape)
        drawn = base * np.exp(spread * noise) if base else spread * noise
        out[name] = jnp.asarray(drawn.astype(out[name].dtype))
    for name, factor in factors.items():
        out[name] = (out[name] * factor).astype(out[name].dtype)
    return out
```

```python
from contextlib import ExitStack

import concourse.bass as bass
from concourse import mybir

P = 128
S, D, H = 2048, 512, 16
HD = D // H
KT = D // P
C = 512
TC = C // P
NC = S // C
ST = S // P
HG = P // HD
NG = H // HG
NI = 1408
IT = NI // P
GU = 2 * NI
WG = 16
NIB = 8
DN = IT * D // NG
PC = GU + DN
EPS = 1e-5
RMS_EPS = 1e-6
MASKED = -1e30
M_UNIT = 64.0
SA, CA, GA, SB, CB, GB = range(6)

F32, F32R = mybir.dt.float32, mybir.dt.float32r
F16, BF16, I32 = mybir.dt.float16, mybir.dt.bfloat16, mybir.dt.int32
ALU = mybir.AluOpType
ACT = mybir.ActivationFunctionType
X = mybir.AxisListType.X


def phase_a(nc, io, keep):
    QK = 2 * KT
    QS = 4
    with ExitStack() as ctx:
        def sb(name, shape, dt=F32):
            return ctx.enter_context(nc.sbuf_tensor(name, shape, dt))

        def sem(name):
            return ctx.enter_context(nc.semaphore(name))

        w_stage = sb("w_stage", [P, KT, 3 * D])
        w_hi = sb("w_hi", [P, KT, 3 * D], F32R)
        w_lo = sb("w_lo", [P, KT, 3 * D], F32R)
        mod_w = sb("mod_w", [P, 2, KT, D])
        mod_junk = sb("mod_junk", [P, D])
        c_row = sb("c_row", [P, D])
        mods = sb("mods", [P, 6, KT])
        absg = sb("absg", [P, 2, KT])
        bias_qk = sb("bias_qk", [P, QK])
        bias_v = sb("bias_v", [P, D])
        eps = sb("eps_a", [P, 1])
        xs = sb("xs", [P, TC, D])
        stats = sb("stats_a", [P, TC, 6])
        mv = sb("mv_a", [P, TC, 2])
        rstd = sb("rstd_a", [P, 2, TC])
        xn = sb("xn_a", [P, TC, D])
        ht = sb("ht_a", [P, KT, C])
        h_hi = sb("h_hi_a", [P, KT, C], F32R)
        h_lo = sb("h_lo_a", [P, KT, C], F32R)
        qf = sb("qf", [P, 2, C])
        qs = sb("qs", [P, QS, 2, C], F16)
        vf = sb("vf", [P, 2, D])
        tp = [ctx.enter_context(nc.psum_tensor(f"tp_a{f}", [P, C], F32)) for f in range(KT)]
        qk_ps = [ctx.enter_context(nc.psum_tensor(f"qk_ps{n}", [P, C], F32)) for n in range(2)]
        v_ps = [ctx.enter_context(nc.psum_tensor(f"v_ps{n}", [P, D], F32)) for n in range(2)]

        w_loaded = [sem(f"w_loaded{k}") for k in range(KT)]
        small_loaded = sem("small_loaded")
        mod_loaded = [sem(f"mod_loaded{n}") for n in range(2)]
        x_loaded = sem("x_loaded")
        silu_done = sem("silu_done")
        mod_done = sem("mod_done")
        clamp_step = sem("clamp_step")
        masks_set = sem("masks_set")
        masks_cut = sem("masks_cut")
        const_done = sem("const_done_a")
        w_hi_done = sem("w_hi_done")
        w_lo_done = sem("w_lo_done")
        stats_done = sem("stats_done_a")
        stats_seen = sem("stats_seen_a")
        mv_done = sem("mv_done_a")
        sd_done = sem("sd_done_a")
        rstd_done = sem("rstd_done_a")
        xn_done = sem("xn_done_a")
        tp_done = sem("tp_done_a")
        ht_done = sem("ht_done_a")
        h_hi_done = sem("h_hi_done_a")
        h_lo_done = sem("h_lo_done_a")
        qk_ready = sem("qk_ready")
        qk_evac = sem("qk_evac")
        qk_hi_done = sem("qk_hi_done")
        qk_lo_done = sem("qk_lo_done")
        v_ready = sem("v_ready")
        v_evac = sem("v_evac")
        qk_out = [sem(f"qk_out{n}") for n in range(QS)]
        v_out = [sem(f"v_out{n}") for n in range(2)]

        MOD_ORDER = [SA, CA, GA, SB, CB, GB]
        UNITS = [("qk", 0), ("qk", 1), ("v", 0), ("qk", 2), ("qk", 3), ("v", 1),
                 ("qk", 4), ("qk", 5), ("v", 2), ("qk", 6), ("qk", 7), ("v", 3)]
        block = ctx.enter_context(nc.Block())

        @block.sync
        def _(sp):
            for started in (*qk_out, *v_out):
                sp.sem_inc(started, 1)

            def load_x(i):
                sp.dma_start(xs[:, :, :], io["x"][bass.ds(i * C, C), :]
                             .rearrange("(t p) d -> p t d", p=P)).then_inc(x_loaded, 16)

            load_x(0)

            def chunk(i, more):
                if more:
                    sp.wait_ge(xn_done, i * TC + TC)
                    load_x(i + 1)
                for kind, n in UNITS:
                    if kind == "qk":
                        sp.wait_ge(qk_lo_done, i * QK + n + 2)
                        sp.dma_start(io["qk_parts"][n].rearrange("l p s -> p l s")[:, :, bass.ds(i * C, C)],
                                     qs[:, n % QS, :, :]).then_inc(qk_out[n % QS], 16)
                    else:
                        sp.wait_ge(v_evac, i * TC + n + 3)
                        sp.dma_start(io["v_rows"][bass.ds(i * C + n * P, P), :],
                                     vf[:, n % 2, :]).then_inc(v_out[n % 2], 16)

            with sp.Fori(0, NC - 1) as i:
                chunk(i, True)
            chunk(NC - 1, False)
            for n in range(QS):
                sp.wait_ge(qk_out[n], 16 * NC * QK // QS + 1)
            for n in range(2):
                sp.wait_ge(v_out[n], 16 * NC * TC // 2 + 1)

        @block.gpsimd
        def _(pool):
            ident, ident16, identb = keep["ident"], keep["ident16"], keep["identb"]
            mask_qk, mask_kq = keep["mask_qk"], keep["mask_kq"]
            nc.gpsimd.memset(eps[:, :], EPS).then_inc(const_done, 1)
            for t in (ident, ident16, identb, mask_qk, mask_kq):
                nc.gpsimd.memset(t[:, :], 0.0).then_inc(masks_set, 1)
            pool.wait_ge(masks_set, 5)
            for t in (ident, ident16, identb):
                nc.gpsimd.affine_select(out=t[:, :], in_=t[:, :], compare_op=ALU.not_equal, fill=1.0, base=0,
                                        pattern=[[-1, P]], channel_multiplier=1).then_inc(masks_cut, 1)
            nc.gpsimd.affine_select(out=mask_qk[:, :], in_=mask_qk[:, :], compare_op=ALU.is_ge, fill=MASKED, base=0,
                                    pattern=[[-1, P]], channel_multiplier=1).then_inc(masks_cut, 1)
            nc.gpsimd.affine_select(out=mask_kq[:, :], in_=mask_kq[:, :], compare_op=ALU.is_ge, fill=MASKED, base=0,
                                    pattern=[[1, P]], channel_multiplier=-1).then_inc(masks_cut, 1)

        @block.scalar
        def _(act):
            act.sem_inc(qk_evac, 2)
            act.sem_inc(ht_done, 1)
            act.dma_start(c_row[:, :], io["c"].partition_broadcast(P)).then_inc(small_loaded, 16)
            act.dma_start(bias_qk[:, :], io["bias_qk"]).then_inc(small_loaded, 16)
            act.dma_start(bias_v[:, :], io["bias_v"].partition_broadcast(P)).then_inc(small_loaded, 16)

            def load_mod(n):
                act.dma_start(mod_w[:, n % 2, :, :], io["wmod"][MOD_ORDER[n]].rearrange("f p k -> p f k"))\
                   .then_inc(mod_loaded[n % 2], 16)

            load_mod(0)
            load_mod(1)
            for k in range(KT):
                act.dma_start(w_stage[:, k, :], io["w_qkv"][k]).then_inc(w_loaded[k], 16)
            act.wait_ge(small_loaded, 48)
            nc.scalar.activation(c_row[:, :], c_row[:, :], ACT.Silu).then_inc(silu_done, 1)
            nc.scalar.preload_act_table(ACT.Sqrt)

            def deviation(i):
                act.wait_ge(mv_done, i * TC + TC)
                nc.scalar.activation(rstd[:, 0, :], mv[:, :, 1], ACT.Sqrt, bias=eps[:, :]).then_inc(sd_done, 1)

            def modulate(i):
                for f in range(KT):
                    act.wait_ge(tp_done, i * KT + f + 2)
                    act.wait_ge(h_lo_done, i * KT + 1)
                    nc.scalar.activation(ht[:, f, :], tp[f][:, :], ACT.Identity, bias=mods[:, SA, f:f + 1],
                                         scale=mods[:, CA, f:f + 1]).then_inc(ht_done, 1)

            act.wait_ge(const_done, 1)
            deviation(0)
            for k in range(KT):
                act.wait_ge(w_loaded[k], 16)
                nc.scalar.activation(w_hi[:, k, :], w_stage[:, k, :], ACT.Copy).then_inc(w_hi_done, 1)
            act.wait_ge(mod_done, 2)
            modulate(0)
            for n in range(2, 6):
                act.wait_ge(mod_done, n - 1)
                load_mod(n)

            def chunk(i, more):
                if more:
                    deviation(i + 1)
                for n in range(QK):
                    act.wait_ge(qk_ready, i * QK + n + 2)
                    if n >= 2:
                        act.wait_ge(qk_lo_done, i * QK + n)
                    else:
                        act.wait_ge(qk_lo_done, i * QK + 1)
                    nc.scalar.activation(qf[:, n % 2, :], qk_ps[n % 2][:, :], ACT.Identity,
                                         bias=bias_qk[:, n:n + 1],
                                         scale=HD ** -0.5 if n < KT else 1.0).then_inc(qk_evac, 1)
                if more:
                    modulate(i + 1)

            act.wait_ge(clamp_step, 1)
            with act.Fori(0, NC - 1) as i:
                chunk(i, True)
            chunk(NC - 1, False)

        @block.vector
        def _(dve):
            dve.sem_inc(v_evac, 2)
            dve.sem_inc(h_lo_done, 1)
            dve.sem_inc(qk_lo_done, 1)

            def normalize(i):
                dve.wait_ge(x_loaded, i * 16 + 16)
                for t in range(TC):
                    nc.vector.bn_stats(stats[:, t, :], xs[:, t, :]).then_inc(stats_done, 1)
                for t in range(TC):
                    dve.wait_ge(stats_done, i * TC + t + 1)
                    dve.sem_inc(stats_seen, 1)
                    nc.vector.bn_aggr(mv[:, t, :], stats[:, t, :]).then_inc(mv_done, 1)
                dve.wait_ge(sd_done, i + 1)
                nc.vector.reciprocal(rstd[:, 1, :], rstd[:, 0, :]).then_inc(rstd_done, 1)
                dve.wait_ge(rstd_done, i + 1)
                dve.wait_ge(tp_done, i * KT + 1)
                for t in range(TC):
                    nc.vector.tensor_scalar(xn[:, t, :], xs[:, t, :], mv[:, t, 0:1], rstd[:, 1, t:t + 1],
                                            ALU.subtract, ALU.mult).then_inc(xn_done, 1)

            def split_h(i):
                dve.wait_ge(qk_ready, i * QK + 1)
                dve.wait_ge(v_ready, i * TC + 1)
                for f in range(KT):
                    dve.wait_ge(ht_done, i * KT + f + 2)
                    nc.vector.tensor_copy(h_hi[:, f, :], ht[:, f, :]).then_inc(h_hi_done, 1)
                for f in range(KT):
                    dve.wait_ge(h_hi_done, i * KT + f + 1)
                    nc.vector.tensor_tensor(h_lo[:, f, :], ht[:, f, :], h_hi[:, f, :].bitcast(F32),
                                            ALU.subtract).then_inc(h_lo_done, 1)

            products = [0]

            def modulation(n):
                m = MOD_ORDER[n]
                dve.wait_ge(mod_loaded[n % 2], 16 * (n // 2) + 16)
                for f in range(KT):
                    if products[0]:
                        dve.wait_ge(clamp_step, products[0])
                    products[0] += 1
                    last = nc.vector.scalar_tensor_tensor(
                        out=mod_junk[:, :], in0=mod_w[:, n % 2, f, :], scalar=1.0, in1=c_row[:, :],
                        op0=ALU.mult, op1=ALU.mult, accum_out=mods[:, m, f:f + 1]).then_inc(clamp_step, 1)
                dve.wait_ge(clamp_step, products[0])
                if m in (CA, CB):
                    nc.vector.tensor_scalar(mods[:, m, :], mods[:, m, :], 1.0, None, ALU.add).then_inc(mod_done, 1)
                elif m in (GA, GB):
                    g = 0 if m == GA else 1
                    nc.vector.scalar_tensor_tensor(out=absg[:, g, :], in0=mods[:, m, :], scalar=-1.0,
                                                   in1=mods[:, m, :], op0=ALU.mult, op1=ALU.max)\
                      .then_inc(clamp_step, 1)
                    dve.wait_ge(clamp_step, products[0] + 1)
                    nc.vector.tensor_scalar(absg[:, g, :], absg[:, g, :], 0.25, None, ALU.max)\
                      .then_inc(clamp_step, 1)
                    nc.vector.tensor_scalar(mods[:, m, :], mods[:, m, :], 0.0, 2.0, ALU.is_ge, ALU.mult)\
                      .then_inc(clamp_step, 1)
                    products[0] += 3
                    dve.wait_ge(clamp_step, products[0])
                    nc.vector.scalar_tensor_tensor(out=keep["gates"][:, g, :], in0=mods[:, m, :], scalar=-1.0,
                                                   in1=absg[:, g, :], op0=ALU.add, op1=ALU.mult)\
                      .then_inc(mod_done, 1)
                else:
                    nc.vector.tensor_scalar(mods[:, m, :], mods[:, m, :], 1.0, None, ALU.mult).then_inc(mod_done, 1)
                if m in (SB, CB):
                    dve.wait_ge(mod_done, n + 1)
                    nc.vector.tensor_copy(keep["ffn_mod"][:, m - SB, :], mods[:, m, :]).then_inc(clamp_step, 1)
                    products[0] += 1

            normalize(0)
            dve.wait_ge(small_loaded, 48)
            nc.vector.tensor_scalar(bias_qk[:, 0:KT], bias_qk[:, 0:KT], HD ** -0.5, None, ALU.mult)\
              .then_inc(clamp_step, 1)
            products[0] += 1
            dve.wait_ge(silu_done, 1)
            modulation(0)
            modulation(1)
            for k in range(KT):
                dve.wait_ge(w_hi_done, k + 1)
                nc.vector.tensor_tensor(w_lo[:, k, :], w_stage[:, k, :], w_hi[:, k, :].bitcast(F32),
                                        ALU.subtract).then_inc(w_lo_done, 1)
            split_h(0)
            for n in range(2, 6):
                modulation(n)

            def chunk(i, more):
                if more:
                    normalize(i + 1)
                for kind, n in UNITS:
                    if kind == "qk":
                        dve.wait_ge(qk_evac, i * QK + n + 3)
                        dve.wait_ge(qk_out[n % QS], i * (16 * QK // QS) + 16 * (n // QS) + 1)
                        nc.vector.tensor_copy(qs[:, n % QS, 0, :], qf[:, n % 2, :]).then_inc(qk_hi_done, 1)
                        dve.wait_ge(qk_hi_done, i * QK + n + 1)
                        nc.vector.tensor_tensor(qs[:, n % QS, 1, :], qf[:, n % 2, :], qs[:, n % QS, 0, :],
                                                ALU.subtract).then_inc(qk_lo_done, 1)
                    else:
                        dve.wait_ge(v_ready, i * TC + n + 2)
                        dve.wait_ge(v_out[n % 2], i * (16 * TC // 2) + 16 * (n // 2) + 1)
                        nc.vector.tensor_tensor(vf[:, n % 2, :], v_ps[n % 2][:, :], bias_v[:, :],
                                                ALU.add).then_inc(v_evac, 1)
                if more:
                    split_h(i + 1)

            with dve.Fori(0, NC - 1) as i:
                chunk(i, True)
            chunk(NC - 1, False)

        @block.tensor
        def _(pe):
            pe.sem_inc(tp_done, 1)
            pe.sem_inc(qk_ready, 1)
            pe.sem_inc(v_ready, 1)

            def transposes(i):
                pe.wait_ge(xn_done, i * TC + TC)
                for f in range(KT):
                    pe.wait_ge(ht_done, i * KT + 1)
                    for t in range(TC):
                        last = nc.tensor.transpose(tp[f][:, t * P:(t + 1) * P], xn[:, t, f * P:(f + 1) * P],
                                                   keep["ident"][:, :])
                    last.then_inc(tp_done, 1)

            def project(i, kind, n):
                if kind == "qk":
                    pe.wait_ge(qk_evac, i * QK + n + 1)
                else:
                    pe.wait_ge(v_evac, i * TC + n + 1)
                for f in range(KT):
                    if kind == "qk":
                        cols = slice(n * P, (n + 1) * P)
                        parts = [(w_hi[:, f, cols], h_hi[:, f, :]), (w_lo[:, f, cols], h_hi[:, f, :]),
                                 (w_hi[:, f, cols], h_lo[:, f, :])]
                        out = qk_ps[n % 2]
                    else:
                        rows = slice(n * P, (n + 1) * P)
                        wv = slice(2 * D, 3 * D)
                        parts = [(h_hi[:, f, rows], w_hi[:, f, wv]), (h_hi[:, f, rows], w_lo[:, f, wv]),
                                 (h_lo[:, f, rows], w_hi[:, f, wv])]
                        out = v_ps[n % 2]
                    for m, (stat, mov) in enumerate(parts):
                        last = nc.tensor.matmul(out[:, :], stat, mov, start=(f == 0 and m == 0),
                                                stop=(f == KT - 1 and m == 2))
                last.then_inc(qk_ready if kind == "qk" else v_ready, 1)

            def chunk(i, more):
                pe.wait_ge(h_lo_done, i * KT + KT + 1)
                for u, (kind, n) in enumerate(UNITS):
                    project(i, kind, n)
                    if more and u == len(UNITS) - 3:
                        transposes(i + 1)

            pe.wait_ge(masks_cut, 5)
            transposes(0)
            pe.wait_ge(w_lo_done, KT)
            with pe.Fori(0, NC - 1) as i:
                chunk(i, True)
            chunk(NC - 1, False)


def phase_b(nc, io, keep):
    PB = 4
    ROWM = 3 * HD
    PIECES = 6
    PW = PC // PIECES
    MAX_UNITS = [[(t, j, b) for t in range(TC) for j in range(HG) for b in range(c + 1)] for c in range(NC)]
    NMX = sum(len(u) for u in MAX_UNITS)
    STEPS = [TC * (c + 1) for c in range(NC)]
    NSTEP = sum(STEPS)
    NENTRY = 2 * (NSTEP + NC)

    def bank_width(c, t, b):
        return (t + 1) * P if b == c else C

    def order(c):
        units = MAX_UNITS[c + 1] if c + 1 < NC else []
        n = STEPS[c] - 1
        cut = [len(units) * k // n for k in range(n + 1)]
        return [units[cut[k]:cut[k + 1]] for k in range(n)] + [[]]

    with ExitStack() as ctx:
        def sb(name, shape, dt=F32):
            return ctx.enter_context(nc.sbuf_tensor(name, shape, dt))

        def sem(name):
            return ctx.enter_context(nc.semaphore(name))

        q_st = sb("q_st", [P, HG, S], F16)
        k_st = sb("k_st", [P, HG, S], F16)
        v_g = sb("v_g", [P, ST, P])
        ones = sb("ones", [P, HD])
        prob = sb("prob", [P, PB, 2, C])
        max_part = sb("max_part", [P, TC * HG, NC])
        row_max = sb("row_max", [P, TC * HG])
        max16 = sb("max16", [P, TC * HG], F16)
        recip = sb("recip", [P, C])
        y = sb("y", [P, 2, C])
        packed = sb("packed", [P, PC], I32)
        shift = sb("shift", [P, 1], I32)
        bits = sb("bits", [P, PW], I32)
        four = sb("four", [P, PW], I32)
        clip = sb("clip", [P, PW])
        wo_stage = sb("wo_stage", [P, D])
        sc_ps = [ctx.enter_context(nc.psum_tensor(f"sc_ps{n}", [P, 2, C], F32)) for n in range(2)]
        mx_ps = [ctx.enter_context(nc.psum_tensor(f"mx_ps{n}", [P, C], F32)) for n in range(2)]
        y_ps = ctx.enter_context(nc.psum_tensor("y_ps", [P, C], F32))
        sum_ps = ctx.enter_context(nc.psum_tensor("sum_ps", [P, C], F32))

        q_loaded = sem("q_loaded")
        k_loaded = sem("k_loaded")
        v_loaded = sem("v_loaded")
        packed_loaded = sem("packed_loaded")
        shift_loaded = sem("shift_loaded")
        wo_loaded = sem("wo_loaded")
        wo_split = sem("wo_split")
        consts = sem("consts_b")
        mx_ready = sem("mx_ready")
        mx_free = sem("mx_free")
        row_max_done = sem("row_max_done")
        max16_done = sem("max16_done")
        sc_ready = sem("sc_ready")
        rows_read = sem("rows_read")
        prob_ready = sem("prob_ready")
        step_done = sem("step_done")
        recip_done = sem("recip_done")
        y_done = sem("y_done")
        y_out = [sem(f"y_out{n}") for n in range(2)]
        shifted = sem("shifted")
        four_set = sem("four_set")
        bits_set = sem("bits_set")
        clipped = sem("clipped")
        differed = sem("differed")
        decoded = sem("decoded")
        block = ctx.enter_context(nc.Block())

        @block.sync
        def _(sp):
            for started in y_out:
                sp.sem_inc(started, 1)
            sp.dma_start(shift[:, :], io["shifts"]).then_inc(shift_loaded, 16)

            def group(g):
                sp.wait_ge(step_done, g * NSTEP + 2)
                for n, part in enumerate((0, 1, 0)):
                    sp.dma_start(k_st[n * HD:(n + 1) * HD, :, :],
                                 io["qk_parts"][bass.ds(g + KT, 1), part].rearrange("a (j d) s -> d (a j) s", j=HG))\
                      .then_inc(k_loaded, 16)
                for n, part in enumerate((0, 0, 1)):
                    sp.dma_start(q_st[n * HD:(n + 1) * HD, :, :],
                                 io["qk_parts"][bass.ds(g, 1), part].rearrange("a (j d) s -> d (a j) s", j=HG))\
                      .then_inc(q_loaded, 16)
                sp.dma_start(v_g[:, :, :], io["v_rows"][:, bass.ds(g * P, P)].rearrange("(t p) d -> p t d", p=P))\
                  .then_inc(v_loaded, 16)
                sp.wait_ge(shifted, g * PIECES + 1)
                for j in range(NIB):
                    sp.dma_start(packed[j * WG:(j + 1) * WG, :],
                                 io["packed"][bass.ds(g, 1), :, :].rearrange("a w n -> (a w) n"))\
                      .then_inc(packed_loaded, 16)
                for c in range(NC):
                    sp.wait_ge(y_done, g * NC + c + 2)
                    sp.dma_start(io["y_cols"][bass.ds(g * P, P), c * C:(c + 1) * C], y[:, c % 2, :])\
                      .then_inc(y_out[c % 2], 16)

            with sp.Fori(0, NG) as g:
                group(g)
            for n in range(2):
                sp.wait_ge(y_out[n], 16 * NG * NC // 2 + 1)

        @block.gpsimd
        def _(pool):
            nc.gpsimd.memset(ones[:, :], 1.0).then_inc(consts, 1)
            pool.wait_ge(consts, 1)
            nc.gpsimd.memset(k_st[ROWM:ROWM + 1, :, :], -M_UNIT).then_inc(consts, 1)
            pool.wait_ge(consts, 2)
            for k in range(KT):
                if k:
                    pool.wait_ge(wo_split, 2 * k)
                pool.dma_start(wo_stage[:, :], io["w_out"][k]).then_inc(wo_loaded, 16)
                pool.wait_ge(wo_loaded, 16 * k + 16)
                nc.gpsimd.tensor_copy(keep["wo_hi"][:, k, :], wo_stage[:, :]).then_inc(wo_split, 1)
                pool.wait_ge(wo_split, 2 * k + 1)
                nc.gpsimd.tensor_tensor(keep["wo_lo"][:, k, :], wo_stage[:, :],
                                        keep["wo_hi"][:, k, :].bitcast(F32), ALU.subtract).then_inc(wo_split, 1)

        @block.scalar
        def _(act):
            act.sem_inc(prob_ready, 1)

            def rows(g, c, entry):
                for p in range(2):
                    act.wait_ge(sc_ready, g * NENTRY + entry + 1)
                    nc.scalar.copy(q_st[ROWM:ROWM + 1, 2 * p:2 * p + 2, c * C:(c + 1) * C],
                                   sc_ps[entry % 2][ROWM:ROWM + 1, :, :]).then_inc(rows_read, 1)
                    entry += 1
                return entry

            def group(g):
                pair = 0
                entry = rows(g, 0, 0)
                for c in range(NC):
                    for k in range(STEPS[c]):
                        lo = max(0, k - TC * c) * P
                        for p in range(2):
                            act.wait_ge(sc_ready, g * NENTRY + entry + 1)
                            act.wait_ge(step_done, g * NSTEP + pair // 2 + 1)
                            act_out = prob[:, pair % PB, :, lo:C]
                            nc.scalar.activation(act_out, sc_ps[entry % 2][:, :, lo:C], ACT.Exp)\
                              .then_inc(prob_ready, 1)
                            entry += 1
                            pair += 1
                    if c + 1 < NC:
                        entry = rows(g, c + 1, entry)

            with act.Fori(0, NG) as g:
                group(g)

        @block.vector
        def _(dve):
            dve.sem_inc(mx_free, 2)
            for started in (y_done, shifted, decoded):
                dve.sem_inc(started, 1)
            dve.wait_ge(shift_loaded, 16)

            def decode(g, n):
                if n == 0:
                    dve.wait_ge(packed_loaded, g * (16 * NIB) + 16 * NIB)
                k = g * PIECES + n
                dve.wait_ge(decoded, k + 1)
                nc.vector.tensor_scalar(bits[:, :], packed[:, n * PW:(n + 1) * PW], shift[:, :], 6,
                                        ALU.logical_shift_left, ALU.arith_shift_right).then_inc(shifted, 1)
                dve.wait_ge(shifted, k + 2)
                nc.vector.tensor_scalar(four[:, :], bits[:, :], -2 ** 31, 0x40800000,
                                        ALU.bitwise_and, ALU.bitwise_or).then_inc(four_set, 1)
                dve.wait_ge(four_set, k + 1)
                nc.vector.tensor_scalar(bits[:, :], bits[:, :], 0x81C00000 - 2 ** 32, 0x40000000,
                                        ALU.bitwise_and, ALU.bitwise_or).then_inc(bits_set, 1)
                dve.wait_ge(bits_set, k + 1)
                nc.vector.tensor_scalar(clip[:, :], bits[:, :].bitcast(F32), 4.0, -4.0, ALU.min, ALU.max)\
                  .then_inc(clipped, 1)
                dve.wait_ge(clipped, k + 1)
                nc.vector.tensor_tensor(clip[:, :], clip[:, :], four[:, :].bitcast(F32), ALU.subtract)\
                  .then_inc(differed, 1)
                dve.wait_ge(differed, k + 1)
                a, b = n * PW, (n + 1) * PW
                if b <= GU:
                    out = keep["w_gu"][:, bass.ds(g * GU + a, PW)]
                else:
                    out = keep["w_dn"][:, bass.ds(g * DN + (a - GU), PW)]
                nc.vector.tensor_tensor(out, clip[:, :], bits[:, :].bitcast(F32), ALU.add).then_inc(decoded, 1)

            def group(g):
                unit = [0]
                piece = [0]

                def maxima(c, todo):
                    for t, j, b in todo:
                        n = unit[0]
                        dve.wait_ge(mx_ready, g * NMX + n + 1)
                        nc.vector.reduce_max(max_part[:, t * HG + j, b:b + 1], mx_ps[n % 2][:, 0:bank_width(c, t, b)],
                                             X).then_inc(mx_free, 1)
                        unit[0] += 1

                def round_max(c):
                    dve.wait_ge(mx_free, g * NMX + unit[0] + 2)
                    nc.vector.reduce_max(row_max[:, :], max_part[:, :, 0:c + 1], X).then_inc(row_max_done, 1)
                    dve.wait_ge(row_max_done, g * NC + c + 1)
                    nc.vector.tensor_scalar(max16[:, :], row_max[:, :], 1.0 / M_UNIT, None, ALU.mult)\
                      .then_inc(max16_done, 1)

                maxima(0, MAX_UNITS[0])
                round_max(0)
                for c in range(NC):
                    if c + 1 < NC:
                        units = MAX_UNITS[c + 1]
                        half = len(units) // 2
                        maxima(c + 1, units[:half])
                        decode(g, piece[0])
                        piece[0] += 1
                        maxima(c + 1, units[half:])
                        round_max(c + 1)
                    else:
                        while piece[0] < PIECES:
                            decode(g, piece[0])
                            piece[0] += 1
                    dve.wait_ge(step_done, g * NSTEP + sum(STEPS[:c + 1]) + 2)
                    nc.vector.reciprocal(recip[:, :], sum_ps[:, :]).then_inc(recip_done, 1)
                    dve.wait_ge(recip_done, g * NC + c + 1)
                    dve.wait_ge(y_out[c % 2], g * (16 * NC // 2) + 16 * (c // 2) + 1)
                    nc.vector.tensor_tensor(y[:, c % 2, :], y_ps[:, :], recip[:, :], ALU.mult).then_inc(y_done, 1)

            with dve.Fori(0, NG) as g:
                group(g)

        @block.tensor
        def _(pe):
            pe.sem_inc(step_done, 2)
            pe.wait_ge(consts, 2)

            def group(g):
                unit = [0]
                readers = []
                exps = [g * (2 * NSTEP) + 1]
                copies = [g * (2 * NC)]

                def wait_free():
                    if len(readers) < 2:
                        pe.wait_ge(prob_ready, g * (2 * NSTEP) + 1)
                    else:
                        pe.wait_ge(*readers[-2])

                def maxima(c, todo):
                    for t, j, b in todo:
                        n = unit[0]
                        w = bank_width(c, t, b)
                        q0 = c * C + t * P
                        pe.wait_ge(mx_free, g * NMX + n + 1)
                        last = nc.tensor.matmul(mx_ps[n % 2][:, 0:w], q_st[0:ROWM, j, q0:q0 + P],
                                                k_st[0:ROWM, j, b * C:b * C + w], start=True, stop=(b < c))
                        if b == c:
                            last = nc.tensor.matmul(mx_ps[n % 2][:, w - P:w], keep["identb"][:, :],
                                                    keep["mask_qk"][:, :], start=False, stop=True)
                        last.then_inc(mx_ready, 1)
                        unit[0] += 1

                def rows(c):
                    pe.wait_ge(max16_done, g * NC + c + 1)
                    for p in range(2):
                        n = len(readers)
                        wait_free()
                        copies[0] = copies[0] + 1
                        readers.append((rows_read, copies[0]))
                        for b in range(2):
                            for t in range(TC):
                                col = t * HG + 2 * p + b
                                last = nc.tensor.matmul(sc_ps[n % 2][ROWM:ROWM + 1, b, t * P:(t + 1) * P],
                                                        max16[:, col:col + 1], keep["ident16"][:, :],
                                                        start=True, stop=True)
                        last.then_inc(sc_ready, 1)

                def scores(c, k):
                    lo = max(0, k - TC * c) * P
                    for p in range(2):
                        n = len(readers)
                        wait_free()
                        if k == 0 and p == 0:
                            pe.wait_ge(rows_read, copies[0])
                        exps[0] = exps[0] + 1
                        readers.append((prob_ready, exps[0]))
                        for b in range(2):
                            j = 2 * p + b
                            last = nc.tensor.matmul(sc_ps[n % 2][:, b, lo:C], k_st[0:ROWM + 1, j, k * P:(k + 1) * P],
                                                    q_st[0:ROWM + 1, j, c * C + lo:(c + 1) * C],
                                                    start=True, stop=(k < TC * c))
                            if k >= TC * c:
                                last = nc.tensor.matmul(sc_ps[n % 2][:, b, lo:lo + P], keep["identb"][:, :],
                                                        keep["mask_kq"][:, :], start=False, stop=True)
                        last.then_inc(sc_ready, 1)

                def sums(c, k):
                    s = sum(STEPS[:c]) + k
                    lo = max(0, k - TC * c) * P
                    pe.wait_ge(prob_ready, g * (2 * NSTEP) + 2 * s + 3)
                    if k == 0:
                        pe.wait_ge(y_done, g * NC + c + 1)
                    first, final = k == 0, k == STEPS[c] - 1
                    for j in range(HG):
                        nc.tensor.matmul(y_ps[j * HD:(j + 1) * HD, lo:C], v_g[:, k, j * HD:(j + 1) * HD],
                                         prob[:, (2 * s + j // 2) % PB, j % 2, lo:C], start=first, stop=final,
                                         tile_position=(0, j * HD))
                    for j in range(HG):
                        last = nc.tensor.matmul(sum_ps[j * HD:(j + 1) * HD, lo:C], ones[:, :],
                                                prob[:, (2 * s + j // 2) % PB, j % 2, lo:C], start=first, stop=final,
                                                tile_position=(0, j * HD))
                    last.then_inc(step_done, 1)

                pe.wait_ge(q_loaded, g * 48 + 48)
                pe.wait_ge(k_loaded, g * 48 + 48)
                maxima(0, MAX_UNITS[0])
                rows(0)
                pe.wait_ge(v_loaded, g * 16 + 16)
                for c in range(NC):
                    plan = order(c)
                    for k in range(STEPS[c]):
                        scores(c, k)
                        maxima(c + 1, plan[k])
                        if k == STEPS[c] - 1 and c + 1 < NC:
                            rows(c + 1)
                        if k:
                            sums(c, k - 1)
                    sums(c, STEPS[c] - 1)

            with pe.Fori(0, NG) as g:
                group(g)


def phase_c(nc, io, keep):
    LAG = 2
    HB = LAG + 1
    AB, DB, FB = 2, 4, 2
    GATE_UP = [(0, 0), (1, 0)] + [(s, k) for k in range(1, KT) for s in range(2)]
    NA, ND = IT * 4, IT * 8
    a_at, d_at = {}, {}
    for o in range(IT + LAG):
        if o < IT:
            for s, k in GATE_UP:
                ring = d_at if k else a_at
                ring["gu", o, s, k] = len(ring)
        if o >= LAG:
            for r in range(KT):
                ring = a_at if r % 2 else d_at
                ring["dn", o - LAG, r] = len(ring)
    assert (len(a_at), len(d_at)) == (NA, ND)

    with ExitStack() as ctx:
        def sb(name, shape, dt=F32):
            return ctx.enter_context(nc.sbuf_tensor(name, shape, dt))

        def sem(name):
            return ctx.enter_context(nc.semaphore(name))

        w_gu = keep["w_gu"][:, :].rearrange("p (k n) -> p k n", k=KT)
        w_dn = keep["w_dn"][:, :].rearrange("p (t o) -> p t o", t=IT)
        wo_hi, wo_lo, ident = keep["wo_hi"], keep["wo_lo"], keep["ident"]
        NSG, NSD = GU // P * KT, KT * IT
        sc16 = sb("sc16", [P, NSG + NSD], F16)
        sc = sb("sc", [P, NSG + NSD])
        sc_gu = sc[:, 0:NSG].rearrange("p (o k) -> p o k", k=KT)
        sc_dn = sc[:, NSG:NSG + NSD].rearrange("p (r t) -> p r t", t=IT)
        gate_rows = sb("gate_rows", [P, 2, D])
        gate_col = sb("gate_col", [P, P])
        gab = sb("gab", [P, D])
        eps = sb("eps_c", [P, 2])
        xy = sb("xy", [P, KT, C])
        y_hi = sb("y_hi", [P, 2, KT, P], F32R)
        y_lo = sb("y_lo", [P, 2, KT, P], F32R)
        prod = sb("prod", [P, 2, D])
        x1 = sb("x1", [P, ST, D])
        stats = sb("stats_c", [P, TC, 6])
        mv = sb("mv_c", [P, TC, 2])
        rstd = sb("rstd_c", [P, 2, TC])
        ht = sb("ht_c", [P, KT, C])
        h_hi = sb("h_hi_c", [P, KT, C], F32R)
        h_lo = sb("h_lo_c", [P, KT, C], F32R)
        gu = sb("gu", [P, 2, 2, C])
        h1 = sb("h1", [P, 2, C])
        h1_hi = sb("h1_hi", [P, HB, C], F32R)
        h1_lo = sb("h1_lo", [P, HB, C], F32R)
        tmp = sb("tmp", [P, 2, C])
        acc = sb("acc", [P, KT, C])
        junk = sb("junk", [P, D])
        sq = sb("sq", [P, TC])
        rms = sb("rms", [P, 2, TC])
        a_ps = [ctx.enter_context(nc.psum_tensor(f"a_ps{n}", [P, C], F32)) for n in range(AB)]
        d_ps = [ctx.enter_context(nc.psum_tensor(f"d_ps{n}", [P, C], F32)) for n in range(DB)]
        f_ps = [ctx.enter_context(nc.psum_tensor(f"f_ps{n}", [P, C], F32)) for n in range(FB)]

        scales_loaded = sem("scales_loaded")
        b_loaded = sem("b_loaded")
        consts = sem("consts_c")
        scaled = sem("scaled")
        col_set = sem("col_set")
        col_used = sem("col_used")
        gates_out = sem("gates_out")
        gab_done = sem("gab_done")
        y_loaded = sem("y_loaded")
        xy_free = sem("xy_free")
        load_started = sem("load_started")
        x_loaded = sem("x_loaded_c")
        y_hi_done = sem("y_hi_done")
        y_lo_done = sem("y_lo_done")
        prod_ready = sem("prod_ready")
        prod_read = sem("prod_read")
        bias_added = sem("bias_added")
        x1_done = sem("x1_done")
        stats_done = sem("stats_done_c")
        rows_seen = sem("rows_seen")
        mv_done = sem("mv_done_c")
        sd_done = sem("sd_done_c")
        rstd_done = sem("rstd_done_c")
        xn_done = sem("xn_done_c")
        tp_done = sem("tp_done_c")
        ht_done = sem("ht_done_c")
        h_hi_done = sem("h_hi_done_c")
        h_lo_done = sem("h_lo_done_c")
        a_ready = sem("a_ready")
        a_read = sem("a_read")
        d_ready = sem("d_ready")
        d_read = sem("d_read")
        silu_done = sem("silu_done_c")
        h1_done = sem("h1_done")
        h1_hi_done = sem("h1_hi_done")
        h1_lo_done = sem("h1_lo_done")
        tmp_added = sem("tmp_added")
        tail_ready = sem("tail_ready")
        rows_copied = sem("rows_copied")
        rows_squared = sem("rows_squared")
        rms_done = sem("rms_done")
        rms_inv = sem("rms_inv")
        normed = sem("normed")
        out_ready = sem("out_ready")
        out_sent = sem("out_sent")
        block = ctx.enter_context(nc.Block())

        @block.sync
        def _(sp):
            sp.sem_inc(out_sent, 1)
            sp.dma_start(sc16[:, :], io["scales"]).then_inc(scales_loaded, 16)
            sp.dma_start(gab[:, :], io["b_out"].partition_broadcast(P)).then_inc(b_loaded, 16)

            def load(i):
                sp.dma_start(x1[:, bass.ds(i * TC, TC), :], io["x"][bass.ds(i * C, C), :]
                             .rearrange("(t p) d -> p t d", p=P)).then_inc(x_loaded, 16)
                sp.wait_ge(tp_done, i * KT + 1)
                sp.sem_inc(xy_free, 1)
                sp.dma_start(xy[:, :, :], io["y_cols"][:, bass.ds(i * C, C)]
                             .rearrange("(f p) s -> p f s", p=P)).then_inc(y_loaded, 16)

            def chunk(i, more):
                if more:
                    sp.wait_ge(x_loaded, i * 16 + 16)
                    sp.wait_ge(y_loaded, i * 16 + 16)
                    sp.sem_inc(load_started, 1)
                    load(i + 1)
                for t in range(TC):
                    sp.wait_ge(out_ready, i * TC + t + 1)
                    sp.dma_start(io["out"][bass.ds(i * C + t * P, P), :], ht[:, t, :]).then_inc(out_sent, 16)

            load(0)
            with sp.Fori(0, NC - 1) as i:
                chunk(i, True)
            chunk(NC - 1, False)
            sp.wait_ge(out_sent, 16 * NC * TC + 1)

        @block.gpsimd
        def _(pool):
            for started in (h1_done, h1_lo_done, tmp_added):
                pool.sem_inc(started, 1)
            nc.gpsimd.memset(eps[:, 0:1], EPS).then_inc(consts, 1)
            nc.gpsimd.memset(eps[:, 1:2], RMS_EPS).then_inc(consts, 1)

            def add_bias(i):
                pool.wait_ge(gab_done, 1)
                pool.wait_ge(x_loaded, i * 16 + 16)
                for t in range(TC):
                    nc.gpsimd.tensor_tensor(x1[:, bass.ds(i * TC + t, 1), :].rearrange("p a d -> p (a d)"),
                                            x1[:, bass.ds(i * TC + t, 1), :].rearrange("p a d -> p (a d)"),
                                            gab[:, :], ALU.add).then_inc(bias_added, 1)

            def hidden(i, o):
                pool.wait_ge(silu_done, i * IT + o + 1)
                pool.wait_ge(d_read, i * ND + DB + d_at["gu", o, 1, KT - 1] + 1)
                nc.gpsimd.tensor_tensor(h1[:, o % 2, :], h1[:, o % 2, :], gu[:, o % 2, 1, :], ALU.mult)\
                  .then_inc(h1_done, 1)

            def add_down(i, t):
                if t == 0:
                    return
                for n, r in enumerate((1, 3)):
                    pool.wait_ge(a_read, i * NA + AB + a_at["dn", t, r] + 1)
                    nc.gpsimd.tensor_tensor(acc[:, r, :], acc[:, r, :], tmp[:, n, :], ALU.add)\
                      .then_inc(tmp_added, 1)

            def low(i, o):
                pool.wait_ge(h1_hi_done, i * IT + o + 1)
                nc.gpsimd.tensor_tensor(h1_lo[:, o % HB, :], h1[:, o % 2, :], h1_hi[:, o % HB, :].bitcast(F32),
                                        ALU.subtract).then_inc(h1_lo_done, 1)

            def chunk(i, more):
                for o in range(IT + LAG):
                    if 1 <= o <= IT:
                        hidden(i, o - 1)
                    if o >= LAG:
                        add_down(i, o - LAG)
                    if 1 <= o <= IT:
                        low(i, o - 1)
                    if o == 1 and more:
                        add_bias(i + 1)
                for t in range(TC):
                    pool.wait_ge(normed, i * TC + t + 1)
                    nc.gpsimd.tensor_tensor(ht[:, t, :], ht[:, t, :],
                                            x1[:, bass.ds(i * TC + t, 1), :].rearrange("p a d -> p (a d)"),
                                            ALU.add).then_inc(out_ready, 1)

            add_bias(0)
            with pool.Fori(0, NC - 1) as i:
                chunk(i, True)
            chunk(NC - 1, False)

        @block.scalar
        def _(act):
            act.sem_inc(a_read, AB)
            act.sem_inc(rows_squared, 1)

            def deviation(i):
                act.wait_ge(mv_done, i * TC + TC)
                nc.scalar.activation(rstd[:, 0, :], mv[:, :, 1], ACT.Sqrt, bias=eps[:, 0:1]).then_inc(sd_done, 1)

            def modulate(i, sent):
                act.wait_ge(out_sent, sent + 1)
                for f in range(KT):
                    act.wait_ge(tp_done, i * KT + f + 2)
                    nc.scalar.activation(ht[:, f, :], f_ps[(TC + f) % FB][:, :], ACT.Identity,
                                         bias=keep["ffn_mod"][:, 0, f:f + 1],
                                         scale=keep["ffn_mod"][:, 1, f:f + 1]).then_inc(ht_done, 1)

            def first_sums(i, o):
                act.wait_ge(h1_done, i * IT + max(0, o - 1) + 1)
                for s in range(2):
                    n = a_at["gu", o, s, 0]
                    act.wait_ge(a_ready, i * NA + n + 1)
                    nc.scalar.activation(gu[:, o % 2, s, :], a_ps[n % AB][:, :], ACT.Copy,
                                         scale=sc_gu[:, s * IT + o, 0:1]).then_inc(a_read, 1)

            def silu(i, o):
                act.wait_ge(d_read, i * ND + DB + d_at["gu", o, 0, KT - 1] + 1)
                act.wait_ge(h1_lo_done, i * IT + max(0, o - 1) + 1)
                nc.scalar.activation(h1[:, o % 2, :], gu[:, o % 2, 0, :], ACT.Silu).then_inc(silu_done, 1)

            def down(i, t):
                for n, r in enumerate((1, 3)):
                    at = a_at["dn", t, r]
                    act.wait_ge(a_ready, i * NA + at + 1)
                    if t == 0:
                        act.wait_ge(tail_ready, i * TC + 1)
                        out = acc[:, r, :]
                    else:
                        act.wait_ge(tmp_added, i * (2 * (IT - 1)) + max(0, 2 * (t - 2) + n + 1) + 1)
                        out = tmp[:, n, :]
                    nc.scalar.activation(out, a_ps[at % AB][:, :], ACT.Copy,
                                         scale=sc_dn[:, r, t:t + 1]).then_inc(a_read, 1)

            def high(i, o):
                act.wait_ge(h1_done, i * IT + o + 2)
                nc.scalar.activation(h1_hi[:, o % HB, :], h1[:, o % 2, :], ACT.Copy).then_inc(h1_hi_done, 1)

            def chunk(i, more):
                for o in range(IT + LAG):
                    if o < IT:
                        first_sums(i, o)
                    if 1 <= o <= IT:
                        silu(i, o - 1)
                    if o >= LAG:
                        down(i, o - LAG)
                    if 1 <= o <= IT:
                        high(i, o - 1)
                    if more and o == 3:
                        deviation(i + 1)
                    if more and o == 7:
                        modulate(i + 1, i * (16 * TC))
                act.wait_ge(out_sent, i * (16 * TC) + 1)
                act.wait_ge(h_lo_done, (i + 1) * KT + (KT if more else 0))
                for t in range(TC):
                    act.wait_ge(tail_ready, i * TC + t + 2)
                    nc.scalar.copy(ht[:, t, :], f_ps[(2 * TC + t) % FB][:, :]).then_inc(rows_copied, 1)
                    act.wait_ge(rows_squared, i * TC + t + 1)
                    nc.scalar.activation(junk[:, :], f_ps[(2 * TC + t) % FB][:, :], ACT.Square,
                                         accum_out=sq[:, t:t + 1]).then_inc(rows_squared, 1)
                act.wait_ge(rows_squared, i * TC + TC + 1)
                nc.scalar.activation(rms[:, 0, :], sq[:, :], ACT.Sqrt, bias=eps[:, 1:2], scale=1.0 / D)\
                  .then_inc(rms_done, 1)

            act.wait_ge(consts, 2)
            act.wait_ge(scaled, 1)
            deviation(0)
            modulate(0, 0)
            with act.Fori(0, NC - 1) as i:
                chunk(i, True)
            chunk(NC - 1, False)

        @block.vector
        def _(dve):
            dve.sem_inc(d_read, DB)
            dve.sem_inc(x1_done, 1)

            def split_y(i, t):
                if t == 0:
                    dve.wait_ge(y_loaded, i * 16 + 16)
                dve.wait_ge(prod_ready, i * TC + max(0, t - 1) + 1)
                cols = slice(t * P, (t + 1) * P)
                nc.vector.tensor_copy(y_hi[:, t % 2, :, :], xy[:, :, cols]).then_inc(y_hi_done, 1)
                dve.wait_ge(y_hi_done, i * TC + t + 1)
                nc.vector.tensor_tensor(y_lo[:, t % 2, :, :], xy[:, :, cols], y_hi[:, t % 2, :, :].bitcast(F32),
                                        ALU.subtract).then_inc(y_lo_done, 1)

            def residual(i):
                for t in range(TC):
                    dve.wait_ge(prod_ready, i * TC + t + 2)
                    dve.wait_ge(x1_done, i * TC + max(0, t - 1) + 1)
                    nc.vector.tensor_tensor(prod[:, t % 2, :], f_ps[t % FB][:, :], gate_rows[:, 0, :], ALU.mult)\
                      .then_inc(prod_read, 1)
                    if t + 2 < TC:
                        split_y(i, t + 2)
                    dve.wait_ge(prod_read, i * TC + t + 1)
                    dve.wait_ge(bias_added, i * TC + t + 1)
                    rows = x1[:, bass.ds(i * TC + t, 1), :].rearrange("p a d -> p (a d)")
                    nc.vector.tensor_tensor(rows, rows, prod[:, t % 2, :], ALU.add).then_inc(x1_done, 1)
                for t in range(TC):
                    dve.wait_ge(x1_done, i * TC + t + 2)
                    dve.sem_inc(rows_seen, 1)
                    nc.vector.bn_stats(stats[:, t, :], x1[:, bass.ds(i * TC + t, 1), :]
                                       .rearrange("p a d -> p (a d)")).then_inc(stats_done, 1)
                for t in range(TC):
                    dve.wait_ge(stats_done, i * TC + t + 1)
                    dve.sem_inc(rows_seen, 1)
                    nc.vector.bn_aggr(mv[:, t, :], stats[:, t, :]).then_inc(mv_done, 1)

            def normalize(i):
                dve.wait_ge(sd_done, i + 1)
                nc.vector.reciprocal(rstd[:, 1, :], rstd[:, 0, :]).then_inc(rstd_done, 1)
                dve.wait_ge(rstd_done, i + 1)
                dve.wait_ge(y_lo_done, i * TC + TC)
                for t in range(TC):
                    nc.vector.tensor_scalar(xy[:, t, :], x1[:, bass.ds(i * TC + t, 1), :]
                                            .rearrange("p a d -> p (a d)"), mv[:, t, 0:1], rstd[:, 1, t:t + 1],
                                            ALU.subtract, ALU.mult).then_inc(xn_done, 1)

            def split_h(i):
                for f in range(KT):
                    dve.wait_ge(ht_done, i * KT + f + 1)
                    nc.vector.tensor_copy(h_hi[:, f, :], ht[:, f, :]).then_inc(h_hi_done, 1)
                for f in range(KT):
                    dve.wait_ge(h_hi_done, i * KT + f + 1)
                    nc.vector.tensor_tensor(h_lo[:, f, :], ht[:, f, :], h_hi[:, f, :].bitcast(F32),
                                            ALU.subtract).then_inc(h_lo_done, 1)

            def gate_up(i, o):
                for s, k in GATE_UP:
                    if k == 0:
                        continue
                    n = d_at["gu", o, s, k]
                    dve.wait_ge(d_ready, i * ND + n + 1)
                    if k == 1:
                        dve.wait_ge(a_read, i * NA + AB + a_at["gu", o, s, 0] + 1)
                    else:
                        dve.wait_ge(d_read, i * ND + DB + d_at["gu", o, s, k - 1] + 1)
                    nc.vector.scalar_tensor_tensor(out=gu[:, o % 2, s, :], in0=d_ps[n % DB][:, :],
                                                   scalar=sc_gu[:, s * IT + o, k:k + 1], in1=gu[:, o % 2, s, :],
                                                   op0=ALU.mult, op1=ALU.add).then_inc(d_read, 1)

            def down(i, t):
                for r in (0, 2):
                    n = d_at["dn", t, r]
                    dve.wait_ge(d_ready, i * ND + n + 1)
                    if t == 0:
                        dve.wait_ge(tail_ready, i * TC + 1)
                        nc.vector.tensor_scalar(acc[:, r, :], d_ps[n % DB][:, :], sc_dn[:, r, 0:1], None,
                                                ALU.mult).then_inc(d_read, 1)
                    else:
                        dve.wait_ge(d_read, i * ND + DB + d_at["dn", t - 1, r] + 1)
                        nc.vector.scalar_tensor_tensor(out=acc[:, r, :], in0=d_ps[n % DB][:, :],
                                                       scalar=sc_dn[:, r, t:t + 1], in1=acc[:, r, :],
                                                       op0=ALU.mult, op1=ALU.add).then_inc(d_read, 1)

            def chunk(i, more):
                for o in range(IT + LAG):
                    if o < IT:
                        gate_up(i, o)
                    if o >= LAG:
                        down(i, o - LAG)
                    if more and o == 1:
                        split_y(i + 1, 0)
                        split_y(i + 1, 1)
                    if more and o == 3:
                        residual(i + 1)
                    if more and o == 4:
                        normalize(i + 1)
                    if more and o == IT - 1:
                        split_h(i + 1)
                dve.wait_ge(rms_done, i + 1)
                nc.vector.reciprocal(rms[:, 1, :], rms[:, 0, :]).then_inc(rms_inv, 1)
                dve.wait_ge(rms_inv, i + 1)
                for t in range(TC):
                    dve.wait_ge(rows_copied, i * TC + t + 1)
                    nc.vector.scalar_tensor_tensor(out=ht[:, t, :], in0=ht[:, t, :], scalar=rms[:, 1, t:t + 1],
                                                   in1=gate_rows[:, 1, :], op0=ALU.mult, op1=ALU.mult)\
                      .then_inc(normed, 1)

            dve.wait_ge(scales_loaded, 16)
            nc.vector.tensor_scalar(sc[:, :], sc16[:, :], 0.25, None, ALU.mult).then_inc(scaled, 1)
            for g in range(2):
                for f in range(KT):
                    n = g * KT + f
                    dve.wait_ge(col_used, n)
                    nc.vector.tensor_copy(gate_col[:, :], keep["gates"][:, g, f:f + 1].to_broadcast([P, P]))\
                      .then_inc(col_set, 1)
            for g in range(2):
                dve.wait_ge(col_used, 2 * KT)
                nc.vector.tensor_copy(gate_rows[:, g, :], f_ps[g][:, :]).then_inc(gates_out, 1)
            dve.wait_ge(gates_out, 2)
            dve.wait_ge(b_loaded, 16)
            nc.vector.tensor_tensor(gab[:, :], gab[:, :], gate_rows[:, 0, :], ALU.mult).then_inc(gab_done, 1)
            split_y(0, 0)
            split_y(0, 1)
            residual(0)
            normalize(0)
            split_h(0)
            with dve.Fori(0, NC - 1) as i:
                chunk(i, True)
            chunk(NC - 1, False)

        @block.tensor
        def _(pe):
            pe.sem_inc(tp_done, 1)
            pe.sem_inc(tail_ready, 1)
            pe.sem_inc(prod_ready, 1)
            for n in range(2 * KT):
                pe.wait_ge(col_set, n + 1)
                nc.tensor.matmul(f_ps[n // KT][:, (n % KT) * P:(n % KT + 1) * P], gate_col[:, :], ident[:, :],
                                 start=True, stop=True).then_inc(col_used, 1)

            def products(i):
                for t in range(TC):
                    if t < FB:
                        pe.wait_ge(rows_squared, (i - 1) * TC + 1 if not (isinstance(i, int) and i == 0) else 1)
                    else:
                        pe.wait_ge(prod_read, i * TC + t - 1)
                    pe.wait_ge(y_lo_done, i * TC + t + 1)
                    for f in range(KT):
                        for m, (a, b) in enumerate(((y_hi, wo_hi), (y_hi, wo_lo), (y_lo, wo_hi))):
                            last = nc.tensor.matmul(f_ps[t % FB][:, :], a[:, t % 2, f, :], b[:, f, :],
                                                    start=(f == 0 and m == 0), stop=(f == KT - 1 and m == 2))
                    last.then_inc(prod_ready, 1)

            def transposes(i):
                pe.wait_ge(xn_done, i * TC + TC)
                for f in range(KT):
                    if f < FB:
                        pe.wait_ge(prod_read, i * TC + TC)
                    else:
                        pe.wait_ge(ht_done, i * KT + f - 1)
                    for t in range(TC):
                        last = nc.tensor.transpose(f_ps[(TC + f) % FB][:, t * P:(t + 1) * P],
                                                   xy[:, t, f * P:(f + 1) * P], ident[:, :])
                    last.then_inc(tp_done, 1)

            def gate_up(i, o):
                if o == 0:
                    pe.wait_ge(h_lo_done, i * KT + KT)
                for s, k in GATE_UP:
                    cols = slice((s * IT + o) * P, (s * IT + o + 1) * P)
                    if k:
                        n = d_at["gu", o, s, k]
                        pe.wait_ge(d_read, i * ND + n + 1)
                        out, ready = d_ps[n % DB], d_ready
                    else:
                        n = a_at["gu", o, s, k]
                        pe.wait_ge(a_read, i * NA + n + 1)
                        out, ready = a_ps[n % AB], a_ready
                    nc.tensor.matmul(out[:, :], w_gu[:, k, cols], h_hi[:, k, :], start=True, stop=False)
                    nc.tensor.matmul(out[:, :], w_gu[:, k, cols], h_lo[:, k, :], start=False, stop=True)\
                      .then_inc(ready, 1)

            def down(i, t):
                pe.wait_ge(h1_lo_done, i * IT + t + 2)
                for r in range(KT):
                    cols = slice(r * P, (r + 1) * P)
                    if r % 2:
                        n = a_at["dn", t, r]
                        pe.wait_ge(a_read, i * NA + n + 1)
                        out, ready = a_ps[n % AB], a_ready
                    else:
                        n = d_at["dn", t, r]
                        pe.wait_ge(d_read, i * ND + n + 1)
                        out, ready = d_ps[n % DB], d_ready
                    nc.tensor.matmul(out[:, :], w_dn[:, t, cols], h1_hi[:, t % HB, :], start=True, stop=False)
                    nc.tensor.matmul(out[:, :], w_dn[:, t, cols], h1_lo[:, t % HB, :], start=False, stop=True)\
                      .then_inc(ready, 1)

            def tail(i, more):
                pe.wait_ge(d_read, i * ND + DB + ND)
                pe.wait_ge(tmp_added, (i + 1) * (2 * (IT - 1)) + 1)
                for t in range(TC):
                    if t < FB:
                        pe.wait_ge(ht_done, (i + 1) * KT + (KT if more else 0))
                    else:
                        pe.wait_ge(rows_squared, i * TC + t)
                    for r in range(KT):
                        last = nc.tensor.transpose(f_ps[(2 * TC + t) % FB][:, r * P:(r + 1) * P],
                                                   acc[:, r, t * P:(t + 1) * P], ident[:, :])
                    last.then_inc(tail_ready, 1)

            def chunk(i, more):
                for o in range(IT + LAG):
                    if o < IT:
                        gate_up(i, o)
                    if o >= LAG:
                        down(i, o - LAG)
                    if more and o == 3:
                        products(i + 1)
                    if more and o == 7:
                        transposes(i + 1)
                tail(i, more)

            pe.wait_ge(gates_out, 2)
            products(0)
            transposes(0)
            with pe.Fori(0, NC - 1) as i:
                chunk(i, True)
            chunk(NC - 1, False)


def adaln_layer(nc, io):
    with ExitStack() as ctx:
        def sb(name, shape, dt=F32):
            return ctx.enter_context(nc.sbuf_tensor(name, shape, dt))

        keep = {
            "ident": sb("ident", [P, P]), "ident16": sb("ident16", [P, P], F16), "identb": sb("identb", [P, P], BF16),
            "mask_qk": sb("mask_qk", [P, P], BF16), "mask_kq": sb("mask_kq", [P, P], BF16),
            "gates": sb("gates", [P, 2, KT]), "ffn_mod": sb("ffn_mod", [P, 2, KT]),
        }
        for name, shape, dt in (("qk_parts", [2 * KT, 2, P, S], F16), ("v_rows", [S, D], F32), ("y_cols", [D, S], F32)):
            io[name] = nc.dram_tensor(name, shape, dt, kind="Internal").ap()
        phase_a(nc, io, keep)
        for name, shape in (("w_gu", [P, KT * GU]), ("w_dn", [P, IT * D]), ("wo_hi", [P, KT, D]), ("wo_lo", [P, KT, D])):
            keep[name] = sb(name, shape, F32R)
        phase_b(nc, io, keep)
        phase_c(nc, io, keep)


def kernel(L0_attn_x, L0_attn_w_qkv, L0_attn_b_qkv, L0_attn_w_out, L0_attn_b_out, L0_ffn_gate_up_packed,
           L0_ffn_gate_up_scales, L0_ffn_down_packed, L0_ffn_down_scales, L0_c, L0_wmod):
    import numpy as np
    from concourse import bacc
    from concourse.bass_utils import run_bass_kernel_spmd

    def nibble_order(n):
        return np.arange(n).reshape(n // P, WG, NIB).transpose(0, 2, 1).reshape(n)

    fo, ho = nibble_order(D), nibble_order(NI)
    gu_order = np.concatenate([ho, NI + ho])
    a = {k: np.asarray(v) for k, v in locals().items() if k.startswith("L0_")}
    gu = a["L0_ffn_gate_up_packed"][gu_order].T.reshape(KT, WG, GU)
    dn = a["L0_ffn_down_packed"][fo].T.reshape(IT, WG, D).transpose(1, 0, 2).reshape(WG, NG, DN).transpose(1, 0, 2)
    gus = a["L0_ffn_gate_up_scales"][:, gu_order].reshape(KT, GU // P, P).transpose(2, 1, 0).reshape(P, -1)
    dns = a["L0_ffn_down_scales"][:, fo].reshape(IT, KT, P).transpose(2, 1, 0).reshape(P, -1)
    arrays = {
        "x": a["L0_attn_x"].reshape(S, D)[:, fo],
        "c": a["L0_c"].reshape(D),
        "wmod": a["L0_wmod"].T.reshape(6, D, D)[:, fo].reshape(6, KT, P, D),
        "w_qkv": a["L0_attn_w_qkv"][fo].reshape(KT, P, 3 * D),
        "bias_qk": a["L0_attn_b_qkv"][:2 * D].reshape(2 * KT, P).T,
        "bias_v": a["L0_attn_b_qkv"][2 * D:],
        "w_out": a["L0_attn_w_out"][:, fo].reshape(KT, P, D),
        "b_out": a["L0_attn_b_out"][fo],
        "packed": np.concatenate([gu, dn], axis=2),
        "scales": np.concatenate([gus, dns], axis=1),
        "shifts": (28 - 4 * (np.arange(P) // WG)).astype(np.int32).reshape(P, 1),
    }
    arrays = {k: np.ascontiguousarray(v) for k, v in arrays.items()}
    nc = bacc.Bacc("TRN2", target_bir_lowering=False, num_devices=1)
    io = {k: nc.dram_tensor(f"in_{k}", v.shape, mybir.dt.from_np(v.dtype), kind="ExternalInput").ap()
          for k, v in arrays.items()}
    io["out"] = nc.dram_tensor("out_0", (S, D), F32, kind="ExternalOutput").ap()
    adaln_layer(nc, io)
    r = run_bass_kernel_spmd(nc, [{f"in_{k}": v for k, v in arrays.items()}], core_ids=[0])
    out = np.empty((1, S, D), np.float32)
    out[0][:, fo] = r.results[0]["out_0"].reshape(S, D)
    return out
```

```python
from contextlib import ExitStack

import concourse.bass as bass
from concourse import mybir

P = 128
S, D, H = 2048, 512, 16
HD = D // H
KT = D // P
C = 512
TC = C // P
NC = S // C
ST = S // P
HG = P // HD
NG = H // HG
NI = 1408
IT = NI // P
GU = 2 * NI
WG = 16
NIB = 8
DN = IT * D // NG
PC = GU + DN
EPS = 1e-5
RMS_EPS = 1e-6
MASKED = -1e30
M_UNIT = 64.0
SA, CA, GA, SB, CB, GB = range(6)

F32, F32R = mybir.dt.float32, mybir.dt.float32r
F16, BF16, I32 = mybir.dt.float16, mybir.dt.bfloat16, mybir.dt.int32
ALU = mybir.AluOpType
ACT = mybir.ActivationFunctionType
X = mybir.AxisListType.X


def phase_a(nc, io, keep):
    QK = 2 * KT
    QS = 4
    with ExitStack() as ctx:
        def sb(name, shape, dt=F32):
            return ctx.enter_context(nc.sbuf_tensor(name, shape, dt))

        def sem(name):
            return ctx.enter_context(nc.semaphore(name))

        w_stage = sb("w_stage", [P, KT, 3 * D])
        w_hi = sb("w_hi", [P, KT, 3 * D], F32R)
        w_lo = sb("w_lo", [P, KT, 3 * D], F32R)
        mod_w = sb("mod_w", [P, 2, KT, D])
        mod_junk = sb("mod_junk", [P, D])
        c_row = sb("c_row", [P, D])
        mods = sb("mods", [P, 6, KT])
        absg = sb("absg", [P, 2, KT])
        bias_qk = sb("bias_qk", [P, QK])
        bias_v = sb("bias_v", [P, D])
        eps = sb("eps_a", [P, 1])
        xs = sb("xs", [P, TC, D])
        stats = sb("stats_a", [P, TC, 6])
        mv = sb("mv_a", [P, TC, 2])
        rstd = sb("rstd_a", [P, 2, TC])
        xn = sb("xn_a", [P, TC, D])
        ht = sb("ht_a", [P, KT, C])
        h_hi = sb("h_hi_a", [P, KT, C], F32R)
        h_lo = sb("h_lo_a", [P, KT, C], F32R)
        qf = sb("qf", [P, 2, C])
        qs = sb("qs", [P, QS, 2, C], F16)
        vf = sb("vf", [P, 2, D])
        tp = [ctx.enter_context(nc.psum_tensor(f"tp_a{f}", [P, C], F32)) for f in range(KT)]
        qk_ps = [ctx.enter_context(nc.psum_tensor(f"qk_ps{n}", [P, C], F32)) for n in range(2)]
        v_ps = [ctx.enter_context(nc.psum_tensor(f"v_ps{n}", [P, D], F32)) for n in range(2)]

        w_loaded = [sem(f"w_loaded{k}") for k in range(KT)]
        small_loaded = sem("small_loaded")
        mod_loaded = [sem(f"mod_loaded{n}") for n in range(2)]
        x_loaded = sem("x_loaded")
        silu_done = sem("silu_done")
        mod_done = sem("mod_done")
        clamp_step = sem("clamp_step")
        masks_set = sem("masks_set")
        masks_cut = sem("masks_cut")
        const_done = sem("const_done_a")
        w_hi_done = sem("w_hi_done")
        w_lo_done = sem("w_lo_done")
        stats_done = sem("stats_done_a")
        stats_seen = sem("stats_seen_a")
        mv_done = sem("mv_done_a")
        sd_done = sem("sd_done_a")
        rstd_done = sem("rstd_done_a")
        xn_done = sem("xn_done_a")
        tp_done = sem("tp_done_a")
        ht_done = sem("ht_done_a")
        h_hi_done = sem("h_hi_done_a")
        h_lo_done = sem("h_lo_done_a")
        qk_ready = sem("qk_ready")
        qk_evac = sem("qk_evac")
        qk_hi_done = sem("qk_hi_done")
        qk_lo_done = sem("qk_lo_done")
        v_ready = sem("v_ready")
        v_evac = sem("v_evac")
        qk_out = [sem(f"qk_out{n}") for n in range(QS)]
        v_out = [sem(f"v_out{n}") for n in range(2)]

        MOD_ORDER = [SA, CA, GA, SB, CB, GB]
        UNITS = [("qk", 0), ("qk", 1), ("v", 0), ("qk", 2), ("qk", 3), ("v", 1),
                 ("qk", 4), ("qk", 5), ("v", 2), ("qk", 6), ("qk", 7), ("v", 3)]
        block = ctx.enter_context(nc.Block())

        @block.sync
        def _(sp):
            for started in (*qk_out, *v_out):
                sp.sem_inc(started, 1)

            def load_x(i):
                sp.dma_start(xs[:, :, :], io["x"][bass.ds(i * C, C), :]
                             .rearrange("(t p) d -> p t d", p=P)).then_inc(x_loaded, 16)

            load_x(0)

            def chunk(i, more):
                if more:
                    sp.wait_ge(xn_done, i * TC + TC)
                    load_x(i + 1)
                for kind, n in UNITS:
                    if kind == "qk":
                        sp.wait_ge(qk_lo_done, i * QK + n + 2)
                        sp.dma_start(io["qk_parts"][n].rearrange("l p s -> p l s")[:, :, bass.ds(i * C, C)],
                                     qs[:, n % QS, :, :]).then_inc(qk_out[n % QS], 16)
                    else:
                        sp.wait_ge(v_evac, i * TC + n + 3)
                        sp.dma_start(io["v_rows"][bass.ds(i * C + n * P, P), :],
                                     vf[:, n % 2, :]).then_inc(v_out[n % 2], 16)

            with sp.Fori(0, NC - 1) as i:
                chunk(i, True)
            chunk(NC - 1, False)
            for n in range(QS):
                sp.wait_ge(qk_out[n], 16 * NC * QK // QS + 1)
            for n in range(2):
                sp.wait_ge(v_out[n], 16 * NC * TC // 2 + 1)

        @block.gpsimd
        def _(pool):
            ident, ident16, identb = keep["ident"], keep["ident16"], keep["identb"]
            mask_qk, mask_kq = keep["mask_qk"], keep["mask_kq"]
            nc.gpsimd.memset(eps[:, :], EPS).then_inc(const_done, 1)
            for t in (ident, ident16, identb, mask_qk, mask_kq):
                nc.gpsimd.memset(t[:, :], 0.0).then_inc(masks_set, 1)
            pool.wait_ge(masks_set, 5)
            for t in (ident, ident16, identb):
                nc.gpsimd.affine_select(out=t[:, :], in_=t[:, :], compare_op=ALU.not_equal, fill=1.0, base=0,
                                        pattern=[[-1, P]], channel_multiplier=1).then_inc(masks_cut, 1)
            nc.gpsimd.affine_select(out=mask_qk[:, :], in_=mask_qk[:, :], compare_op=ALU.is_ge, fill=MASKED, base=0,
                                    pattern=[[-1, P]], channel_multiplier=1).then_inc(masks_cut, 1)
            nc.gpsimd.affine_select(out=mask_kq[:, :], in_=mask_kq[:, :], compare_op=ALU.is_ge, fill=MASKED, base=0,
                                    pattern=[[1, P]], channel_multiplier=-1).then_inc(masks_cut, 1)

        @block.scalar
        def _(act):
            act.sem_inc(qk_evac, 2)
            act.sem_inc(ht_done, 1)
            act.dma_start(c_row[:, :], io["c"].partition_broadcast(P)).then_inc(small_loaded, 16)
            act.dma_start(bias_qk[:, :], io["bias_qk"]).then_inc(small_loaded, 16)
            act.dma_start(bias_v[:, :], io["bias_v"].partition_broadcast(P)).then_inc(small_loaded, 16)

            def load_mod(n):
                act.dma_start(mod_w[:, n % 2, :, :], io["wmod"][MOD_ORDER[n]].rearrange("f p k -> p f k"))\
                   .then_inc(mod_loaded[n % 2], 16)

            load_mod(0)
            load_mod(1)
            for k in range(KT):
                act.dma_start(w_stage[:, k, :], io["w_qkv"][k]).then_inc(w_loaded[k], 16)
            act.wait_ge(small_loaded, 48)
            nc.scalar.activation(c_row[:, :], c_row[:, :], ACT.Silu).then_inc(silu_done, 1)
            nc.scalar.preload_act_table(ACT.Sqrt)

            def deviation(i):
                act.wait_ge(mv_done, i * TC + TC)
                nc.scalar.activation(rstd[:, 0, :], mv[:, :, 1], ACT.Sqrt, bias=eps[:, :]).then_inc(sd_done, 1)

            def modulate(i):
                for f in range(KT):
                    act.wait_ge(tp_done, i * KT + f + 2)
                    act.wait_ge(h_lo_done, i * KT + 1)
                    nc.scalar.activation(ht[:, f, :], tp[f][:, :], ACT.Identity, bias=mods[:, SA, f:f + 1],
                                         scale=mods[:, CA, f:f + 1]).then_inc(ht_done, 1)

            act.wait_ge(const_done, 1)
            deviation(0)
            for k in range(KT):
                act.wait_ge(w_loaded[k], 16)
                nc.scalar.activation(w_hi[:, k, :], w_stage[:, k, :], ACT.Copy).then_inc(w_hi_done, 1)
            act.wait_ge(mod_done, 2)
            modulate(0)
            for n in range(2, 6):
                act.wait_ge(mod_done, n - 1)
                load_mod(n)

            def chunk(i, more):
                if more:
                    deviation(i + 1)
                for n in range(QK):
                    act.wait_ge(qk_ready, i * QK + n + 2)
                    if n >= 2:
                        act.wait_ge(qk_lo_done, i * QK + n)
                    else:
                        act.wait_ge(qk_lo_done, i * QK + 1)
                    nc.scalar.activation(qf[:, n % 2, :], qk_ps[n % 2][:, :], ACT.Identity,
                                         bias=bias_qk[:, n:n + 1],
                                         scale=HD ** -0.5 if n < KT else 1.0).then_inc(qk_evac, 1)
                if more:
                    modulate(i + 1)

            act.wait_ge(clamp_step, 1)
            with act.Fori(0, NC - 1) as i:
                chunk(i, True)
            chunk(NC - 1, False)

        @block.vector
        def _(dve):
            dve.sem_inc(v_evac, 2)
            dve.sem_inc(h_lo_done, 1)
            dve.sem_inc(qk_lo_done, 1)

            def normalize(i):
                dve.wait_ge(x_loaded, i * 16 + 16)
                for t in range(TC):
                    nc.vector.bn_stats(stats[:, t, :], xs[:, t, :]).then_inc(stats_done, 1)
                for t in range(TC):
                    dve.wait_ge(stats_done, i * TC + t + 1)
                    dve.sem_inc(stats_seen, 1)
                    nc.vector.bn_aggr(mv[:, t, :], stats[:, t, :]).then_inc(mv_done, 1)
                dve.wait_ge(sd_done, i + 1)
                nc.vector.reciprocal(rstd[:, 1, :], rstd[:, 0, :]).then_inc(rstd_done, 1)
                dve.wait_ge(rstd_done, i + 1)
                dve.wait_ge(tp_done, i * KT + 1)
                for t in range(TC):
                    nc.vector.tensor_scalar(xn[:, t, :], xs[:, t, :], mv[:, t, 0:1], rstd[:, 1, t:t + 1],
                                            ALU.subtract, ALU.mult).then_inc(xn_done, 1)

            def split_h(i):
                dve.wait_ge(qk_ready, i * QK + 1)
                dve.wait_ge(v_ready, i * TC + 1)
                for f in range(KT):
                    dve.wait_ge(ht_done, i * KT + f + 2)
                    nc.vector.tensor_copy(h_hi[:, f, :], ht[:, f, :]).then_inc(h_hi_done, 1)
                for f in range(KT):
                    dve.wait_ge(h_hi_done, i * KT + f + 1)
                    nc.vector.tensor_tensor(h_lo[:, f, :], ht[:, f, :], h_hi[:, f, :].bitcast(F32),
                                            ALU.subtract).then_inc(h_lo_done, 1)

            products = [0]

            def modulation(n):
                m = MOD_ORDER[n]
                dve.wait_ge(mod_loaded[n % 2], 16 * (n // 2) + 16)
                for f in range(KT):
                    if products[0]:
                        dve.wait_ge(clamp_step, products[0])
                    products[0] += 1
                    last = nc.vector.scalar_tensor_tensor(
                        out=mod_junk[:, :], in0=mod_w[:, n % 2, f, :], scalar=1.0, in1=c_row[:, :],
                        op0=ALU.mult, op1=ALU.mult, accum_out=mods[:, m, f:f + 1]).then_inc(clamp_step, 1)
                dve.wait_ge(clamp_step, products[0])
                if m in (CA, CB):
                    nc.vector.tensor_scalar(mods[:, m, :], mods[:, m, :], 1.0, None, ALU.add).then_inc(mod_done, 1)
                elif m in (GA, GB):
                    g = 0 if m == GA else 1
                    nc.vector.scalar_tensor_tensor(out=absg[:, g, :], in0=mods[:, m, :], scalar=-1.0,
                                                   in1=mods[:, m, :], op0=ALU.mult, op1=ALU.max)\
                      .then_inc(clamp_step, 1)
                    dve.wait_ge(clamp_step, products[0] + 1)
                    nc.vector.tensor_scalar(absg[:, g, :], absg[:, g, :], 0.25, None, ALU.max)\
                      .then_inc(clamp_step, 1)
                    nc.vector.tensor_scalar(mods[:, m, :], mods[:, m, :], 0.0, 2.0, ALU.is_ge, ALU.mult)\
                      .then_inc(clamp_step, 1)
                    products[0] += 3
                    dve.wait_ge(clamp_step, products[0])
                    nc.vector.scalar_tensor_tensor(out=keep["gates"][:, g, :], in0=mods[:, m, :], scalar=-1.0,
                                                   in1=absg[:, g, :], op0=ALU.add, op1=ALU.mult)\
                      .then_inc(mod_done, 1)
                else:
                    nc.vector.tensor_scalar(mods[:, m, :], mods[:, m, :], 1.0, None, ALU.mult).then_inc(mod_done, 1)
                if m in (SB, CB):
                    dve.wait_ge(mod_done, n + 1)
                    nc.vector.tensor_copy(keep["ffn_mod"][:, m - SB, :], mods[:, m, :]).then_inc(clamp_step, 1)
                    products[0] += 1

            normalize(0)
            dve.wait_ge(small_loaded, 48)
            nc.vector.tensor_scalar(bias_qk[:, 0:KT], bias_qk[:, 0:KT], HD ** -0.5, None, ALU.mult)\
              .then_inc(clamp_step, 1)
            products[0] += 1
            dve.wait_ge(silu_done, 1)
            modulation(0)
            modulation(1)
            for k in range(KT):
                dve.wait_ge(w_hi_done, k + 1)
                nc.vector.tensor_tensor(w_lo[:, k, :], w_stage[:, k, :], w_hi[:, k, :].bitcast(F32),
                                        ALU.subtract).then_inc(w_lo_done, 1)
            split_h(0)
            for n in range(2, 6):
                modulation(n)

            def chunk(i, more):
                if more:
                    normalize(i + 1)
                for kind, n in UNITS:
                    if kind == "qk":
                        dve.wait_ge(qk_evac, i * QK + n + 3)
                        dve.wait_ge(qk_out[n % QS], i * (16 * QK // QS) + 16 * (n // QS) + 1)
                        nc.vector.tensor_copy(qs[:, n % QS, 0, :], qf[:, n % 2, :]).then_inc(qk_hi_done, 1)
                        dve.wait_ge(qk_hi_done, i * QK + n + 1)
                        nc.vector.tensor_tensor(qs[:, n % QS, 1, :], qf[:, n % 2, :], qs[:, n % QS, 0, :],
                                                ALU.subtract).then_inc(qk_lo_done, 1)
                    else:
                        dve.wait_ge(v_ready, i * TC + n + 2)
                        dve.wait_ge(v_out[n % 2], i * (16 * TC // 2) + 16 * (n // 2) + 1)
                        nc.vector.tensor_tensor(vf[:, n % 2, :], v_ps[n % 2][:, :], bias_v[:, :],
                                                ALU.add).then_inc(v_evac, 1)
                if more:
                    split_h(i + 1)

            with dve.Fori(0, NC - 1) as i:
                chunk(i, True)
            chunk(NC - 1, False)

        @block.tensor
        def _(pe):
            pe.sem_inc(tp_done, 1)
            pe.sem_inc(qk_ready, 1)
            pe.sem_inc(v_ready, 1)

            def transposes(i):
                pe.wait_ge(xn_done, i * TC + TC)
                for f in range(KT):
                    pe.wait_ge(ht_done, i * KT + 1)
                    for t in range(TC):
                        last = nc.tensor.transpose(tp[f][:, t * P:(t + 1) * P], xn[:, t, f * P:(f + 1) * P],
                                                   keep["ident"][:, :])
                    last.then_inc(tp_done, 1)

            def project(i, kind, n):
                if kind == "qk":
                    pe.wait_ge(qk_evac, i * QK + n + 1)
                else:
                    pe.wait_ge(v_evac, i * TC + n + 1)
                for f in range(KT):
                    if kind == "qk":
                        cols = slice(n * P, (n + 1) * P)
                        parts = [(w_hi[:, f, cols], h_hi[:, f, :]), (w_lo[:, f, cols], h_hi[:, f, :]),
                                 (w_hi[:, f, cols], h_lo[:, f, :])]
                        out = qk_ps[n % 2]
                    else:
                        rows = slice(n * P, (n + 1) * P)
                        wv = slice(2 * D, 3 * D)
                        parts = [(h_hi[:, f, rows], w_hi[:, f, wv]), (h_hi[:, f, rows], w_lo[:, f, wv]),
                                 (h_lo[:, f, rows], w_hi[:, f, wv])]
                        out = v_ps[n % 2]
                    for m, (stat, mov) in enumerate(parts):
                        last = nc.tensor.matmul(out[:, :], stat, mov, start=(f == 0 and m == 0),
                                                stop=(f == KT - 1 and m == 2))
                last.then_inc(qk_ready if kind == "qk" else v_ready, 1)

            def chunk(i, more):
                pe.wait_ge(h_lo_done, i * KT + KT + 1)
                for u, (kind, n) in enumerate(UNITS):
                    project(i, kind, n)
                    if more and u == len(UNITS) - 3:
                        transposes(i + 1)

            pe.wait_ge(masks_cut, 5)
            transposes(0)
            pe.wait_ge(w_lo_done, KT)
            with pe.Fori(0, NC - 1) as i:
                chunk(i, True)
            chunk(NC - 1, False)


def phase_b(nc, io, keep):
    BR, XR, PR = 3, 3, 3
    ROWM = 3 * HD
    PIECES = 12
    PW = PC // PIECES
    STEPS = [TC * (c + 1) for c in range(NC)]
    NSTEP = sum(STEPS)
    ROUND = [(s, c, k) for s in range(2) for c in range(NC) for k in range(STEPS[c])]
    START = {(s, c): ROUND.index((s, c, 0)) for s in range(2) for c in range(NC)}

    def units(s, c):
        return [(s, c, t, j, b) for t in range(TC) for j in range(HG) for b in range(c + 1)]

    SHARED = [((0, 0), (0, 1), [(0, 1)]), ((0, 1), (0, 2), [(0, 2)]), ((0, 2), (0, 3), [(0, 3)]),
              ((0, 3), (1, 0), [(1, 0), (1, 1), (1, 2)]), ((1, 0), (1, 3), [(1, 3)])]
    PLAN = [[] for _ in ROUND]
    ROWS_AT = [[] for _ in ROUND]
    for first, last, chunks in SHARED:
        a, b = START[first], START[last] - 1
        todo = [x for s, c in chunks for x in units(s, c)]
        for n, x in enumerate(todo):
            at = a + n * (b - a) // len(todo)
            PLAN[at].append(x)
            if n + 1 == len(todo) or todo[n + 1][:2] != x[:2]:
                ROWS_AT[at + 1].append(x[:2])
    ROW_ORDER = [(0, 0)] + [x for at in ROWS_AT for x in at]
    NMX = 2 * sum(len(units(0, c)) for c in range(NC))
    NENTRY = HG * (2 * NSTEP + 2 * NC)
    first_piece = START[1, 0]
    PIECES_AT = [[] for _ in ROUND]
    for n in range(2 * PIECES):
        PIECES_AT[first_piece + n * (len(ROUND) - first_piece) // (2 * PIECES)].append(n)
    MX0 = 1000
    DELAY = 2

    def lo(c, k):
        return max(0, k - TC * c) * P

    def bank_width(c, t, b):
        return (t + 1) * P if b == c else C

    with ExitStack() as ctx:
        def sb(name, shape, dt=F32):
            return ctx.enter_context(nc.sbuf_tensor(name, shape, dt))

        def sem(name):
            return ctx.enter_context(nc.semaphore(name))

        q_st = [sb(f"q_st{s}", [P, HG, S], F16) for s in range(2)]
        k_st = [sb(f"k_st{s}", [P, HG, S], F16) for s in range(2)]
        v_g = [sb(f"v_g{s}", [P, ST, P]) for s in range(2)]
        ones = sb("ones", [P, HD])
        prob = sb("prob", [P, PR, HG, C])
        max_part = sb("max_part", [P, TC * HG, NC])
        row_max = sb("row_max", [P, TC * HG])
        max16 = sb("max16", [P, TC * HG], F16)
        sums_sb = sb("sums_sb", [P, C])
        recip = sb("recip", [P, C])
        y = sb("y", [P, 2, C])
        packed = sb("packed", [P, 2, PW], I32)
        shift = sb("shift", [P, 1], I32)
        bits = sb("bits", [P, PW], I32)
        four = sb("four", [P, PW], I32)
        clip = sb("clip", [P, PW])
        wo_stage = sb("wo_stage", [P, D])
        sc_ps = [ctx.enter_context(nc.psum_tensor(f"sc_ps{n}", [P, C], F32)) for n in range(BR)]
        mx_ps = [ctx.enter_context(nc.psum_tensor(f"mx_ps{n}", [P, C], F32)) for n in range(XR)]
        y_ps = ctx.enter_context(nc.psum_tensor("y_ps", [P, C], F32))
        sum_ps = ctx.enter_context(nc.psum_tensor("sum_ps", [P, C], F32))

        q_loaded = [sem(f"q_loaded{s}") for s in range(2)]
        k_loaded = [sem(f"k_loaded{s}") for s in range(2)]
        v_loaded = [sem(f"v_loaded{s}") for s in range(2)]
        packed_loaded = [sem(f"packed_loaded{n}") for n in range(2)]
        shift_loaded = sem("shift_loaded")
        wo_loaded = sem("wo_loaded")
        wo_split = sem("wo_split")
        consts = sem("consts_b")
        mx_ready = sem("mx_ready")
        mx_free = sem("mx_free")
        row_max_done = sem("row_max_done")
        max16_done = sem("max16_done")
        sc_ready = sem("sc_ready")
        rows_read = sem("rows_read")
        prob_ready = sem("prob_ready")
        step_done = sem("step_done")
        y_copied = sem("y_copied")
        sums_copied = sem("sums_copied")
        recip_done = sem("recip_done")
        y_done = sem("y_done")
        y_out = sem("y_out")
        y_free = sem("y_free")
        shifted = sem("shifted")
        four_set = sem("four_set")
        bits_set = sem("bits_set")
        clipped = sem("clipped")
        differed = sem("differed")
        decoded = sem("decoded")
        block = ctx.enter_context(nc.Block())

        @block.sync
        def _(sp):
            sp.dma_start(shift[:, :], io["shifts"]).then_inc(shift_loaded, 16)

            def load(u, s):
                sp.wait_ge(step_done, u * (2 * NSTEP) + s * NSTEP + PR)
                g = 2 * u + s
                for n, part in enumerate((0, 1, 0)):
                    sp.dma_start(k_st[s][n * HD:(n + 1) * HD, :, :],
                                 io["qk_parts"][bass.ds(g + KT, 1), part].rearrange("a (j d) s -> d (a j) s", j=HG))\
                      .then_inc(k_loaded[s], 16)
                for n, part in enumerate((0, 0, 1)):
                    sp.dma_start(q_st[s][n * HD:(n + 1) * HD, :, :],
                                 io["qk_parts"][bass.ds(g, 1), part].rearrange("a (j d) s -> d (a j) s", j=HG))\
                      .then_inc(q_loaded[s], 16)
                sp.dma_start(v_g[s][:, :, :], io["v_rows"][:, bass.ds(g * P, P)].rearrange("(t p) d -> p t d", p=P))\
                  .then_inc(v_loaded[s], 16)

            with sp.Fori(0, NG // 2) as u:
                load(u, 0)
                load(u, 1)

        @block.gpsimd
        def _(pool):
            pool.sem_inc(y_free, 2)
            nc.gpsimd.memset(ones[:, :], 1.0).then_inc(consts, 1)
            for n in range(2):
                pool.wait_ge(consts, n + 1)
                nc.gpsimd.memset(k_st[n][ROWM:ROWM + 1, :, :], -M_UNIT).then_inc(consts, 1)
            pool.wait_ge(consts, 3)
            for k in range(KT):
                if k:
                    pool.wait_ge(wo_split, 2 * k)
                pool.dma_start(wo_stage[:, :], io["w_out"][k]).then_inc(wo_loaded, 16)
                pool.wait_ge(wo_loaded, 16 * k + 16)
                nc.gpsimd.tensor_copy(keep["wo_hi"][:, k, :], wo_stage[:, :]).then_inc(wo_split, 1)
                pool.wait_ge(wo_split, 2 * k + 1)
                nc.gpsimd.tensor_tensor(keep["wo_lo"][:, k, :], wo_stage[:, :],
                                        keep["wo_hi"][:, k, :].bitcast(F32), ALU.subtract).then_inc(wo_split, 1)

            def load_piece(u, n):
                pool.wait_ge(shifted, u * (2 * PIECES) + n + 1)
                pool.dma_start(packed[:, n % 2, :], io["packed"][bass.ds(2 * u + n // PIECES, 1), :,
                                                                 (n % PIECES) * PW:(n % PIECES + 1) * PW]
                               .rearrange("a p n -> (a p) n")).then_inc(packed_loaded[n % 2], 16)

            def send(u, s, c):
                n = u * (2 * NC) + s * NC + c
                pool.wait_ge(y_done, n + 2)
                pool.dma_start(io["y_cols"][bass.ds((2 * u + s) * P, P), c * C:(c + 1) * C], y[:, c % 2, :])\
                    .then_inc(y_out, 16)
                pool.wait_ge(y_out, 16 * n + 16)
                pool.sem_inc(y_free, 1)

            with pool.Fori(0, NG // 2) as u:
                load_piece(u, 0)
                load_piece(u, 1)
                for at in range(len(ROUND) + DELAY):
                    for s, c in START:
                        if at == START[s, c] + STEPS[c] + DELAY - 1:
                            send(u, s, c)
                    if at < len(ROUND):
                        for n in PIECES_AT[at]:
                            if n + 2 < 2 * PIECES:
                                load_piece(u, n + 2)

        @block.scalar
        def _(act):
            act.sem_inc(prob_ready, 1)
            act.sem_inc(y_copied, 1)
            act.sem_inc(sums_copied, 1)

            def round_(u):
                entry = [0]

                def rows(s, c):
                    for j in range(HG):
                        act.wait_ge(sc_ready, u * NENTRY + entry[0] + 1)
                        nc.scalar.copy(q_st[s][ROWM:ROWM + 1, j, c * C:(c + 1) * C],
                                       sc_ps[entry[0] % BR][ROWM:ROWM + 1, :]).then_inc(rows_read, 1)
                        entry[0] += 1

                def copy_out(s, c):
                    n = u * (2 * NC) + s * NC + c
                    end = START[s, c] + STEPS[c]
                    act.wait_ge(step_done, u * (2 * NSTEP) + end + NSTEP + PR)
                    act.wait_ge(y_free, n + 1)
                    nc.scalar.copy(y[:, c % 2, :], y_ps[:, :]).then_inc(y_copied, 1)
                    act.wait_ge(recip_done, n + 1)
                    nc.scalar.copy(sums_sb[:, :], sum_ps[:, :]).then_inc(sums_copied, 1)

                rows(0, 0)
                for at, (s, c, k) in enumerate(ROUND):
                    for j in range(HG):
                        act.wait_ge(sc_ready, u * NENTRY + entry[0] + 1)
                        if j == 0:
                            act.wait_ge(step_done, u * (2 * NSTEP) + at + NSTEP + 1)
                        nc.scalar.activation(prob[:, at % PR, j, lo(c, k):C], sc_ps[entry[0] % BR][:, lo(c, k):C],
                                             ACT.Exp).then_inc(prob_ready, 1)
                        entry[0] += 1
                    if k == 0 and at:
                        copy_out(*ROUND[at - 1][:2])
                    for row in ROWS_AT[at]:
                        rows(*row)
                copy_out(1, NC - 1)

            with act.Fori(0, NG // 2) as u:
                round_(u)

        @block.vector
        def _(dve):
            dve.sem_inc(mx_free, MX0 + XR)
            dve.sem_inc(shifted, 2)
            for started in (y_done, recip_done, decoded):
                dve.sem_inc(started, 1)
            dve.wait_ge(shift_loaded, 16)

            def decode(u, n):
                k = u * (2 * PIECES) + n
                dve.wait_ge(packed_loaded[n % 2], u * (16 * PIECES) + 16 * (n // 2) + 16)
                dve.wait_ge(decoded, k + 1)
                nc.vector.tensor_scalar(bits[:, :], packed[:, n % 2, :], shift[:, :], 6,
                                        ALU.logical_shift_left, ALU.arith_shift_right).then_inc(shifted, 1)
                dve.wait_ge(shifted, k + 3)
                nc.vector.tensor_scalar(four[:, :], bits[:, :], -2 ** 31, 0x40800000,
                                        ALU.bitwise_and, ALU.bitwise_or).then_inc(four_set, 1)
                dve.wait_ge(four_set, k + 1)
                nc.vector.tensor_scalar(bits[:, :], bits[:, :], 0x81C00000 - 2 ** 32, 0x40000000,
                                        ALU.bitwise_and, ALU.bitwise_or).then_inc(bits_set, 1)
                dve.wait_ge(bits_set, k + 1)
                nc.vector.tensor_scalar(clip[:, :], bits[:, :].bitcast(F32), 4.0, -4.0, ALU.min, ALU.max)\
                  .then_inc(clipped, 1)
                dve.wait_ge(clipped, k + 1)
                nc.vector.tensor_tensor(clip[:, :], clip[:, :], four[:, :].bitcast(F32), ALU.subtract)\
                  .then_inc(differed, 1)
                dve.wait_ge(differed, k + 1)
                a = n % PIECES * PW
                g = 2 * u + n // PIECES
                if a < GU:
                    out = keep["w_gu"][:, bass.ds(g * GU + a, PW)]
                else:
                    out = keep["w_dn"][:, bass.ds(g * DN + (a - GU), PW)]
                nc.vector.tensor_tensor(out, clip[:, :], bits[:, :].bitcast(F32), ALU.add).then_inc(decoded, 1)

            def round_(u):
                unit = [0]
                rounded = [0]

                def maxima(todo):
                    for s, c, t, j, b in todo:
                        n = unit[0]
                        dve.wait_ge(mx_ready, u * NMX + n + 1)
                        nc.vector.reduce_max(max_part[:, t * HG + j, b:b + 1], mx_ps[n % XR][:, 0:bank_width(c, t, b)],
                                             X).then_inc(mx_free, 1)
                        unit[0] += 1
                        if (t, j, b) == (TC - 1, HG - 1, c):
                            round_max(c)

                def round_max(c):
                    dve.wait_ge(mx_free, u * NMX + MX0 + unit[0] + XR)
                    nc.vector.reduce_max(row_max[:, :], max_part[:, :, 0:c + 1], X).then_inc(row_max_done, 1)
                    rounded[0] += 1
                    dve.wait_ge(row_max_done, u * (2 * NC) + rounded[0])
                    nc.vector.tensor_scalar(max16[:, :], row_max[:, :], 1.0 / M_UNIT, None, ALU.mult)\
                      .then_inc(max16_done, 1)

                def normalize(s, c):
                    n = u * (2 * NC) + s * NC + c
                    dve.wait_ge(sums_copied, n + 2)
                    dve.wait_ge(y_done, n + 1)
                    nc.vector.reciprocal(recip[:, :], sums_sb[:, :]).then_inc(recip_done, 1)
                    dve.wait_ge(recip_done, n + 2)
                    dve.wait_ge(y_copied, n + 2)
                    nc.vector.tensor_tensor(y[:, c % 2, :], y[:, c % 2, :], recip[:, :], ALU.mult).then_inc(y_done, 1)

                maxima(units(0, 0))
                for at in range(len(ROUND) + DELAY):
                    if at < len(ROUND):
                        maxima(PLAN[at])
                    for s, c in START:
                        if at == START[s, c] + STEPS[c] + DELAY - 1:
                            normalize(s, c)
                    if at < len(ROUND):
                        for n in PIECES_AT[at]:
                            decode(u, n)

            with dve.Fori(0, NG // 2) as u:
                round_(u)

        @block.tensor
        def _(pe):
            pe.sem_inc(step_done, NSTEP + PR)
            pe.wait_ge(consts, 3)

            def round_(u):
                unit = [0]
                readers = []
                exps, copies = [0], [0]

                def wait_free():
                    if len(readers) < BR:
                        pe.wait_ge(prob_ready, u * (HG * 2 * NSTEP) + 1)
                    else:
                        signal, by_round, count = readers[-BR]
                        pe.wait_ge(signal, u * by_round + count)

                def maxima(todo):
                    for s, c, t, j, b in todo:
                        n = unit[0]
                        w = bank_width(c, t, b)
                        q0 = c * C + t * P
                        pe.wait_ge(mx_free, u * NMX + MX0 + n + 1)
                        last = nc.tensor.matmul(mx_ps[n % XR][:, 0:w], q_st[s][0:ROWM, j, q0:q0 + P],
                                                k_st[s][0:ROWM, j, b * C:b * C + w], start=True, stop=(b < c))
                        if b == c:
                            last = nc.tensor.matmul(mx_ps[n % XR][:, w - P:w], keep["identb"][:, :],
                                                    keep["mask_qk"][:, :], start=False, stop=True)
                        last.then_inc(mx_ready, 1)
                        unit[0] += 1

                def rows(s, c):
                    pe.wait_ge(max16_done, u * (2 * NC) + ROW_ORDER.index((s, c)) + 1)
                    for j in range(HG):
                        n = len(readers)
                        wait_free()
                        copies[0] += 1
                        readers.append((rows_read, HG * 2 * NC, copies[0]))
                        for t in range(TC):
                            last = nc.tensor.matmul(sc_ps[n % BR][ROWM:ROWM + 1, t * P:(t + 1) * P],
                                                    max16[:, t * HG + j:t * HG + j + 1], keep["ident16"][:, :],
                                                    start=True, stop=True)
                        last.then_inc(sc_ready, 1)

                def scores(s, c, k, heads):
                    a = lo(c, k)
                    for j in heads:
                        n = len(readers)
                        wait_free()
                        if k == 0 and j == 0:
                            pe.wait_ge(rows_read, u * (HG * 2 * NC) + HG * (ROW_ORDER.index((s, c)) + 1))
                        exps[0] += 1
                        readers.append((prob_ready, HG * 2 * NSTEP, exps[0] + 1))
                        last = nc.tensor.matmul(sc_ps[n % BR][:, a:C], k_st[s][0:ROWM + 1, j, k * P:(k + 1) * P],
                                                q_st[s][0:ROWM + 1, j, c * C + a:(c + 1) * C],
                                                start=True, stop=(k < TC * c))
                        if k >= TC * c:
                            last = nc.tensor.matmul(sc_ps[n % BR][:, a:a + P], keep["identb"][:, :],
                                                    keep["mask_kq"][:, :], start=False, stop=True)
                        last.then_inc(sc_ready, 1)

                def products(at):
                    s, c, k = ROUND[at]
                    a = lo(c, k)
                    pe.wait_ge(prob_ready, u * (HG * 2 * NSTEP) + HG * at + HG + 1)
                    if k == 0:
                        pe.wait_ge(y_copied, u * (2 * NC) + s * NC + c + 1)
                    for j in range(HG):
                        nc.tensor.matmul(y_ps[j * HD:(j + 1) * HD, a:C], v_g[s][:, k, j * HD:(j + 1) * HD],
                                         prob[:, at % PR, j, a:C], start=(k == 0), stop=(k == STEPS[c] - 1),
                                         tile_position=(0, j * HD))

                def sums(at):
                    s, c, k = ROUND[at]
                    a = lo(c, k)
                    if k == 0:
                        pe.wait_ge(sums_copied, u * (2 * NC) + s * NC + c + 1)
                    for j in range(HG):
                        last = nc.tensor.matmul(sum_ps[j * HD:(j + 1) * HD, a:C], ones[:, :],
                                                prob[:, at % PR, j, a:C], start=(k == 0), stop=(k == STEPS[c] - 1),
                                                tile_position=(0, j * HD))
                    last.then_inc(step_done, 1)

                for s in range(2):
                    pe.wait_ge(q_loaded[s], u * 48 + 48)
                    pe.wait_ge(k_loaded[s], u * 48 + 48)
                    if s == 0:
                        maxima(units(0, 0))
                        rows(0, 0)
                    pe.wait_ge(v_loaded[s], u * 16 + 16)
                for at, (s, c, k) in enumerate(ROUND):
                    todo = PLAN[at]
                    cut = [len(todo) * n // 6 for n in (0, 1, 3, 4, 6)]
                    scores(s, c, k, (0, 1))
                    maxima(todo[cut[0]:cut[1]])
                    if at:
                        products(at - 1)
                    maxima(todo[cut[1]:cut[2]])
                    scores(s, c, k, (2, 3))
                    maxima(todo[cut[2]:cut[3]])
                    if at:
                        sums(at - 1)
                    maxima(todo[cut[3]:cut[4]])
                    for row in ROWS_AT[at]:
                        rows(*row)
                products(len(ROUND) - 1)
                sums(len(ROUND) - 1)

            with pe.Fori(0, NG // 2) as u:
                round_(u)


def phase_c(nc, io, keep):
    LAG = 2
    HB = LAG + 1
    AB, DB, FB = 2, 4, 2
    GATE_UP = [(0, 0), (1, 0)] + [(s, k) for k in range(1, KT) for s in range(2)]
    NA, ND = IT * 4, IT * 8
    a_at, d_at = {}, {}
    for o in range(IT + LAG):
        if o < IT:
            for s, k in GATE_UP:
                ring = d_at if k else a_at
                ring["gu", o, s, k] = len(ring)
        if o >= LAG:
            for r in range(KT):
                ring = a_at if r % 2 else d_at
                ring["dn", o - LAG, r] = len(ring)
    assert (len(a_at), len(d_at)) == (NA, ND)

    with ExitStack() as ctx:
        def sb(name, shape, dt=F32):
            return ctx.enter_context(nc.sbuf_tensor(name, shape, dt))

        def sem(name):
            return ctx.enter_context(nc.semaphore(name))

        w_gu = keep["w_gu"][:, :].rearrange("p (k n) -> p k n", k=KT)
        w_dn = keep["w_dn"][:, :].rearrange("p (t o) -> p t o", t=IT)
        wo_hi, wo_lo, ident = keep["wo_hi"], keep["wo_lo"], keep["ident"]
        NSG, NSD = GU // P * KT, KT * IT
        sc16 = sb("sc16", [P, NSG + NSD], F16)
        sc = sb("sc", [P, NSG + NSD])
        sc_gu = sc[:, 0:NSG].rearrange("p (o k) -> p o k", k=KT)
        sc_dn = sc[:, NSG:NSG + NSD].rearrange("p (r t) -> p r t", t=IT)
        gate_rows = sb("gate_rows", [P, 2, D])
        gate_col = sb("gate_col", [P, P])
        gab = sb("gab", [P, D])
        eps = sb("eps_c", [P, 2])
        xy = sb("xy", [P, KT, C])
        y_hi = sb("y_hi", [P, 2, KT, P], F32R)
        y_lo = sb("y_lo", [P, 2, KT, P], F32R)
        prod = sb("prod", [P, 2, D])
        x1 = sb("x1", [P, ST, D])
        stats = sb("stats_c", [P, TC, 6])
        mv = sb("mv_c", [P, TC, 2])
        rstd = sb("rstd_c", [P, 2, TC])
        ht = sb("ht_c", [P, KT, C])
        h_hi = sb("h_hi_c", [P, KT, C], F32R)
        h_lo = sb("h_lo_c", [P, KT, C], F32R)
        gu = sb("gu", [P, 2, 2, C])
        h1 = sb("h1", [P, 2, C])
        h1_hi = sb("h1_hi", [P, HB, C], F32R)
        h1_lo = sb("h1_lo", [P, HB, C], F32R)
        tmp = sb("tmp", [P, 2, C])
        acc = sb("acc", [P, KT, C])
        junk = sb("junk", [P, D])
        sq = sb("sq", [P, TC])
        rms = sb("rms", [P, 2, TC])
        a_ps = [ctx.enter_context(nc.psum_tensor(f"a_ps{n}", [P, C], F32)) for n in range(AB)]
        d_ps = [ctx.enter_context(nc.psum_tensor(f"d_ps{n}", [P, C], F32)) for n in range(DB)]
        f_ps = [ctx.enter_context(nc.psum_tensor(f"f_ps{n}", [P, C], F32)) for n in range(FB)]

        scales_loaded = sem("scales_loaded")
        b_loaded = sem("b_loaded")
        consts = sem("consts_c")
        scaled = sem("scaled")
        col_set = sem("col_set")
        col_used = sem("col_used")
        gates_out = sem("gates_out")
        gab_done = sem("gab_done")
        y_loaded = sem("y_loaded")
        xy_free = sem("xy_free")
        load_started = sem("load_started")
        x_loaded = sem("x_loaded_c")
        y_hi_done = sem("y_hi_done")
        y_lo_done = sem("y_lo_done")
        prod_ready = sem("prod_ready")
        prod_read = sem("prod_read")
        bias_added = sem("bias_added")
        x1_done = sem("x1_done")
        stats_done = sem("stats_done_c")
        rows_seen = sem("rows_seen")
        mv_done = sem("mv_done_c")
        sd_done = sem("sd_done_c")
        rstd_done = sem("rstd_done_c")
        xn_done = sem("xn_done_c")
        tp_done = sem("tp_done_c")
        ht_done = sem("ht_done_c")
        h_hi_done = sem("h_hi_done_c")
        h_lo_done = sem("h_lo_done_c")
        a_ready = sem("a_ready")
        a_read = sem("a_read")
        d_ready = sem("d_ready")
        d_read = sem("d_read")
        silu_done = sem("silu_done_c")
        h1_done = sem("h1_done")
        h1_hi_done = sem("h1_hi_done")
        h1_lo_done = sem("h1_lo_done")
        tmp_added = sem("tmp_added")
        tail_ready = sem("tail_ready")
        rows_copied = sem("rows_copied")
        rows_squared = sem("rows_squared")
        rms_done = sem("rms_done")
        rms_inv = sem("rms_inv")
        normed = sem("normed")
        out_ready = sem("out_ready")
        out_sent = sem("out_sent")
        block = ctx.enter_context(nc.Block())

        @block.sync
        def _(sp):
            sp.sem_inc(out_sent, 1)
            sp.dma_start(sc16[:, :], io["scales"]).then_inc(scales_loaded, 16)
            sp.dma_start(gab[:, :], io["b_out"].partition_broadcast(P)).then_inc(b_loaded, 16)

            def load(i):
                sp.dma_start(x1[:, bass.ds(i * TC, TC), :], io["x"][bass.ds(i * C, C), :]
                             .rearrange("(t p) d -> p t d", p=P)).then_inc(x_loaded, 16)
                sp.wait_ge(tp_done, i * KT + 1)
                sp.sem_inc(xy_free, 1)
                sp.dma_start(xy[:, :, :], io["y_cols"][:, bass.ds(i * C, C)]
                             .rearrange("(f p) s -> p f s", p=P)).then_inc(y_loaded, 16)

            def chunk(i, more):
                if more:
                    sp.wait_ge(x_loaded, i * 16 + 16)
                    sp.wait_ge(y_loaded, i * 16 + 16)
                    sp.sem_inc(load_started, 1)
                    load(i + 1)
                for t in range(TC):
                    sp.wait_ge(out_ready, i * TC + t + 1)
                    sp.dma_start(io["out"][bass.ds(i * C + t * P, P), :], ht[:, t, :]).then_inc(out_sent, 16)

            load(0)
            with sp.Fori(0, NC - 1) as i:
                chunk(i, True)
            chunk(NC - 1, False)
            sp.wait_ge(out_sent, 16 * NC * TC + 1)

        @block.gpsimd
        def _(pool):
            for started in (h1_done, h1_lo_done, tmp_added):
                pool.sem_inc(started, 1)
            nc.gpsimd.memset(eps[:, 0:1], EPS).then_inc(consts, 1)
            nc.gpsimd.memset(eps[:, 1:2], RMS_EPS).then_inc(consts, 1)

            def add_bias(i):
                pool.wait_ge(gab_done, 1)
                pool.wait_ge(x_loaded, i * 16 + 16)
                for t in range(TC):
                    nc.gpsimd.tensor_tensor(x1[:, bass.ds(i * TC + t, 1), :].rearrange("p a d -> p (a d)"),
                                            x1[:, bass.ds(i * TC + t, 1), :].rearrange("p a d -> p (a d)"),
                                            gab[:, :], ALU.add).then_inc(bias_added, 1)

            def hidden(i, o):
                pool.wait_ge(silu_done, i * IT + o + 1)
                pool.wait_ge(d_read, i * ND + DB + d_at["gu", o, 1, KT - 1] + 1)
                nc.gpsimd.tensor_tensor(h1[:, o % 2, :], h1[:, o % 2, :], gu[:, o % 2, 1, :], ALU.mult)\
                  .then_inc(h1_done, 1)

            def add_down(i, t):
                if t == 0:
                    return
                for n, r in enumerate((1, 3)):
                    pool.wait_ge(a_read, i * NA + AB + a_at["dn", t, r] + 1)
                    nc.gpsimd.tensor_tensor(acc[:, r, :], acc[:, r, :], tmp[:, n, :], ALU.add)\
                      .then_inc(tmp_added, 1)

            def low(i, o):
                pool.wait_ge(h1_hi_done, i * IT + o + 1)
                nc.gpsimd.tensor_tensor(h1_lo[:, o % HB, :], h1[:, o % 2, :], h1_hi[:, o % HB, :].bitcast(F32),
                                        ALU.subtract).then_inc(h1_lo_done, 1)

            def chunk(i, more):
                for o in range(IT + LAG):
                    if 1 <= o <= IT:
                        hidden(i, o - 1)
                    if o >= LAG:
                        add_down(i, o - LAG)
                    if 1 <= o <= IT:
                        low(i, o - 1)
                    if o == 1 and more:
                        add_bias(i + 1)
                for t in range(TC):
                    pool.wait_ge(normed, i * TC + t + 1)
                    nc.gpsimd.tensor_tensor(ht[:, t, :], ht[:, t, :],
                                            x1[:, bass.ds(i * TC + t, 1), :].rearrange("p a d -> p (a d)"),
                                            ALU.add).then_inc(out_ready, 1)

            add_bias(0)
            with pool.Fori(0, NC - 1) as i:
                chunk(i, True)
            chunk(NC - 1, False)

        @block.scalar
        def _(act):
            act.sem_inc(a_read, AB)
            act.sem_inc(rows_squared, 1)

            def deviation(i):
                act.wait_ge(mv_done, i * TC + TC)
                nc.scalar.activation(rstd[:, 0, :], mv[:, :, 1], ACT.Sqrt, bias=eps[:, 0:1]).then_inc(sd_done, 1)

            def modulate(i, sent):
                act.wait_ge(out_sent, sent + 1)
                for f in range(KT):
                    act.wait_ge(tp_done, i * KT + f + 2)
                    nc.scalar.activation(ht[:, f, :], f_ps[(TC + f) % FB][:, :], ACT.Identity,
                                         bias=keep["ffn_mod"][:, 0, f:f + 1],
                                         scale=keep["ffn_mod"][:, 1, f:f + 1]).then_inc(ht_done, 1)

            def first_sums(i, o):
                act.wait_ge(h1_done, i * IT + max(0, o - 1) + 1)
                for s in range(2):
                    n = a_at["gu", o, s, 0]
                    act.wait_ge(a_ready, i * NA + n + 1)
                    nc.scalar.activation(gu[:, o % 2, s, :], a_ps[n % AB][:, :], ACT.Copy,
                                         scale=sc_gu[:, s * IT + o, 0:1]).then_inc(a_read, 1)

            def silu(i, o):
                act.wait_ge(d_read, i * ND + DB + d_at["gu", o, 0, KT - 1] + 1)
                act.wait_ge(h1_lo_done, i * IT + max(0, o - 1) + 1)
                nc.scalar.activation(h1[:, o % 2, :], gu[:, o % 2, 0, :], ACT.Silu).then_inc(silu_done, 1)

            def down(i, t):
                for n, r in enumerate((1, 3)):
                    at = a_at["dn", t, r]
                    act.wait_ge(a_ready, i * NA + at + 1)
                    if t == 0:
                        act.wait_ge(tail_ready, i * TC + 1)
                        out = acc[:, r, :]
                    else:
                        act.wait_ge(tmp_added, i * (2 * (IT - 1)) + max(0, 2 * (t - 2) + n + 1) + 1)
                        out = tmp[:, n, :]
                    nc.scalar.activation(out, a_ps[at % AB][:, :], ACT.Copy,
                                         scale=sc_dn[:, r, t:t + 1]).then_inc(a_read, 1)

            def high(i, o):
                act.wait_ge(h1_done, i * IT + o + 2)
                nc.scalar.activation(h1_hi[:, o % HB, :], h1[:, o % 2, :], ACT.Copy).then_inc(h1_hi_done, 1)

            def chunk(i, more):
                for o in range(IT + LAG):
                    if o < IT:
                        first_sums(i, o)
                    if 1 <= o <= IT:
                        silu(i, o - 1)
                    if o >= LAG:
                        down(i, o - LAG)
                    if 1 <= o <= IT:
                        high(i, o - 1)
                    if more and o == 3:
                        deviation(i + 1)
                    if more and o == 7:
                        modulate(i + 1, i * (16 * TC))
                act.wait_ge(out_sent, i * (16 * TC) + 1)
                act.wait_ge(h_lo_done, (i + 1) * KT + (KT if more else 0))
                for t in range(TC):
                    act.wait_ge(tail_ready, i * TC + t + 2)
                    nc.scalar.copy(ht[:, t, :], f_ps[(2 * TC + t) % FB][:, :]).then_inc(rows_copied, 1)
                    act.wait_ge(rows_squared, i * TC + t + 1)
                    nc.scalar.activation(junk[:, :], f_ps[(2 * TC + t) % FB][:, :], ACT.Square,
                                         accum_out=sq[:, t:t + 1]).then_inc(rows_squared, 1)
                act.wait_ge(rows_squared, i * TC + TC + 1)
                nc.scalar.activation(rms[:, 0, :], sq[:, :], ACT.Sqrt, bias=eps[:, 1:2], scale=1.0 / D)\
                  .then_inc(rms_done, 1)

            act.wait_ge(consts, 2)
            act.wait_ge(scaled, 1)
            deviation(0)
            modulate(0, 0)
            with act.Fori(0, NC - 1) as i:
                chunk(i, True)
            chunk(NC - 1, False)

        @block.vector
        def _(dve):
            dve.sem_inc(d_read, DB)
            dve.sem_inc(x1_done, 1)

            def split_y(i, t):
                if t == 0:
                    dve.wait_ge(y_loaded, i * 16 + 16)
                dve.wait_ge(prod_ready, i * TC + max(0, t - 1) + 1)
                cols = slice(t * P, (t + 1) * P)
                nc.vector.tensor_copy(y_hi[:, t % 2, :, :], xy[:, :, cols]).then_inc(y_hi_done, 1)
                dve.wait_ge(y_hi_done, i * TC + t + 1)
                nc.vector.tensor_tensor(y_lo[:, t % 2, :, :], xy[:, :, cols], y_hi[:, t % 2, :, :].bitcast(F32),
                                        ALU.subtract).then_inc(y_lo_done, 1)

            def residual(i):
                for t in range(TC):
                    dve.wait_ge(prod_ready, i * TC + t + 2)
                    dve.wait_ge(x1_done, i * TC + max(0, t - 1) + 1)
                    nc.vector.tensor_tensor(prod[:, t % 2, :], f_ps[t % FB][:, :], gate_rows[:, 0, :], ALU.mult)\
                      .then_inc(prod_read, 1)
                    if t + 2 < TC:
                        split_y(i, t + 2)
                    dve.wait_ge(prod_read, i * TC + t + 1)
                    dve.wait_ge(bias_added, i * TC + t + 1)
                    rows = x1[:, bass.ds(i * TC + t, 1), :].rearrange("p a d -> p (a d)")
                    nc.vector.tensor_tensor(rows, rows, prod[:, t % 2, :], ALU.add).then_inc(x1_done, 1)
                for t in range(TC):
                    dve.wait_ge(x1_done, i * TC + t + 2)
                    dve.sem_inc(rows_seen, 1)
                    nc.vector.bn_stats(stats[:, t, :], x1[:, bass.ds(i * TC + t, 1), :]
                                       .rearrange("p a d -> p (a d)")).then_inc(stats_done, 1)
                for t in range(TC):
                    dve.wait_ge(stats_done, i * TC + t + 1)
                    dve.sem_inc(rows_seen, 1)
                    nc.vector.bn_aggr(mv[:, t, :], stats[:, t, :]).then_inc(mv_done, 1)

            def normalize(i):
                dve.wait_ge(sd_done, i + 1)
                nc.vector.reciprocal(rstd[:, 1, :], rstd[:, 0, :]).then_inc(rstd_done, 1)
                dve.wait_ge(rstd_done, i + 1)
                dve.wait_ge(y_lo_done, i * TC + TC)
                for t in range(TC):
                    nc.vector.tensor_scalar(xy[:, t, :], x1[:, bass.ds(i * TC + t, 1), :]
                                            .rearrange("p a d -> p (a d)"), mv[:, t, 0:1], rstd[:, 1, t:t + 1],
                                            ALU.subtract, ALU.mult).then_inc(xn_done, 1)

            def split_h(i):
                for f in range(KT):
                    dve.wait_ge(ht_done, i * KT + f + 1)
                    nc.vector.tensor_copy(h_hi[:, f, :], ht[:, f, :]).then_inc(h_hi_done, 1)
                for f in range(KT):
                    dve.wait_ge(h_hi_done, i * KT + f + 1)
                    nc.vector.tensor_tensor(h_lo[:, f, :], ht[:, f, :], h_hi[:, f, :].bitcast(F32),
                                            ALU.subtract).then_inc(h_lo_done, 1)

            def gate_up(i, o):
                for s, k in GATE_UP:
                    if k == 0:
                        continue
                    n = d_at["gu", o, s, k]
                    dve.wait_ge(d_ready, i * ND + n + 1)
                    if k == 1:
                        dve.wait_ge(a_read, i * NA + AB + a_at["gu", o, s, 0] + 1)
                    else:
                        dve.wait_ge(d_read, i * ND + DB + d_at["gu", o, s, k - 1] + 1)
                    nc.vector.scalar_tensor_tensor(out=gu[:, o % 2, s, :], in0=d_ps[n % DB][:, :],
                                                   scalar=sc_gu[:, s * IT + o, k:k + 1], in1=gu[:, o % 2, s, :],
                                                   op0=ALU.mult, op1=ALU.add).then_inc(d_read, 1)

            def down(i, t):
                for r in (0, 2):
                    n = d_at["dn", t, r]
                    dve.wait_ge(d_ready, i * ND + n + 1)
                    if t == 0:
                        dve.wait_ge(tail_ready, i * TC + 1)
                        nc.vector.tensor_scalar(acc[:, r, :], d_ps[n % DB][:, :], sc_dn[:, r, 0:1], None,
                                                ALU.mult).then_inc(d_read, 1)
                    else:
                        dve.wait_ge(d_read, i * ND + DB + d_at["dn", t - 1, r] + 1)
                        nc.vector.scalar_tensor_tensor(out=acc[:, r, :], in0=d_ps[n % DB][:, :],
                                                       scalar=sc_dn[:, r, t:t + 1], in1=acc[:, r, :],
                                                       op0=ALU.mult, op1=ALU.add).then_inc(d_read, 1)

            def chunk(i, more):
                for o in range(IT + LAG):
                    if o < IT:
                        gate_up(i, o)
                    if o >= LAG:
                        down(i, o - LAG)
                    if more and o == 1:
                        split_y(i + 1, 0)
                        split_y(i + 1, 1)
                    if more and o == 3:
                        residual(i + 1)
                    if more and o == 4:
                        normalize(i + 1)
                    if more and o == IT - 1:
                        split_h(i + 1)
                dve.wait_ge(rms_done, i + 1)
                nc.vector.reciprocal(rms[:, 1, :], rms[:, 0, :]).then_inc(rms_inv, 1)
                dve.wait_ge(rms_inv, i + 1)
                for t in range(TC):
                    dve.wait_ge(rows_copied, i * TC + t + 1)
                    nc.vector.scalar_tensor_tensor(out=ht[:, t, :], in0=ht[:, t, :], scalar=rms[:, 1, t:t + 1],
                                                   in1=gate_rows[:, 1, :], op0=ALU.mult, op1=ALU.mult)\
                      .then_inc(normed, 1)

            dve.wait_ge(scales_loaded, 16)
            nc.vector.tensor_scalar(sc[:, :], sc16[:, :], 0.25, None, ALU.mult).then_inc(scaled, 1)
            for g in range(2):
                for f in range(KT):
                    n = g * KT + f
                    dve.wait_ge(col_used, n)
                    nc.vector.tensor_copy(gate_col[:, :], keep["gates"][:, g, f:f + 1].to_broadcast([P, P]))\
                      .then_inc(col_set, 1)
            for g in range(2):
                dve.wait_ge(col_used, 2 * KT)
                nc.vector.tensor_copy(gate_rows[:, g, :], f_ps[g][:, :]).then_inc(gates_out, 1)
            dve.wait_ge(gates_out, 2)
            dve.wait_ge(b_loaded, 16)
            nc.vector.tensor_tensor(gab[:, :], gab[:, :], gate_rows[:, 0, :], ALU.mult).then_inc(gab_done, 1)
            split_y(0, 0)
            split_y(0, 1)
            residual(0)
            normalize(0)
            split_h(0)
            with dve.Fori(0, NC - 1) as i:
                chunk(i, True)
            chunk(NC - 1, False)

        @block.tensor
        def _(pe):
            pe.sem_inc(tp_done, 1)
            pe.sem_inc(tail_ready, 1)
            pe.sem_inc(prod_ready, 1)
            for n in range(2 * KT):
                pe.wait_ge(col_set, n + 1)
                nc.tensor.matmul(f_ps[n // KT][:, (n % KT) * P:(n % KT + 1) * P], gate_col[:, :], ident[:, :],
                                 start=True, stop=True).then_inc(col_used, 1)

            def products(i):
                for t in range(TC):
                    if t < FB:
                        pe.wait_ge(rows_squared, (i - 1) * TC + 1 if not (isinstance(i, int) and i == 0) else 1)
                    else:
                        pe.wait_ge(prod_read, i * TC + t - 1)
                    pe.wait_ge(y_lo_done, i * TC + t + 1)
                    for f in range(KT):
                        for m, (a, b) in enumerate(((y_hi, wo_hi), (y_hi, wo_lo), (y_lo, wo_hi))):
                            last = nc.tensor.matmul(f_ps[t % FB][:, :], a[:, t % 2, f, :], b[:, f, :],
                                                    start=(f == 0 and m == 0), stop=(f == KT - 1 and m == 2))
                    last.then_inc(prod_ready, 1)

            def transposes(i):
                pe.wait_ge(xn_done, i * TC + TC)
                for f in range(KT):
                    if f < FB:
                        pe.wait_ge(prod_read, i * TC + TC)
                    else:
                        pe.wait_ge(ht_done, i * KT + f - 1)
                    for t in range(TC):
                        last = nc.tensor.transpose(f_ps[(TC + f) % FB][:, t * P:(t + 1) * P],
                                                   xy[:, t, f * P:(f + 1) * P], ident[:, :])
                    last.then_inc(tp_done, 1)

            def gate_up(i, o):
                if o == 0:
                    pe.wait_ge(h_lo_done, i * KT + KT)
                for s, k in GATE_UP:
                    cols = slice((s * IT + o) * P, (s * IT + o + 1) * P)
                    if k:
                        n = d_at["gu", o, s, k]
                        pe.wait_ge(d_read, i * ND + n + 1)
                        out, ready = d_ps[n % DB], d_ready
                    else:
                        n = a_at["gu", o, s, k]
                        pe.wait_ge(a_read, i * NA + n + 1)
                        out, ready = a_ps[n % AB], a_ready
                    nc.tensor.matmul(out[:, :], w_gu[:, k, cols], h_hi[:, k, :], start=True, stop=False)
                    nc.tensor.matmul(out[:, :], w_gu[:, k, cols], h_lo[:, k, :], start=False, stop=True)\
                      .then_inc(ready, 1)

            def down(i, t):
                pe.wait_ge(h1_lo_done, i * IT + t + 2)
                for r in range(KT):
                    cols = slice(r * P, (r + 1) * P)
                    if r % 2:
                        n = a_at["dn", t, r]
                        pe.wait_ge(a_read, i * NA + n + 1)
                        out, ready = a_ps[n % AB], a_ready
                    else:
                        n = d_at["dn", t, r]
                        pe.wait_ge(d_read, i * ND + n + 1)
                        out, ready = d_ps[n % DB], d_ready
                    nc.tensor.matmul(out[:, :], w_dn[:, t, cols], h1_hi[:, t % HB, :], start=True, stop=False)
                    nc.tensor.matmul(out[:, :], w_dn[:, t, cols], h1_lo[:, t % HB, :], start=False, stop=True)\
                      .then_inc(ready, 1)

            def tail(i, more):
                pe.wait_ge(d_read, i * ND + DB + ND)
                pe.wait_ge(tmp_added, (i + 1) * (2 * (IT - 1)) + 1)
                for t in range(TC):
                    if t < FB:
                        pe.wait_ge(ht_done, (i + 1) * KT + (KT if more else 0))
                    else:
                        pe.wait_ge(rows_squared, i * TC + t)
                    for r in range(KT):
                        last = nc.tensor.transpose(f_ps[(2 * TC + t) % FB][:, r * P:(r + 1) * P],
                                                   acc[:, r, t * P:(t + 1) * P], ident[:, :])
                    last.then_inc(tail_ready, 1)

            def chunk(i, more):
                for o in range(IT + LAG):
                    if o < IT:
                        gate_up(i, o)
                    if o >= LAG:
                        down(i, o - LAG)
                    if more and o == 3:
                        products(i + 1)
                    if more and o == 7:
                        transposes(i + 1)
                tail(i, more)

            pe.wait_ge(gates_out, 2)
            products(0)
            transposes(0)
            with pe.Fori(0, NC - 1) as i:
                chunk(i, True)
            chunk(NC - 1, False)


def adaln_layer(nc, io):
    with ExitStack() as ctx:
        def sb(name, shape, dt=F32):
            return ctx.enter_context(nc.sbuf_tensor(name, shape, dt))

        keep = {
            "ident": sb("ident", [P, P]), "ident16": sb("ident16", [P, P], F16), "identb": sb("identb", [P, P], BF16),
            "mask_qk": sb("mask_qk", [P, P], BF16), "mask_kq": sb("mask_kq", [P, P], BF16),
            "gates": sb("gates", [P, 2, KT]), "ffn_mod": sb("ffn_mod", [P, 2, KT]),
        }
        for name, shape, dt in (("qk_parts", [2 * KT, 2, P, S], F16), ("v_rows", [S, D], F32), ("y_cols", [D, S], F32)):
            io[name] = nc.dram_tensor(name, shape, dt, kind="Internal").ap()
        phase_a(nc, io, keep)
        for name, shape in (("w_gu", [P, KT * GU]), ("w_dn", [P, IT * D]), ("wo_hi", [P, KT, D]), ("wo_lo", [P, KT, D])):
            keep[name] = sb(name, shape, F32R)
        phase_b(nc, io, keep)
        phase_c(nc, io, keep)


def kernel(L0_attn_x, L0_attn_w_qkv, L0_attn_b_qkv, L0_attn_w_out, L0_attn_b_out, L0_ffn_gate_up_packed,
           L0_ffn_gate_up_scales, L0_ffn_down_packed, L0_ffn_down_scales, L0_c, L0_wmod):
    import numpy as np
    from concourse import bacc
    from concourse.bass_utils import run_bass_kernel_spmd

    def nibble_order(n):
        return np.arange(n).reshape(n // P, WG, NIB).transpose(0, 2, 1).reshape(n)

    fo, ho = nibble_order(D), nibble_order(NI)
    gu_order = np.concatenate([ho, NI + ho])
    a = {k: np.asarray(v) for k, v in locals().items() if k.startswith("L0_")}
    gu = a["L0_ffn_gate_up_packed"][gu_order].T.reshape(KT, WG, GU)
    dn = a["L0_ffn_down_packed"][fo].T.reshape(IT, WG, D).transpose(1, 0, 2).reshape(WG, NG, DN).transpose(1, 0, 2)
    gus = a["L0_ffn_gate_up_scales"][:, gu_order].reshape(KT, GU // P, P).transpose(2, 1, 0).reshape(P, -1)
    dns = a["L0_ffn_down_scales"][:, fo].reshape(IT, KT, P).transpose(2, 1, 0).reshape(P, -1)
    arrays = {
        "x": a["L0_attn_x"].reshape(S, D)[:, fo],
        "c": a["L0_c"].reshape(D),
        "wmod": a["L0_wmod"].T.reshape(6, D, D)[:, fo].reshape(6, KT, P, D),
        "w_qkv": a["L0_attn_w_qkv"][fo].reshape(KT, P, 3 * D),
        "bias_qk": a["L0_attn_b_qkv"][:2 * D].reshape(2 * KT, P).T,
        "bias_v": a["L0_attn_b_qkv"][2 * D:],
        "w_out": a["L0_attn_w_out"][:, fo].reshape(KT, P, D),
        "b_out": a["L0_attn_b_out"][fo],
        "packed": np.tile(np.concatenate([gu, dn], axis=2), (1, NIB, 1)),
        "scales": np.concatenate([gus, dns], axis=1),
        "shifts": (28 - 4 * (np.arange(P) // WG)).astype(np.int32).reshape(P, 1),
    }
    arrays = {k: np.ascontiguousarray(v) for k, v in arrays.items()}
    nc = bacc.Bacc("TRN2", target_bir_lowering=False, num_devices=1)
    io = {k: nc.dram_tensor(f"in_{k}", v.shape, mybir.dt.from_np(v.dtype), kind="ExternalInput").ap()
          for k, v in arrays.items()}
    io["out"] = nc.dram_tensor("out_0", (S, D), F32, kind="ExternalOutput").ap()
    adaln_layer(nc, io)
    r = run_bass_kernel_spmd(nc, [{f"in_{k}": v for k, v in arrays.items()}], core_ids=[0])
    out = np.empty((1, S, D), np.float32)
    out[0][:, fo] = r.results[0]["out_0"].reshape(S, D)
    return out
```

```python
from contextlib import ExitStack

import concourse.bass as bass
from concourse import mybir

P = 128
S, D, H = 2048, 512, 16
HD = D // H
KT = D // P
C = 512
TC = C // P
NC = S // C
ST = S // P
HG = P // HD
NG = H // HG
NI = 1408
IT = NI // P
GU = 2 * NI
WG = 16
NIB = 8
DN = IT * D // NG
PC = GU + DN
EPS = 1e-5
RMS_EPS = 1e-6
MASKED = -1e30
M_UNIT = 64.0
SA, CA, GA, SB, CB, GB = range(6)

F32, F32R = mybir.dt.float32, mybir.dt.float32r
F16, BF16, I32 = mybir.dt.float16, mybir.dt.bfloat16, mybir.dt.int32
ALU = mybir.AluOpType
ACT = mybir.ActivationFunctionType
X = mybir.AxisListType.X


def phase_a(nc, io, keep):
    QK = 2 * KT
    QS = 4
    with ExitStack() as ctx:
        def sb(name, shape, dt=F32):
            return ctx.enter_context(nc.sbuf_tensor(name, shape, dt))

        def sem(name):
            return ctx.enter_context(nc.semaphore(name))

        w_stage = sb("w_stage", [P, KT, 3 * D])
        w_hi = sb("w_hi", [P, KT, 3 * D], F32R)
        w_lo = sb("w_lo", [P, KT, 3 * D], F32R)
        mod_w = sb("mod_w", [P, 2, KT, D])
        mod_junk = sb("mod_junk", [P, D])
        c_row = sb("c_row", [P, D])
        mods = sb("mods", [P, 6, KT])
        absg = sb("absg", [P, 2, KT])
        bias_qk = sb("bias_qk", [P, QK])
        bias_v = sb("bias_v", [P, D])
        eps = sb("eps_a", [P, 1])
        xs = sb("xs", [P, TC, D])
        stats = sb("stats_a", [P, TC, 6])
        mv = sb("mv_a", [P, TC, 2])
        rstd = sb("rstd_a", [P, 2, TC])
        xn = sb("xn_a", [P, TC, D])
        ht = sb("ht_a", [P, KT, C])
        h_hi = sb("h_hi_a", [P, KT, C], F32R)
        h_lo = sb("h_lo_a", [P, KT, C], F32R)
        qf = sb("qf", [P, 2, C])
        qs = sb("qs", [P, QS, 2, C], F16)
        vf = sb("vf", [P, 2, D])
        tp = [ctx.enter_context(nc.psum_tensor(f"tp_a{f}", [P, C], F32)) for f in range(KT)]
        qk_ps = [ctx.enter_context(nc.psum_tensor(f"qk_ps{n}", [P, C], F32)) for n in range(2)]
        v_ps = [ctx.enter_context(nc.psum_tensor(f"v_ps{n}", [P, D], F32)) for n in range(2)]

        w_loaded = [sem(f"w_loaded{k}") for k in range(KT)]
        small_loaded = sem("small_loaded")
        mod_loaded = [sem(f"mod_loaded{n}") for n in range(2)]
        x_loaded = sem("x_loaded")
        silu_done = sem("silu_done")
        mod_done = sem("mod_done")
        clamp_step = sem("clamp_step")
        masks_set = sem("masks_set")
        masks_cut = sem("masks_cut")
        const_done = sem("const_done_a")
        w_hi_done = sem("w_hi_done")
        w_lo_by_pool = sem("w_lo_by_pool")
        w_lo_done = sem("w_lo_done")
        stats_done = sem("stats_done_a")
        stats_seen = sem("stats_seen_a")
        mv_done = sem("mv_done_a")
        sd_done = sem("sd_done_a")
        rstd_done = sem("rstd_done_a")
        xn_done = sem("xn_done_a")
        tp_done = sem("tp_done_a")
        ht_done = sem("ht_done_a")
        h_hi_done = sem("h_hi_done_a")
        h_lo_done = sem("h_lo_done_a")
        qk_ready = sem("qk_ready")
        qk_evac = sem("qk_evac")
        qk_hi_done = sem("qk_hi_done")
        qk_lo_done = sem("qk_lo_done")
        v_ready = sem("v_ready")
        v_evac = sem("v_evac")
        qk_out = [sem(f"qk_out{n}") for n in range(QS)]
        v_out = [sem(f"v_out{n}") for n in range(2)]

        MOD_ORDER = [SA, CA, GA, SB, CB, GB]
        UNITS = [("qk", 0), ("qk", 1), ("v", 0), ("qk", 2), ("qk", 3), ("v", 1),
                 ("qk", 4), ("qk", 5), ("v", 2), ("qk", 6), ("qk", 7), ("v", 3)]
        block = ctx.enter_context(nc.Block())

        @block.sync
        def _(sp):
            for started in (*qk_out, *v_out):
                sp.sem_inc(started, 1)

            def load_x(i):
                sp.dma_start(xs[:, :, :], io["x"][bass.ds(i * C, C), :]
                             .rearrange("(t p) d -> p t d", p=P)).then_inc(x_loaded, 16)

            load_x(0)

            def chunk(i, more):
                if more:
                    sp.wait_ge(xn_done, i * TC + TC)
                    load_x(i + 1)
                for kind, n in UNITS:
                    if kind == "qk":
                        sp.wait_ge(qk_lo_done, i * QK + n + 2)
                        sp.dma_start(io["qk_parts"][n].rearrange("l p s -> p l s")[:, :, bass.ds(i * C, C)],
                                     qs[:, n % QS, :, :]).then_inc(qk_out[n % QS], 16)
                    else:
                        sp.wait_ge(v_evac, i * TC + n + 3)
                        sp.dma_start(io["v_rows"][bass.ds(i * C + n * P, P), :],
                                     vf[:, n % 2, :]).then_inc(v_out[n % 2], 16)

            with sp.Fori(0, NC - 1) as i:
                chunk(i, True)
            chunk(NC - 1, False)
            for n in range(QS):
                sp.wait_ge(qk_out[n], 16 * NC * QK // QS + 1)
            for n in range(2):
                sp.wait_ge(v_out[n], 16 * NC * TC // 2 + 1)

        @block.gpsimd
        def _(pool):
            ident, ident16, identb = keep["ident"], keep["ident16"], keep["identb"]
            mask_qk, mask_kq = keep["mask_qk"], keep["mask_kq"]
            nc.gpsimd.memset(eps[:, :], EPS).then_inc(const_done, 1)
            nc.gpsimd.memset(ident[:, :], 0.0).then_inc(masks_set, 1)
            pool.wait_ge(masks_set, 1)
            nc.gpsimd.affine_select(out=ident[:, :], in_=ident[:, :], compare_op=ALU.not_equal, fill=1.0, base=0,
                                    pattern=[[-1, P]], channel_multiplier=1).then_inc(masks_cut, 1)
            for k in range(KT // 2):
                pool.wait_ge(w_hi_done, k + 1)
                nc.gpsimd.tensor_tensor(w_lo[:, k, :], w_stage[:, k, :], w_hi[:, k, :].bitcast(F32),
                                        ALU.subtract).then_inc(w_lo_by_pool, 1)
            for t in (ident16, identb, mask_qk, mask_kq):
                nc.gpsimd.memset(t[:, :], 0.0).then_inc(masks_set, 1)
            pool.wait_ge(masks_set, 5)
            for t in (ident16, identb):
                nc.gpsimd.affine_select(out=t[:, :], in_=t[:, :], compare_op=ALU.not_equal, fill=1.0, base=0,
                                        pattern=[[-1, P]], channel_multiplier=1).then_inc(masks_cut, 1)
            nc.gpsimd.affine_select(out=mask_qk[:, :], in_=mask_qk[:, :], compare_op=ALU.is_ge, fill=MASKED, base=0,
                                    pattern=[[-1, P]], channel_multiplier=1).then_inc(masks_cut, 1)
            nc.gpsimd.affine_select(out=mask_kq[:, :], in_=mask_kq[:, :], compare_op=ALU.is_ge, fill=MASKED, base=0,
                                    pattern=[[1, P]], channel_multiplier=-1).then_inc(masks_cut, 1)

        @block.scalar
        def _(act):
            act.sem_inc(qk_evac, 2)
            act.sem_inc(ht_done, 1)
            act.dma_start(c_row[:, :], io["c"].partition_broadcast(P)).then_inc(small_loaded, 16)
            act.dma_start(bias_qk[:, :], io["bias_qk"]).then_inc(small_loaded, 16)
            act.dma_start(bias_v[:, :], io["bias_v"].partition_broadcast(P)).then_inc(small_loaded, 16)

            def load_mod(n):
                act.dma_start(mod_w[:, n % 2, :, :], io["wmod"][MOD_ORDER[n]].rearrange("f p k -> p f k"))\
                   .then_inc(mod_loaded[n % 2], 16)

            load_mod(0)
            load_mod(1)
            for k in range(KT):
                act.dma_start(w_stage[:, k, :], io["w_qkv"][k]).then_inc(w_loaded[k], 16)
            act.wait_ge(small_loaded, 48)
            nc.scalar.activation(c_row[:, :], c_row[:, :], ACT.Silu).then_inc(silu_done, 1)
            nc.scalar.preload_act_table(ACT.Sqrt)

            def deviation(i):
                act.wait_ge(mv_done, i * TC + TC)
                nc.scalar.activation(rstd[:, 0, :], mv[:, :, 1], ACT.Sqrt, bias=eps[:, :]).then_inc(sd_done, 1)

            def modulate(i, tiles=range(KT)):
                for f in tiles:
                    act.wait_ge(tp_done, i * KT + f + 2)
                    act.wait_ge(h_lo_done, i * KT + 1)
                    nc.scalar.activation(ht[:, f, :], tp[f][:, :], ACT.Identity, bias=mods[:, SA, f:f + 1],
                                         scale=mods[:, CA, f:f + 1]).then_inc(ht_done, 1)

            act.wait_ge(const_done, 1)
            deviation(0)
            for k in range(KT):
                act.wait_ge(w_loaded[k], 16)
                nc.scalar.activation(w_hi[:, k, :], w_stage[:, k, :], ACT.Copy).then_inc(w_hi_done, 1)
            act.wait_ge(mod_done, 2)
            modulate(0)
            for n in range(2, 4):
                load_mod(n)

            def chunk(i, more):
                for n in range(QK):
                    if more and n == 4:
                        deviation(i + 1)
                    act.wait_ge(qk_ready, i * QK + n + 2)
                    if n >= 2:
                        act.wait_ge(qk_lo_done, i * QK + n)
                    else:
                        act.wait_ge(qk_lo_done, i * QK + 1)
                    nc.scalar.activation(qf[:, n % 2, :], qk_ps[n % 2][:, :], ACT.Identity,
                                         bias=bias_qk[:, n:n + 1],
                                         scale=HD ** -0.5 if n < KT else 1.0).then_inc(qk_evac, 1)
                    if not more and n in (3, 5):
                        act.wait_ge(mod_done, 3 + (n == 5))
                        load_mod(4 + (n == 5))
                    if more and n >= QK - 2:
                        modulate(i + 1, (0, 1) if n == QK - 2 else (2, 3))

            act.wait_ge(clamp_step, 1)
            with act.Fori(0, NC - 1) as i:
                chunk(i, True)
            chunk(NC - 1, False)

        @block.vector
        def _(dve):
            dve.sem_inc(v_evac, 2)
            dve.sem_inc(h_lo_done, 1)
            dve.sem_inc(qk_lo_done, 1)

            def statistics(i, t):
                if t == 0:
                    dve.wait_ge(x_loaded, i * 16 + 16)
                nc.vector.bn_stats(stats[:, t, :], xs[:, t, :]).then_inc(stats_done, 1)
                dve.wait_ge(stats_done, i * TC + t + 1)
                dve.sem_inc(stats_seen, 1)
                nc.vector.bn_aggr(mv[:, t, :], stats[:, t, :]).then_inc(mv_done, 1)

            def normalize(i):
                dve.wait_ge(sd_done, i + 1)
                nc.vector.reciprocal(rstd[:, 1, :], rstd[:, 0, :]).then_inc(rstd_done, 1)
                dve.wait_ge(rstd_done, i + 1)
                dve.wait_ge(tp_done, i * KT + 1)
                for t in range(TC):
                    nc.vector.tensor_scalar(xn[:, t, :], xs[:, t, :], mv[:, t, 0:1], rstd[:, 1, t:t + 1],
                                            ALU.subtract, ALU.mult).then_inc(xn_done, 1)

            def split_h(i):
                dve.wait_ge(qk_ready, i * QK + 1)
                dve.wait_ge(v_ready, i * TC + 1)
                for f in range(KT):
                    dve.wait_ge(ht_done, i * KT + f + 2)
                    nc.vector.tensor_copy(h_hi[:, f, :], ht[:, f, :]).then_inc(h_hi_done, 1)
                    dve.wait_ge(h_hi_done, i * KT + f + 1)
                    nc.vector.tensor_tensor(h_lo[:, f, :], ht[:, f, :], h_hi[:, f, :].bitcast(F32),
                                            ALU.subtract).then_inc(h_lo_done, 1)

            products = [0]

            def modulation(n):
                m = MOD_ORDER[n]
                dve.wait_ge(mod_loaded[n % 2], 16 * (n // 2) + 16)
                for f in range(KT):
                    if products[0]:
                        dve.wait_ge(clamp_step, products[0])
                    products[0] += 1
                    last = nc.vector.scalar_tensor_tensor(
                        out=mod_junk[:, :], in0=mod_w[:, n % 2, f, :], scalar=1.0, in1=c_row[:, :],
                        op0=ALU.mult, op1=ALU.mult, accum_out=mods[:, m, f:f + 1]).then_inc(clamp_step, 1)
                dve.wait_ge(clamp_step, products[0])
                if m in (CA, CB):
                    nc.vector.tensor_scalar(mods[:, m, :], mods[:, m, :], 1.0, None, ALU.add).then_inc(mod_done, 1)
                elif m in (GA, GB):
                    g = 0 if m == GA else 1
                    nc.vector.scalar_tensor_tensor(out=absg[:, g, :], in0=mods[:, m, :], scalar=-1.0,
                                                   in1=mods[:, m, :], op0=ALU.mult, op1=ALU.max)\
                      .then_inc(clamp_step, 1)
                    dve.wait_ge(clamp_step, products[0] + 1)
                    nc.vector.tensor_scalar(absg[:, g, :], absg[:, g, :], 0.25, None, ALU.max)\
                      .then_inc(clamp_step, 1)
                    nc.vector.tensor_scalar(mods[:, m, :], mods[:, m, :], 0.0, 2.0, ALU.is_ge, ALU.mult)\
                      .then_inc(clamp_step, 1)
                    products[0] += 3
                    dve.wait_ge(clamp_step, products[0])
                    nc.vector.scalar_tensor_tensor(out=keep["gates"][:, g, :], in0=mods[:, m, :], scalar=-1.0,
                                                   in1=absg[:, g, :], op0=ALU.add, op1=ALU.mult)\
                      .then_inc(mod_done, 1)
                else:
                    nc.vector.tensor_scalar(mods[:, m, :], mods[:, m, :], 1.0, None, ALU.mult).then_inc(mod_done, 1)
                if m in (SB, CB):
                    dve.wait_ge(mod_done, n + 1)
                    nc.vector.tensor_copy(keep["ffn_mod"][:, m - SB, :], mods[:, m, :]).then_inc(clamp_step, 1)
                    products[0] += 1

            for t in range(TC):
                statistics(0, t)
            normalize(0)
            dve.wait_ge(small_loaded, 48)
            nc.vector.tensor_scalar(bias_qk[:, 0:KT], bias_qk[:, 0:KT], HD ** -0.5, None, ALU.mult)\
              .then_inc(clamp_step, 1)
            products[0] += 1
            dve.wait_ge(silu_done, 1)
            modulation(0)
            modulation(1)
            for k in range(KT // 2, KT):
                dve.wait_ge(w_hi_done, k + 1)
                nc.vector.tensor_tensor(w_lo[:, k, :], w_stage[:, k, :], w_hi[:, k, :].bitcast(F32),
                                        ALU.subtract).then_inc(w_lo_done, 1)
            split_h(0)

            def chunk(i, more):
                for at, (kind, n) in enumerate(UNITS):
                    if kind == "qk":
                        dve.wait_ge(qk_evac, i * QK + n + 3)
                        dve.wait_ge(qk_out[n % QS], i * (16 * QK // QS) + 16 * (n // QS) + 1)
                        nc.vector.tensor_copy(qs[:, n % QS, 0, :], qf[:, n % 2, :]).then_inc(qk_hi_done, 1)
                        dve.wait_ge(qk_hi_done, i * QK + n + 1)
                        nc.vector.tensor_tensor(qs[:, n % QS, 1, :], qf[:, n % 2, :], qs[:, n % QS, 0, :],
                                                ALU.subtract).then_inc(qk_lo_done, 1)
                    else:
                        dve.wait_ge(v_ready, i * TC + n + 2)
                        dve.wait_ge(v_out[n % 2], i * (16 * TC // 2) + 16 * (n // 2) + 1)
                        nc.vector.tensor_tensor(vf[:, n % 2, :], v_ps[n % 2][:, :], bias_v[:, :],
                                                ALU.add).then_inc(v_evac, 1)
                    if more and at < TC:
                        statistics(i + 1, at)
                    if more and at == TC + 1:
                        normalize(i + 1)
                    if not more and at % 3 == 1:
                        modulation(2 + at // 3)
                if more:
                    split_h(i + 1)

            with dve.Fori(0, NC - 1) as i:
                chunk(i, True)
            chunk(NC - 1, False)

        @block.tensor
        def _(pe):
            pe.sem_inc(tp_done, 1)
            pe.sem_inc(qk_ready, 1)
            pe.sem_inc(v_ready, 1)

            def transposes(i):
                pe.wait_ge(xn_done, i * TC + TC)
                for f in range(KT):
                    pe.wait_ge(ht_done, i * KT + 1)
                    for t in range(TC):
                        last = nc.tensor.transpose(tp[f][:, t * P:(t + 1) * P], xn[:, t, f * P:(f + 1) * P],
                                                   keep["ident"][:, :])
                    last.then_inc(tp_done, 1)

            def project(i, kind, n):
                if kind == "qk":
                    pe.wait_ge(qk_evac, i * QK + n + 1)
                else:
                    pe.wait_ge(v_evac, i * TC + n + 1)
                for f in range(KT):
                    if (kind, n) == UNITS[0]:
                        pe.wait_ge(h_lo_done, i * KT + f + 2)
                    if kind == "qk":
                        cols = slice(n * P, (n + 1) * P)
                        parts = [(w_hi[:, f, cols], h_hi[:, f, :]), (w_lo[:, f, cols], h_hi[:, f, :]),
                                 (w_hi[:, f, cols], h_lo[:, f, :])]
                        out = qk_ps[n % 2]
                    else:
                        rows = slice(n * P, (n + 1) * P)
                        wv = slice(2 * D, 3 * D)
                        parts = [(h_hi[:, f, rows], w_hi[:, f, wv]), (h_hi[:, f, rows], w_lo[:, f, wv]),
                                 (h_lo[:, f, rows], w_hi[:, f, wv])]
                        out = v_ps[n % 2]
                    for m, (stat, mov) in enumerate(parts):
                        last = nc.tensor.matmul(out[:, :], stat, mov, start=(f == 0 and m == 0),
                                                stop=(f == KT - 1 and m == 2))
                last.then_inc(qk_ready if kind == "qk" else v_ready, 1)

            def chunk(i, more):
                for u, (kind, n) in enumerate(UNITS):
                    project(i, kind, n)
                    if more and u == len(UNITS) - 4:
                        transposes(i + 1)

            pe.wait_ge(masks_cut, 1)
            transposes(0)
            pe.wait_ge(w_lo_by_pool, KT // 2)
            pe.wait_ge(w_lo_done, KT // 2)
            with pe.Fori(0, NC - 1) as i:
                chunk(i, True)
            chunk(NC - 1, False)


def phase_b(nc, io, keep):
    BR, XR, PR = 3, 3, 3
    ROWM = 3 * HD
    PIECES = 12
    PW = PC // PIECES
    DOWN_PIECES = DN // PW
    STEPS = [TC * (c + 1) for c in range(NC)]
    NSTEP = sum(STEPS)
    ROUND = [(s, c, k) for s in range(2) for c in range(NC) for k in range(STEPS[c])]
    START = {(s, c): ROUND.index((s, c, 0)) for s in range(2) for c in range(NC)}

    def units(s, c):
        return [(s, c, t, j, b) for t in range(TC) for j in range(HG) for b in range(c + 1)]

    NMX = 2 * sum(len(units(0, c)) for c in range(NC))
    AHEAD = 44
    BEFORE = (units(0, 0) + units(0, 1))[:AHEAD]
    TODO = [x for s in range(3) for c in range(NC) for x in units(s, c)][AHEAD:AHEAD + NMX]
    PLAN = [[] for _ in ROUND]
    ROWS_AT = [[] for _ in ROUND]
    for s, first, end in ((0, 0, START[0, 3] - 3), (1, START[0, 3] - 3, START[1, 3] - 2),
                          (2, START[1, 3] - 2, len(ROUND) - 2)):
        todo = [x for x in TODO if x[0] == s]
        for n, x in enumerate(todo):
            at = first + n * (end - first) // len(todo)
            PLAN[at].append(x)
            if x[2:] == (TC - 1, HG - 1, x[1]):
                ROWS_AT[at + 1].append(x[:2])
                assert s == 2 or at + 1 < START[x[:2]]
    ROW_ORDER = [(0, 0)] + [x for at in ROWS_AT for x in at]
    assert BEFORE[len(units(0, 0)) - 1] == units(0, 0)[-1] and ROW_ORDER[-1] == (2, 0) and not ROWS_AT[-1]
    NENTRY = HG * 2 * NSTEP + 2 * NC
    PIECE_ORDER = sorted(((s, p) for s in range(2) for p in range(PIECES)), key=lambda x: x[1] < PIECES - DOWN_PIECES)
    SPARSE = 2 * DOWN_PIECES + 8
    PIECES_AT = [[] for _ in ROUND]
    for n in range(2 * PIECES):
        a, b = START[0, 3], START[1, 3]
        if n < SPARSE:
            PIECES_AT[a + n * (b - a) // SPARSE].append(n)
        else:
            PIECES_AT[b + (n - SPARSE) * (len(ROUND) - b) // (2 * PIECES - SPARSE)].append(n)
    MX0 = 1000
    PACE = 2
    DELAY = 2

    def lo(c, k):
        return max(0, k - TC * c) * P

    def bank_width(c, t, b):
        return (t + 1) * P if b == c else C

    with ExitStack() as ctx:
        def sb(name, shape, dt=F32):
            return ctx.enter_context(nc.sbuf_tensor(name, shape, dt))

        def sem(name):
            return ctx.enter_context(nc.semaphore(name))

        q_st = [sb(f"q_st{s}", [P, HG, S], F16) for s in range(2)]
        k_st = [sb(f"k_st{s}", [P, HG, S], F16) for s in range(2)]
        v_g = [sb(f"v_g{s}", [P, ST, P]) for s in range(2)]
        ones = sb("ones", [P, HD])
        prob = sb("prob", [P, PR, HG, C])
        max_part = sb("max_part", [P, TC * HG, NC])
        row_max = sb("row_max", [P, TC * HG])
        max16 = sb("max16", [P, TC * HG], F16)
        sums_sb = sb("sums_sb", [P, C])
        recip = sb("recip", [P, C])
        y = sb("y", [P, 2, C])
        packed = sb("packed", [P, 2, PW], I32)
        shift = sb("shift", [P, 1], I32)
        bits = sb("bits", [P, PW], I32)
        four = sb("four", [P, PW], I32)
        clip = sb("clip", [P, PW])
        down_val = sb("down_val", [P, PW])
        down_scale = sb("down_scale", [P, PW], F16)
        down_lo = sb("down_lo", [P, PW], F32R)
        sc_ps = [ctx.enter_context(nc.psum_tensor(f"sc_ps{n}", [P, C], F32)) for n in range(BR)]
        mx_ps = [ctx.enter_context(nc.psum_tensor(f"mx_ps{n}", [P, C], F32)) for n in range(XR)]
        y_ps = ctx.enter_context(nc.psum_tensor("y_ps", [P, C], F32))
        sum_ps = ctx.enter_context(nc.psum_tensor("sum_ps", [P, C], F32))

        first_loaded = [sem(f"first_loaded{c}") for c in range(2)]
        rest_loaded = sem("rest_loaded")
        q_loaded = [sem(f"q_loaded{s}") for s in range(2)]
        k_loaded = [sem(f"k_loaded{s}") for s in range(2)]
        v_loaded = [sem(f"v_loaded{s}") for s in range(2)]
        packed_loaded = [sem(f"packed_loaded{n}") for n in range(2)]
        shift_loaded = sem("shift_loaded")
        wo_loaded = sem("wo_loaded")
        wo_split = sem("wo_split")
        scale_loaded = sem("scale_loaded")
        down_scaled = sem("down_scaled")
        down_hi_done = sem("down_hi_done")
        down_lo_done = sem("down_lo_done")
        down_out = sem("down_out")
        down_seen = sem("down_seen")
        consts = sem("consts_b")
        units_loaded = sem("units_loaded")
        stack_free = sem("stack_free")
        mx_ready = sem("mx_ready")
        mx_free = sem("mx_free")
        row_max_done = sem("row_max_done")
        max16_done = sem("max16_done")
        sc_ready = sem("sc_ready")
        rows_read = sem("rows_read")
        prob_ready = sem("prob_ready")
        step_done = sem("step_done")
        y_copied = sem("y_copied")
        sums_copied = sem("sums_copied")
        recip_done = sem("recip_done")
        y_done = sem("y_done")
        y_out = sem("y_out")
        y_free = sem("y_free")
        shifted = sem("shifted")
        four_set = sem("four_set")
        bits_set = sem("bits_set")
        clipped = sem("clipped")
        differed = sem("differed")
        decoded = sem("decoded")
        block = ctx.enter_context(nc.Block())

        @block.sync
        def _(sp):
            sp.dma_start(shift[:, :], io["shifts"]).then_inc(shift_loaded, 16)

            def load(g, s, progress):
                for n, part in enumerate((0, 1, 0)):
                    sp.wait_ge(step_done, progress + 2 * PACE * n)
                    sp.sem_inc(stack_free, 1)
                    sp.dma_start(k_st[s][n * HD:(n + 1) * HD, :, :],
                                 io["qk_parts"][bass.ds(g + KT, 1), part].rearrange("a (j d) s -> d (a j) s", j=HG))\
                      .then_inc(k_loaded[s], 16)
                    part = (0, 0, 1)[n]
                    sp.wait_ge(step_done, progress + 2 * PACE * n + PACE)
                    sp.sem_inc(stack_free, 1)
                    sp.dma_start(q_st[s][n * HD:(n + 1) * HD, :, :],
                                 io["qk_parts"][bass.ds(g, 1), part].rearrange("a (j d) s -> d (a j) s", j=HG))\
                      .then_inc(q_loaded[s], 16)
                sp.wait_ge(step_done, progress + 6 * PACE)
                sp.sem_inc(stack_free, 1)
                sp.dma_start(v_g[s][:, :, :], io["v_rows"][:, bass.ds(g * P, P)].rearrange("(t p) d -> p t d", p=P))\
                  .then_inc(v_loaded[s], 16)

            for cols, loaded in ((slice(0, C), first_loaded[0]), (slice(C, 2 * C), first_loaded[1]),
                                 (slice(2 * C, S), rest_loaded)):
                for stack, tile, parts in ((k_st[0], KT, (0, 1, 0)), (q_st[0], 0, (0, 0, 1))):
                    for n, part in enumerate(parts):
                        sp.dma_start(stack[n * HD:(n + 1) * HD, :, cols],
                                     io["qk_parts"][tile, part].rearrange("(j d) s -> d j s", j=HG)[:, :, cols])\
                          .then_inc(loaded, 16)
                if loaded is first_loaded[1]:
                    for s in range(2):
                        sp.dma_start(k_st[s][ROWM:ROWM + 1, :, :], io["minus_unit"]).then_inc(units_loaded, 16)
            sp.dma_start(v_g[0][:, :, :], io["v_rows"][:, 0:P].rearrange("(t p) d -> p t d", p=P))\
              .then_inc(v_loaded[0], 16)
            with sp.Fori(0, NG // 2) as u:
                load(2 * u + 1, 1, u * (2 * NSTEP) + NSTEP + PR)
                load((2 * u + 2) & (NG - 1), 0, u * (2 * NSTEP) + 2 * NSTEP + PR)
            sp.wait_ge(v_loaded[0], 16 * (NG // 2 + 1))

        @block.gpsimd
        def _(pool):
            pool.sem_inc(y_free, 2)
            wo_stage = packed[:, :, :].rearrange("p n w -> p (n w)")[:, 0:D].bitcast(F32)
            for k in range(KT):
                if k:
                    pool.wait_ge(wo_split, 2 * k)
                pool.dma_start(wo_stage, io["w_out"][k]).then_inc(wo_loaded, 16)
                pool.wait_ge(wo_loaded, 16 * k + 16)
                nc.gpsimd.tensor_copy(keep["wo_hi"][:, k, :], wo_stage).then_inc(wo_split, 1)
                pool.wait_ge(wo_split, 2 * k + 1)
                nc.gpsimd.tensor_tensor(keep["wo_lo"][:, k, :], wo_stage,
                                        keep["wo_hi"][:, k, :].bitcast(F32), ALU.subtract).then_inc(wo_split, 1)

            pool.wait_ge(wo_split, 2 * KT)

            def assemble(u, n):
                k = u * (2 * PIECES) + n
                pool.wait_ge(clipped, k + 1)
                nc.gpsimd.tensor_tensor(clip[:, :], clip[:, :], four[:, :].bitcast(F32), ALU.subtract)\
                  .then_inc(differed, 1)
                pool.wait_ge(differed, k + 1)
                s, p = PIECE_ORDER[n]
                if n < 2 * DOWN_PIECES:
                    nc.gpsimd.tensor_tensor(down_val[:, :], clip[:, :], bits[:, :].bitcast(F32), ALU.add)\
                      .then_inc(decoded, 1)
                else:
                    pool.sem_inc(down_seen, 1)
                    nc.gpsimd.tensor_tensor(keep["w_gu"][:, bass.ds((2 * u + s) * GU + p * PW, PW)], clip[:, :],
                                            bits[:, :].bitcast(F32), ALU.add).then_inc(decoded, 1)

            def split_down(u, d):
                k = u * (2 * DOWN_PIECES) + d
                s, p = PIECE_ORDER[d]
                g = 2 * u + s
                at = p * PW - GU
                pool.wait_ge(scale_loaded, 16 * k + 16)
                pool.wait_ge(decoded, u * (2 * PIECES) + d + 2)
                nc.gpsimd.tensor_tensor(down_val[:, :], down_val[:, :], down_scale[:, :], ALU.mult)\
                  .then_inc(down_scaled, 1)
                pool.wait_ge(down_scaled, k + 1)
                if d + 1 < 2 * DOWN_PIECES:
                    load_scale(u, d + 1)
                high = keep["w_dn"][:, bass.ds(g * DN + at, PW)]
                nc.gpsimd.tensor_copy(high, down_val[:, :]).then_inc(down_hi_done, 1)
                pool.wait_ge(down_hi_done, k + 1)
                if d:
                    pool.wait_ge(down_out, 16 * k)
                pool.sem_inc(down_seen, 1)
                nc.gpsimd.tensor_tensor(down_lo[:, :], down_val[:, :], high.bitcast(F32),
                                        ALU.subtract).then_inc(down_lo_done, 1)
                pool.wait_ge(down_lo_done, k + 2)
                pool.sem_inc(down_seen, 1)
                pool.dma_start(io["w_dn_lo"][:, bass.ds(g * DN + at, PW)], down_lo[:, :]).then_inc(down_out, 16)
                if d == 2 * DOWN_PIECES - 1:
                    pool.wait_ge(down_out, 16 * k + 16)

            def load_scale(u, d):
                pool.dma_start(down_scale[:, :],
                               io["down_scales"][bass.ds(u * (2 * DN) + d * PW, PW)].partition_broadcast(P))\
                    .then_inc(scale_loaded, 16)

            def load_piece(u, n):
                pool.wait_ge(shifted, u * (2 * PIECES) + n + 1)
                s, p = PIECE_ORDER[n]
                pool.dma_start(packed[:, n % 2, :], io["packed"][bass.ds(2 * u + s, 1), :, p * PW:(p + 1) * PW]
                               .rearrange("a p n -> (a p) n")).then_inc(packed_loaded[n % 2], 16)

            def send(u, s, c):
                n = u * (2 * NC) + s * NC + c
                if (s, c) != (0, 0):
                    sent(n)
                pool.wait_ge(y_done, n + 2)
                pool.dma_start(io["y_cols"][bass.ds((2 * u + s) * P, P), c * C:(c + 1) * C], y[:, c % 2, :])\
                    .then_inc(y_out, 16)

            def sent(n):
                pool.wait_ge(y_out, 16 * n)
                pool.sem_inc(y_free, 1)

            pool.sem_inc(down_lo_done, 1)
            with pool.Fori(0, NG // 2) as u:
                load_scale(u, 0)
                load_piece(u, 0)
                load_piece(u, 1)
                for at in range(len(ROUND) + DELAY):
                    for s, c in START:
                        if at == START[s, c] + STEPS[c] + DELAY - 1:
                            send(u, s, c)
                    if at < len(ROUND):
                        for n in PIECES_AT[at]:
                            if n + 2 < 2 * PIECES:
                                load_piece(u, n + 2)
                            assemble(u, n)
                            if n < 2 * DOWN_PIECES:
                                split_down(u, n)
                sent(u * (2 * NC) + 2 * NC)

        @block.scalar
        def _(act):
            act.sem_inc(prob_ready, 1)
            act.sem_inc(y_copied, 1)
            act.sem_inc(sums_copied, 1)

            def round_(u):
                entry = [0]

                def rows(s, c):
                    act.wait_ge(sc_ready, u * NENTRY + entry[0] + 2)
                    for j in range(HG):
                        nc.scalar.copy(q_st[s % 2][ROWM:ROWM + 1, j, c * C:(c + 1) * C],
                                       sc_ps[entry[0] % BR][j * HD:j * HD + 1, :]).then_inc(rows_read, 1)
                    entry[0] += 1

                def copy_out(s, c):
                    n = u * (2 * NC) + s * NC + c
                    end = START[s, c] + STEPS[c]
                    act.wait_ge(step_done, u * (2 * NSTEP) + end + NSTEP + PR)
                    act.wait_ge(y_free, n + 1)
                    nc.scalar.copy(y[:, c % 2, :], y_ps[:, :]).then_inc(y_copied, 1)
                    act.wait_ge(recip_done, KT * n + 1)
                    nc.scalar.copy(sums_sb[:, :], sum_ps[:, :]).then_inc(sums_copied, 1)

                for at, (s, c, k) in enumerate(ROUND):
                    for j in range(HG):
                        act.wait_ge(sc_ready, u * NENTRY + entry[0] + 2)
                        if j == 0:
                            act.wait_ge(step_done, u * (2 * NSTEP) + at + NSTEP + 1)
                        nc.scalar.activation(prob[:, at % PR, j, lo(c, k):C], sc_ps[entry[0] % BR][:, lo(c, k):C],
                                             ACT.Exp).then_inc(prob_ready, 1)
                        entry[0] += 1
                    if k == 0 and at:
                        copy_out(*ROUND[at - 1][:2])
                    for row in ROWS_AT[at]:
                        rows(*row)
                copy_out(1, NC - 1)

            act.wait_ge(sc_ready, 1)
            for j in range(HG):
                nc.scalar.copy(q_st[0][ROWM:ROWM + 1, j, 0:C], sc_ps[0][j * HD:j * HD + 1, :]).then_inc(rows_read, 1)
            with act.Fori(0, NG // 2) as u:
                round_(u)

        @block.vector
        def _(dve):
            nc.vector.memset(ones[:, :], 1.0).then_inc(consts, 1)
            dve.sem_inc(mx_free, MX0 + XR)
            dve.sem_inc(shifted, 2)
            for started in (y_done, recip_done, decoded):
                dve.sem_inc(started, 1)
            dve.wait_ge(shift_loaded, 16)

            def decode(u, n, half):
                k = u * (2 * PIECES) + n
                if half == 0:
                    dve.wait_ge(packed_loaded[n % 2], u * (16 * PIECES) + 16 * (n // 2) + 16)
                    dve.wait_ge(decoded, k + 1)
                    nc.vector.tensor_scalar(bits[:, :], packed[:, n % 2, :], shift[:, :], 6,
                                            ALU.logical_shift_left, ALU.arith_shift_right).then_inc(shifted, 1)
                    dve.wait_ge(shifted, k + 3)
                    nc.vector.tensor_scalar(four[:, :], bits[:, :], -2 ** 31, 0x40800000,
                                            ALU.bitwise_and, ALU.bitwise_or).then_inc(four_set, 1)
                    return
                if half == 1:
                    dve.wait_ge(four_set, k + 1)
                    nc.vector.tensor_scalar(bits[:, :], bits[:, :], 0x81C00000 - 2 ** 32, 0x40000000,
                                            ALU.bitwise_and, ALU.bitwise_or).then_inc(bits_set, 1)
                    dve.wait_ge(bits_set, k + 1)
                    nc.vector.tensor_scalar(clip[:, :], bits[:, :].bitcast(F32), 4.0, -4.0, ALU.min, ALU.max)\
                      .then_inc(clipped, 1)

            def maxima(todo, units_before, chunks_before):
                chunks = 0
                for n, (s, c, t, j, b) in enumerate(todo):
                    dve.wait_ge(mx_ready, units_before + n + 1)
                    nc.vector.reduce_max(max_part[:, t * HG + j, b:b + 1],
                                         mx_ps[mx_bank[0] % XR][:, 0:bank_width(c, t, b)], X).then_inc(mx_free, 1)
                    mx_bank[0] += 1
                    if (t, j, b) == (TC - 1, HG - 1, c):
                        dve.wait_ge(mx_free, units_before + n + 1 + MX0 + XR)
                        nc.vector.reduce_max(row_max[:, :], max_part[:, :, 0:c + 1], X).then_inc(row_max_done, 1)
                        chunks += 1
                        dve.wait_ge(row_max_done, chunks_before + chunks)
                        nc.vector.tensor_scalar(max16[:, :], row_max[:, :], 1.0 / M_UNIT, None, ALU.mult)\
                          .then_inc(max16_done, 1)

            def round_(u):
                unit = 0
                mx_bank[0] = 0

                def normalize(s, c, quarter):
                    n = u * (2 * NC) + s * NC + c
                    if quarter == 0:
                        dve.wait_ge(sums_copied, n + 2)
                        dve.wait_ge(y_done, n + 1)
                    cols = slice(quarter * P, (quarter + 1) * P)
                    nc.vector.reciprocal(recip[:, cols], sums_sb[:, cols]).then_inc(recip_done, 1)
                    if quarter == KT - 1:
                        dve.wait_ge(recip_done, KT * n + KT + 1)
                        dve.wait_ge(y_copied, n + 2)
                        nc.vector.tensor_tensor(y[:, c % 2, :], y[:, c % 2, :], recip[:, :], ALU.mult)\
                          .then_inc(y_done, 1)

                for at in range(len(ROUND) + DELAY):
                    todo = PLAN[at] if at < len(ROUND) else []
                    for part in range(KT):
                        a, b = len(todo) * part // KT, len(todo) * (part + 1) // KT
                        maxima(todo[a:b], u * NMX + AHEAD + unit + a, u * (2 * NC) + 1 + sum(map(len, ROWS_AT[:at + 1])))
                        for s, c in START:
                            if at == START[s, c] + STEPS[c] + DELAY - 1:
                                normalize(s, c, part)
                        for n in PIECES_AT[at] if at < len(ROUND) and part % 2 == 0 else []:
                            decode(u, n, part // 2)
                    unit += len(todo)

            mx_bank = [0]
            maxima(BEFORE, 0, 0)
            with dve.Fori(0, NG // 2) as u:
                round_(u)

        @block.tensor
        def _(pe):
            pe.sem_inc(step_done, NSTEP + PR)

            def unit_scores(x, bank, free):
                s, c, t, j, b = x
                w = bank_width(c, t, b)
                q0 = c * C + t * P
                pe.wait_ge(mx_free, free)
                last = nc.tensor.matmul(mx_ps[bank][:, 0:w], q_st[s % 2][0:ROWM, j, q0:q0 + P],
                                        k_st[s % 2][0:ROWM, j, b * C:b * C + w], start=True, stop=(b < c))
                if b == c:
                    last = nc.tensor.matmul(mx_ps[bank][:, w - P:w], keep["identb"][:, :],
                                            keep["mask_qk"][:, :], start=False, stop=True)
                last.then_inc(mx_ready, 1)

            def row_scores(bank):
                for j in range(HG):
                    for t in range(TC):
                        last = nc.tensor.matmul(sc_ps[bank][j * HD:j * HD + 1, t * P:(t + 1) * P],
                                                max16[:, t * HG + j:t * HG + j + 1], keep["ident16"][:, :],
                                                start=True, stop=True, tile_position=(0, j * HD))
                last.then_inc(sc_ready, 1)

            def round_(u):
                unit = [0]
                readers = []
                exps, copies = [0], [0]

                def wait_free():
                    if len(readers) < BR:
                        pe.wait_ge(prob_ready, u * (HG * 2 * NSTEP) + 1)
                    else:
                        signal, by_round, count = readers[-BR]
                        pe.wait_ge(signal, u * by_round + count)

                def maxima(todo):
                    for x in todo:
                        n = unit[0]
                        s = x[0]
                        if s and TODO[n - 1][0] != s:
                            pe.wait_ge(q_loaded[s % 2], u * 48 + 48)
                            pe.wait_ge(k_loaded[s % 2], u * 48 + 48)
                        if x == TODO[0]:
                            pe.wait_ge(rest_loaded, 96)
                        unit_scores(x, n % XR, u * NMX + AHEAD + MX0 + max(n + 1, XR))
                        unit[0] += 1

                def rows(s, c):
                    pe.wait_ge(max16_done, u * (2 * NC) + ROW_ORDER.index((s, c)) + 1)
                    n = len(readers)
                    wait_free()
                    copies[0] += 1
                    readers.append((rows_read, HG * 2 * NC, HG + HG * copies[0]))
                    row_scores(n % BR)

                def scores(s, c, k, heads):
                    a = lo(c, k)
                    for j in heads:
                        n = len(readers)
                        wait_free()
                        if k == 0 and j == 0:
                            pe.wait_ge(rows_read, u * (HG * 2 * NC) + HG * (ROW_ORDER.index((s, c)) + 1))
                        exps[0] += 1
                        readers.append((prob_ready, HG * 2 * NSTEP, exps[0] + 1))
                        last = nc.tensor.matmul(sc_ps[n % BR][:, a:C], k_st[s][0:ROWM + 1, j, k * P:(k + 1) * P],
                                                q_st[s][0:ROWM + 1, j, c * C + a:(c + 1) * C],
                                                start=True, stop=(k < TC * c))
                        if k >= TC * c:
                            last = nc.tensor.matmul(sc_ps[n % BR][:, a:a + P], keep["identb"][:, :],
                                                    keep["mask_kq"][:, :], start=False, stop=True)
                        last.then_inc(sc_ready, 1)

                def products(at):
                    s, c, k = ROUND[at]
                    a = lo(c, k)
                    pe.wait_ge(prob_ready, u * (HG * 2 * NSTEP) + HG * at + HG + 1)
                    if k == c == 0:
                        pe.wait_ge(v_loaded[s], u * 16 + 16)
                    if k == 0:
                        pe.wait_ge(y_copied, u * (2 * NC) + s * NC + c + 1)
                    for j in range(HG):
                        nc.tensor.matmul(y_ps[j * HD:(j + 1) * HD, a:C], v_g[s][:, k, j * HD:(j + 1) * HD],
                                         prob[:, at % PR, j, a:C], start=(k == 0), stop=(k == STEPS[c] - 1),
                                         tile_position=(0, j * HD))

                def sums(at):
                    s, c, k = ROUND[at]
                    a = lo(c, k)
                    if k == 0:
                        pe.wait_ge(sums_copied, u * (2 * NC) + s * NC + c + 1)
                    for j in range(HG):
                        last = nc.tensor.matmul(sum_ps[j * HD:(j + 1) * HD, a:C], ones[:, :],
                                                prob[:, at % PR, j, a:C], start=(k == 0), stop=(k == STEPS[c] - 1),
                                                tile_position=(0, j * HD))
                    last.then_inc(step_done, 1)

                for at, (s, c, k) in enumerate(ROUND):
                    todo = PLAN[at]
                    cut = [len(todo) * n // 4 for n in range(5)]
                    scores(s, c, k, (0, 1))
                    maxima(todo[cut[0]:cut[1]])
                    if at:
                        products(at - 1)
                    maxima(todo[cut[1]:cut[2]])
                    scores(s, c, k, (2, 3))
                    maxima(todo[cut[2]:cut[3]])
                    for row in ROWS_AT[at]:
                        rows(*row)
                    if at:
                        sums(at - 1)
                    maxima(todo[cut[3]:cut[4]])
                products(len(ROUND) - 1)
                sums(len(ROUND) - 1)

            for n, x in enumerate(BEFORE):
                if x[2:] == (0, 0, 0):
                    pe.wait_ge(first_loaded[x[1]], 96)
                unit_scores(x, n % XR, MX0 + n + 1)
            pe.wait_ge(max16_done, 1)
            row_scores(0)
            pe.wait_ge(consts, 1)
            pe.wait_ge(units_loaded, 32)
            with pe.Fori(0, NG // 2) as u:
                round_(u)


def phase_c(nc, io, keep):
    LAG = 2
    HB = LAG + 1
    DB = 2
    NA, ND = IT * 2, IT * 2 * (KT - 1)
    TILE = [("gu", 0, 1), ("dn", 0), ("gu", 1, 1), ("slot", 0), ("gu", 0, 2), ("gu", 0, 0), ("dn", 1), ("gu", 1, 2),
            ("slot", 1), ("gu", 0, 3), ("gu", 1, 0), ("dn", 2), ("gu", 1, 3), ("dn", 3)]
    TAIL_AT = {(1, 0): 0, (1, 1): 1, (2, 0): 2, (2, 1): 3}
    PROD_AT = {(5, 0): 0, (5, 1): 1, (6, 0): 2, (6, 1): 3}
    NORM_AT = 7
    TP_AT = {(8, 1): 0, (9, 0): 1, (9, 1): 2, (10, 0): 3}

    def d_place(o, s, k):
        return (o * (KT - 1) + k - 1) * 2 + s

    with ExitStack() as ctx:
        def sb(name, shape, dt=F32):
            return ctx.enter_context(nc.sbuf_tensor(name, shape, dt))

        def sem(name):
            return ctx.enter_context(nc.semaphore(name))

        w_gu = keep["w_gu"][:, :].rearrange("p (k n) -> p k n", k=KT)
        w_dn = keep["w_dn"][:, :].rearrange("p (t o) -> p t o", t=IT)
        wo_hi, wo_lo, ident = keep["wo_hi"], keep["wo_lo"], keep["ident"]
        w_dn_lo = sb("w_dn_lo_sb", [P, IT, D], F32R)
        sc16 = sb("sc16", [P, GU // P * KT], F16)
        sc = sb("sc", [P, GU // P * KT])
        sc_gu = sc[:, :].rearrange("p (o k) -> p o k", k=KT)
        gate_rows = sb("gate_rows", [P, 2, D])
        gab = sb("gab", [P, D])
        eps = sb("eps_c", [P, 2])
        xy = sb("xy", [P, KT, C])
        y_hi = sb("y_hi", [P, 2, KT, P], F32R)
        y_lo = sb("y_lo", [P, 2, KT, P], F32R)
        prod = sb("prod", [P, 2, D])
        x1 = sb("x1", [P, 2 * TC, D])
        stats = sb("stats_c", [P, TC, 6])
        mv = sb("mv_c", [P, TC, 2])
        rstd = sb("rstd_c", [P, 2, TC])
        ht = sb("ht_c", [P, KT, C])
        gate_col = ht[:, 0:2, :].rearrange("p g (f m) -> p g f m", f=KT)
        h_hi = sb("h_hi_c", [P, KT, C], F32R)
        h_lo = sb("h_lo_c", [P, KT, C], F32R)
        gu = sb("gu", [P, 2, 2, C])
        h1 = sb("h1", [P, 2, C])
        h1_hi = sb("h1_hi", [P, HB, C], F32R)
        h1_lo = sb("h1_lo", [P, HB, C], F32R)
        acc = sb("acc", [P, KT, C])
        sq = sb("sq", [P, TC])
        rms = sb("rms", [P, 2, TC])
        a_ps = ctx.enter_context(nc.psum_tensor("a_ps", [P, C], F32))
        d_ps = [ctx.enter_context(nc.psum_tensor(f"d_ps{n}", [P, C], F32)) for n in range(DB)]
        f_ps = ctx.enter_context(nc.psum_tensor("f_ps", [P, C], F32))
        acc_ps = [ctx.enter_context(nc.psum_tensor(f"acc_ps{r}", [P, C], F32)) for r in range(KT)]

        scales_loaded = sem("scales_loaded")
        b_loaded = sem("b_loaded")
        lo_loaded = sem("lo_loaded")
        consts = sem("consts_c")
        scaled = sem("scaled")
        col_set = sem("col_set")
        col_used = sem("col_used")
        gates_out = sem("gates_out")
        gab_done = sem("gab_done")
        y_loaded = sem("y_loaded")
        xy_free = sem("xy_free")
        x_free = sem("x_free")
        x_loaded = sem("x_loaded_c")
        y_hi_done = sem("y_hi_done")
        y_lo_done = sem("y_lo_done")
        prod_ready = sem("prod_ready")
        prod_read = sem("prod_read")
        bias_added = sem("bias_added")
        x1_done = sem("x1_done")
        stats_done = sem("stats_done_c")
        rows_seen = sem("rows_seen")
        mv_done = sem("mv_done_c")
        sd_done = sem("sd_done_c")
        rstd_done = sem("rstd_done_c")
        xn_done = sem("xn_done_c")
        tp_done = sem("tp_done_c")
        ht_done = sem("ht_done_c")
        h_hi_done = sem("h_hi_done_c")
        h_lo_done = sem("h_lo_done_c")
        a_ready = sem("a_ready")
        a_read = sem("a_read")
        d_ready = sem("d_ready")
        d_read = sem("d_read")
        silu_done = sem("silu_done_c")
        h1_done = sem("h1_done")
        h1_hi_done = sem("h1_hi_done")
        h1_lo_done = sem("h1_lo_done")
        acc_ready = sem("acc_ready")
        acc_by_act = sem("acc_by_act")
        acc_by_dve = sem("acc_by_dve")
        tail_ready = sem("tail_ready")
        rows_squared = sem("rows_squared")
        rows_copied = sem("rows_copied")
        rms_done = sem("rms_done")
        rms_inv = sem("rms_inv")
        normed = sem("normed")
        out_ready = sem("out_ready")
        out_sent = sem("out_sent")
        block = ctx.enter_context(nc.Block())

        FIRST_BANKS = (f_ps, acc_ps[2], acc_ps[3], acc_ps[1])
        LAST_BANKS = (f_ps, a_ps, *d_ps)

        def front_bank(i, t):
            return FIRST_BANKS[t] if isinstance(i, int) and i == 0 else f_ps

        def x1_rows(i, t, n=1):
            return x1[:, bass.ds((i & 1) * TC + t, n), :]

        def row_tile(i, t):
            return x1_rows(i, t).rearrange("p a d -> p (a d)")

        @block.sync
        def _(sp):
            def load_y(i):
                sp.dma_start(xy[:, :, :], io["y_cols"][:, bass.ds(i * C, C)]
                             .rearrange("(f p) s -> p f s", p=P)).then_inc(y_loaded, 16)

            def load_x(i):
                sp.dma_start(x1_rows(i, 0, TC), io["x"][bass.ds(i * C, C), :]
                             .rearrange("(t p) d -> p t d", p=P)).then_inc(x_loaded, 16)

            def tail(i):
                for t in range(TC):
                    sp.wait_ge(out_ready, i * TC + t + 1)
                    sp.dma_start(io["out"][bass.ds(i * C + t * P, P), :], ht[:, t, :]).then_inc(out_sent, 16)

            def chunk(i, first, last):
                if not last:
                    sp.wait_ge(tp_done, i * KT + KT)
                    sp.wait_ge(y_loaded, i * 16 + 16)
                    sp.sem_inc(xy_free, 1)
                    load_y(i + 1)
                if not first:
                    tail(i - 1)
                if not last:
                    sp.wait_ge(x_loaded, i * 16 + 16)
                    sp.sem_inc(x_free, 1)
                    load_x(i + 1)

            sp.dma_start(gab[:, :], io["b_out"].partition_broadcast(P)).then_inc(b_loaded, 16)
            load_y(0)
            load_x(0)
            sp.dma_start(sc16[:, :], io["scales"]).then_inc(scales_loaded, 16)
            chunk(0, True, False)
            with sp.Fori(1, NC - 1) as i:
                chunk(i, False, False)
            chunk(NC - 1, False, True)
            tail(NC - 1)
            sp.wait_ge(out_sent, 16 * NC * TC)

        @block.gpsimd
        def _(pool):
            for started in (h1_done, h1_lo_done):
                pool.sem_inc(started, 1)
            nc.gpsimd.memset(eps[:, 0:1], EPS).then_inc(consts, 1)
            nc.gpsimd.memset(eps[:, 1:2], RMS_EPS).then_inc(consts, 1)

            def add_bias(i):
                pool.wait_ge(gab_done, 1)
                pool.wait_ge(x_loaded, i * 16 + 16)
                for t in range(TC):
                    nc.gpsimd.tensor_tensor(row_tile(i, t), row_tile(i, t), gab[:, :], ALU.add)\
                      .then_inc(bias_added, 1)

            def hidden(i, o):
                pool.wait_ge(silu_done, i * IT + o + 1)
                pool.wait_ge(d_read, i * ND + DB + d_place(o, 1, KT - 1) + 1)
                nc.gpsimd.tensor_tensor(h1[:, o % 2, :], h1[:, o % 2, :], gu[:, o % 2, 1, :], ALU.mult)\
                  .then_inc(h1_done, 1)

            def low(i, o):
                pool.wait_ge(h1_hi_done, i * IT + o + 1)
                nc.gpsimd.tensor_tensor(h1_lo[:, o % HB, :], h1[:, o % 2, :], h1_hi[:, o % HB, :].bitcast(F32),
                                        ALU.subtract).then_inc(h1_lo_done, 1)

            def finish(i):
                for t in range(TC):
                    pool.wait_ge(normed, i * TC + t + 1)
                    nc.gpsimd.tensor_tensor(ht[:, t, :], ht[:, t, :], row_tile(i, t), ALU.add).then_inc(out_ready, 1)

            def chunk(i, first, last):
                for o in range(IT + 1):
                    if o >= 1:
                        hidden(i, o - 1)
                        low(i, o - 1)
                    if not first and o == 3:
                        finish(i - 1)
                    if not last and o == 4:
                        add_bias(i + 1)

            pool.wait_ge(y_loaded, 16)
            pool.wait_ge(x_loaded, 16)
            pool.dma_start(w_dn_lo[:, :, :], io["w_dn_lo"].rearrange("p (t o) -> p t o", t=IT)).then_inc(lo_loaded, 16)
            add_bias(0)
            chunk(0, True, False)
            with pool.Fori(1, NC - 1) as i:
                chunk(i, False, False)
            chunk(NC - 1, False, True)
            finish(NC - 1)

        @block.scalar
        def _(act):
            act.sem_inc(a_read, 1)

            def deviation(i):
                act.wait_ge(mv_done, i * TC + TC)
                nc.scalar.activation(rstd[:, 0, :], mv[:, :, 1], ACT.Sqrt, bias=eps[:, 0:1]).then_inc(sd_done, 1)

            def modulate(i, f):
                act.wait_ge(tp_done, i * KT + f + 1)
                nc.scalar.activation(ht[:, f, :], front_bank(i, f)[:, :], ACT.Identity,
                                     bias=keep["ffn_mod"][:, 0, f:f + 1],
                                     scale=keep["ffn_mod"][:, 1, f:f + 1]).then_inc(ht_done, 1)

            def first_sum(i, o, s):
                act.wait_ge(h1_done, i * IT + max(0, o - 1) + 1)
                act.wait_ge(a_ready, i * NA + 2 * o + s + 1)
                nc.scalar.activation(gu[:, o % 2, s, :], a_ps[:, :], ACT.Copy,
                                     scale=sc_gu[:, s * IT + o, 0:1]).then_inc(a_read, 1)

            def silu(i, o):
                act.wait_ge(d_read, i * ND + DB + d_place(o, 0, KT - 1) + 1)
                act.wait_ge(h1_lo_done, i * IT + max(0, o - 1) + 1)
                nc.scalar.activation(h1[:, o % 2, :], gu[:, o % 2, 0, :], ACT.Silu).then_inc(silu_done, 1)

            def high(i, o):
                act.wait_ge(h1_done, i * IT + o + 2)
                nc.scalar.activation(h1_hi[:, o % HB, :], h1[:, o % 2, :], ACT.Copy).then_inc(h1_hi_done, 1)

            def acc_out(i):
                for n, r in enumerate((1, 3)):
                    act.wait_ge(acc_ready, i * KT + r + 1)
                    nc.scalar.copy(acc[:, r, :], acc_ps[r][:, :]).then_inc(acc_by_act, 1)

            def tail_rows(i, t):
                act.wait_ge(tail_ready, i * TC + t + 1)
                nc.scalar.activation(ht[:, t, :], f_ps[:, :], ACT.Square,
                                     accum_out=sq[:, t:t + 1]).then_inc(rows_squared, 1)
                act.wait_ge(rows_squared, i * TC + t + 1)
                nc.scalar.copy(ht[:, t, :], f_ps[:, :]).then_inc(rows_copied, 1)

            def root(i):
                act.wait_ge(rows_squared, i * TC + TC)
                nc.scalar.activation(rms[:, 0, :], sq[:, :], ACT.Sqrt, bias=eps[:, 1:2], scale=1.0 / (16 * D))\
                  .then_inc(rms_done, 1)

            def chunk(i, first, last):
                if not first:
                    acc_out(i - 1)
                for s in range(2):
                    first_sum(i, 0, s)
                for o in range(IT + 1):
                    if o >= 1:
                        silu(i, o - 1)
                    if (o, 0) in TAIL_AT and not first:
                        act.wait_ge(h_lo_done, i * KT + KT)
                        tail_rows(i - 1, TAIL_AT[o, 0])
                    if (o, 0) in TP_AT and not last:
                        modulate(i + 1, TP_AT[o, 0])
                    if o + 1 < IT:
                        first_sum(i, o + 1, 0)
                    if o >= 1:
                        high(i, o - 1)
                    if (o, 1) in TAIL_AT and not first:
                        tail_rows(i - 1, TAIL_AT[o, 1])
                        if TAIL_AT[o, 1] == TC - 1:
                            root(i - 1)
                    if (o, 1) in TP_AT and not last:
                        if TP_AT[o, 1] == 0 and not first:
                            act.wait_ge(out_sent, i * (16 * TC))
                        modulate(i + 1, TP_AT[o, 1])
                    if o + 1 < IT:
                        first_sum(i, o + 1, 1)
                    if o == NORM_AT and not last:
                        deviation(i + 1)

            act.wait_ge(consts, 2)
            act.wait_ge(scaled, 1)
            deviation(0)
            for f in range(KT):
                modulate(0, f)
            chunk(0, True, False)
            with act.Fori(1, NC - 1) as i:
                chunk(i, False, False)
            chunk(NC - 1, False, True)
            act.wait_ge(out_sent, 16 * TC * (NC - 1))
            acc_out(NC - 1)
            for t in range(TC):
                act.wait_ge(tail_ready, (NC - 1) * TC + t + 1)
                nc.scalar.activation(ht[:, t, :], LAST_BANKS[t][:, :], ACT.Square,
                                     accum_out=sq[:, t:t + 1]).then_inc(rows_squared, 1)
            root(NC - 1)

        @block.vector
        def _(dve):
            dve.sem_inc(d_read, DB)
            dve.sem_inc(x1_done, 1)

            def split_y(i, t):
                if t == 0:
                    dve.wait_ge(y_loaded, i * 16 + 16)
                dve.wait_ge(prod_ready, i * TC + max(0, t - 1) + 1)
                cols = slice(t * P, (t + 1) * P)
                nc.vector.tensor_copy(y_hi[:, t % 2, :, :], xy[:, :, cols]).then_inc(y_hi_done, 1)
                dve.wait_ge(y_hi_done, i * TC + t + 1)
                nc.vector.tensor_tensor(y_lo[:, t % 2, :, :], xy[:, :, cols], y_hi[:, t % 2, :, :].bitcast(F32),
                                        ALU.subtract).then_inc(y_lo_done, 1)

            def gate_product(i, t):
                dve.wait_ge(prod_ready, i * TC + t + 2)
                dve.wait_ge(x1_done, i * TC + max(0, t - 1) + 1)
                nc.vector.tensor_tensor(prod[:, t % 2, :], front_bank(i, t)[:, :], gate_rows[:, 0, :], ALU.mult)\
                  .then_inc(prod_read, 1)

            def residual(i, t):
                dve.wait_ge(prod_read, i * TC + t + 1)
                dve.wait_ge(bias_added, i * TC + t + 1)
                nc.vector.tensor_tensor(row_tile(i, t), row_tile(i, t), prod[:, t % 2, :], ALU.add)\
                  .then_inc(x1_done, 1)

            def statistics(i, t):
                dve.wait_ge(x1_done, i * TC + t + 2)
                dve.sem_inc(rows_seen, 1)
                nc.vector.bn_stats(stats[:, t, :], row_tile(i, t)).then_inc(stats_done, 1)
                dve.wait_ge(stats_done, i * TC + t + 1)
                dve.sem_inc(rows_seen, 1)
                nc.vector.bn_aggr(mv[:, t, :], stats[:, t, :]).then_inc(mv_done, 1)

            def normalize(i):
                dve.wait_ge(sd_done, i + 1)
                nc.vector.reciprocal(rstd[:, 1, :], rstd[:, 0, :]).then_inc(rstd_done, 1)
                dve.wait_ge(rstd_done, i + 1)
                dve.wait_ge(y_lo_done, i * TC + TC)
                for t in range(TC):
                    nc.vector.tensor_scalar(xy[:, t, :], row_tile(i, t), mv[:, t, 0:1], rstd[:, 1, t:t + 1],
                                            ALU.subtract, ALU.mult).then_inc(xn_done, 1)

            def split_h(i):
                for f in range(KT):
                    dve.wait_ge(ht_done, i * KT + f + 1)
                    nc.vector.tensor_copy(h_hi[:, f, :], ht[:, f, :]).then_inc(h_hi_done, 1)
                    dve.wait_ge(h_hi_done, i * KT + f + 1)
                    nc.vector.tensor_tensor(h_lo[:, f, :], ht[:, f, :], h_hi[:, f, :].bitcast(F32),
                                            ALU.subtract).then_inc(h_lo_done, 1)

            def add_group(i, o, s, k):
                n = d_place(o, s, k)
                dve.wait_ge(d_ready, i * ND + n + 1)
                if k == 1:
                    dve.wait_ge(a_read, i * NA + 2 * o + s + 2)
                else:
                    dve.wait_ge(d_read, i * ND + DB + d_place(o, s, k - 1) + 1)
                nc.vector.scalar_tensor_tensor(out=gu[:, o % 2, s, :], in0=d_ps[n % DB][:, :],
                                               scalar=sc_gu[:, s * IT + o, k:k + 1], in1=gu[:, o % 2, s, :],
                                               op0=ALU.mult, op1=ALU.add).then_inc(d_read, 1)

            def acc_out(i):
                for r in (0, 2):
                    dve.wait_ge(acc_ready, i * KT + r + 1)
                    nc.vector.tensor_copy(acc[:, r, :], acc_ps[r][:, :]).then_inc(acc_by_dve, 1)

            def tail_norm(i, tiles=range(TC), last_chunk=False):
                if 0 in tiles:
                    dve.wait_ge(rms_done, i + 1)
                    nc.vector.reciprocal(rms[:, 1, :], rms[:, 0, :]).then_inc(rms_inv, 1)
                    dve.wait_ge(rms_inv, i + 1)
                for t in tiles:
                    if last_chunk:
                        rows = LAST_BANKS[t][:, :]
                    else:
                        dve.wait_ge(rows_copied, i * TC + t + 1)
                        rows = ht[:, t, :]
                    nc.vector.scalar_tensor_tensor(out=ht[:, t, :], in0=rows, scalar=rms[:, 1, t:t + 1],
                                                   in1=gate_rows[:, 1, :], op0=ALU.mult, op1=ALU.mult)\
                      .then_inc(normed, 1)

            def chunk(i, first, last):
                if not first:
                    acc_out(i - 1)
                for o in range(IT):
                    for k in range(1, KT):
                        for s in range(2):
                            add_group(i, o, s, k)
                        if not first and (o, k) == (3, 1):
                            tail_norm(i - 1, (2, 3))
                        if not last:
                            place = o * (KT - 1) + k - 1
                            for (tile, slot), t in PROD_AT.items():
                                after = place - (tile * (KT - 1) + slot)
                                if after == 0:
                                    gate_product(i + 1, t)
                                if after == 1:
                                    residual(i + 1, t)
                                    statistics(i + 1, t)
                                if after == 2 and t + 2 < TC:
                                    split_y(i + 1, t + 2)
                            if o == 3 and k < KT - 1:
                                split_y(i + 1, k - 1)
                    if not first and o == 2:
                        tail_norm(i - 1, (0, 1))
                    if not last and o == NORM_AT:
                        normalize(i + 1)
                if not last:
                    split_h(i + 1)

            for g in range(2):
                nc.vector.tensor_copy(gate_col[:, g, :, :], keep["gates"][:, g, :].rearrange("p (f a) -> p f a", a=1)
                                      .to_broadcast([P, KT, P])).then_inc(col_set, 1)
            dve.wait_ge(col_used, 2)
            nc.vector.tensor_copy(gate_rows[:, 0, :], acc_ps[0][:, :]).then_inc(gates_out, 1)
            nc.vector.tensor_scalar(gate_rows[:, 1, :], acc_ps[1][:, :], 0.25, None, ALU.mult).then_inc(gates_out, 1)
            dve.wait_ge(gates_out, 2)
            dve.wait_ge(b_loaded, 16)
            nc.vector.tensor_tensor(gab[:, :], gab[:, :], gate_rows[:, 0, :], ALU.mult).then_inc(gab_done, 1)
            split_y(0, 0)
            split_y(0, 1)
            dve.wait_ge(scales_loaded, 16)
            nc.vector.tensor_scalar(sc[:, :], sc16[:, :], 0.25, None, ALU.mult).then_inc(scaled, 1)
            for t in range(TC):
                gate_product(0, t)
                if t + 2 < TC:
                    split_y(0, t + 2)
                residual(0, t)
                statistics(0, t)
            normalize(0)
            split_h(0)
            chunk(0, True, False)
            with dve.Fori(1, NC - 1) as i:
                chunk(i, False, False)
            chunk(NC - 1, False, True)
            acc_out(NC - 1)
            tail_norm(NC - 1, last_chunk=True)

        @block.tensor
        def _(pe):
            pe.sem_inc(prod_ready, 1)
            for g in range(2):
                pe.wait_ge(col_set, g + 1)
                for f in range(KT):
                    last = nc.tensor.matmul(acc_ps[g][:, f * P:(f + 1) * P], gate_col[:, g, f, :], ident[:, :],
                                            start=True, stop=True)
                last.then_inc(col_used, 1)

            def products(i, t):
                if front_bank(i, t) is not f_ps:
                    pe.wait_ge(gates_out, 2)
                elif t:
                    pe.wait_ge(prod_read, i * TC + t)
                pe.wait_ge(y_lo_done, i * TC + t + 1)
                for f in range(KT):
                    for m, (a, b) in enumerate(((y_hi, wo_hi), (y_hi, wo_lo), (y_lo, wo_hi))):
                        last = nc.tensor.matmul(front_bank(i, t)[:, :], a[:, t % 2, f, :], b[:, f, :],
                                                start=(f == 0 and m == 0), stop=(f == KT - 1 and m == 2))
                last.then_inc(prod_ready, 1)

            def transposes(i, f):
                if f == 0:
                    pe.wait_ge(prod_read, i * TC + TC)
                    pe.wait_ge(xn_done, i * TC + TC)
                elif front_bank(i, f) is f_ps:
                    pe.wait_ge(ht_done, i * KT + f)
                for t in range(TC):
                    last = nc.tensor.transpose(front_bank(i, f)[:, t * P:(t + 1) * P], xy[:, t, f * P:(f + 1) * P], ident[:, :])
                last.then_inc(tp_done, 1)

            def tail(i, t, bank_free, last_chunk=False):
                if t == 0:
                    pe.wait_ge(ht_done, bank_free)
                    pe.wait_ge(acc_by_act, i * 2 + 2)
                    pe.wait_ge(acc_by_dve, i * 2 + 2)
                elif last_chunk:
                    pass
                else:
                    pe.wait_ge(rows_copied, i * TC + t)
                bank = LAST_BANKS[t] if last_chunk else f_ps
                for r in range(KT):
                    last = nc.tensor.transpose(bank[:, r * P:(r + 1) * P], acc[:, r, t * P:(t + 1) * P], ident[:, :])
                last.then_inc(tail_ready, 1)

            def group_sum(i, o, s, k):
                cols = slice((s * IT + o) * P, (s * IT + o + 1) * P)
                if o == s == 0:
                    pe.wait_ge(h_lo_done, i * KT + k + 1)
                if k:
                    n = d_place(o, s, k)
                    pe.wait_ge(d_read, i * ND + n + 1)
                    out, ready = d_ps[n % DB], d_ready
                else:
                    pe.wait_ge(a_read, i * NA + 2 * o + s + 1)
                    out, ready = a_ps, a_ready
                nc.tensor.matmul(out[:, :], w_gu[:, k, cols], h_hi[:, k, :], start=True, stop=False)
                nc.tensor.matmul(out[:, :], w_gu[:, k, cols], h_lo[:, k, :], start=False, stop=True)\
                  .then_inc(ready, 1)

            def down(i, t, r, first):
                if r == 0:
                    pe.wait_ge(h1_lo_done, i * IT + t + 2)
                if t == 0 and not first:
                    pe.wait_ge(acc_by_act if r % 2 else acc_by_dve, (i - 1) * 2 + r // 2 + 1)
                if t == 0 and r == 0 and first:
                    pe.wait_ge(lo_loaded, 16)
                    pe.wait_ge(gates_out, 2)
                cols = slice(r * P, (r + 1) * P)
                nc.tensor.matmul(acc_ps[r][:, :], w_dn[:, t, cols], h1_hi[:, t % HB, :], start=(t == 0), stop=False)
                nc.tensor.matmul(acc_ps[r][:, :], w_dn[:, t, cols], h1_lo[:, t % HB, :], start=False, stop=False)
                last = nc.tensor.matmul(acc_ps[r][:, :], w_dn_lo[:, t, cols], h1_hi[:, t % HB, :], start=False,
                                        stop=(t == IT - 1))
                if t == IT - 1:
                    last.then_inc(acc_ready, 1)

            def chunk(i, first, last):
                for s in range(2):
                    group_sum(i, 0, s, 0)
                for o in range(IT + LAG):
                    for kind, *which in TILE:
                        if kind == "gu" and o + (which[1] == 0) < IT:
                            group_sum(i, o + (which[1] == 0), *which)
                        if kind == "dn" and o >= LAG:
                            down(i, o - LAG, which[0], first)
                        if kind == "slot":
                            at = (o, which[0])
                            if at in TAIL_AT and not first:
                                tail(i - 1, TAIL_AT[at], i * KT + KT)
                            if at in PROD_AT and not last:
                                if PROD_AT[at] == 0:
                                    if first:
                                        pe.wait_ge(ht_done, KT)
                                    else:
                                        pe.wait_ge(rows_copied, i * TC)
                                products(i + 1, PROD_AT[at])
                            if at in TP_AT and not last:
                                transposes(i + 1, TP_AT[at])

            for t in range(TC):
                products(0, t)
            for f in range(KT):
                transposes(0, f)
            chunk(0, True, False)
            with pe.Fori(1, NC - 1) as i:
                chunk(i, False, False)
            chunk(NC - 1, False, True)
            for t in range(TC):
                tail(NC - 1, t, NC * KT, True)


def adaln_layer(nc, io):
    with ExitStack() as ctx:
        def sb(name, shape, dt=F32):
            return ctx.enter_context(nc.sbuf_tensor(name, shape, dt))

        keep = {
            "ident": sb("ident", [P, P]), "ident16": sb("ident16", [P, P], F16), "identb": sb("identb", [P, P], BF16),
            "mask_qk": sb("mask_qk", [P, P], BF16), "mask_kq": sb("mask_kq", [P, P], BF16),
            "gates": sb("gates", [P, 2, KT]), "ffn_mod": sb("ffn_mod", [P, 2, KT]),
        }
        io["w_dn_lo"] = nc.dram_tensor("w_dn_lo", [P, IT * D], F32R, kind="Internal").ap()
        for name, shape, dt in (("qk_parts", [2 * KT, 2, P, S], F16), ("v_rows", [S, D], F32), ("y_cols", [D, S], F32)):
            io[name] = nc.dram_tensor(name, shape, dt, kind="Internal").ap()
        phase_a(nc, io, keep)
        for name, shape in (("w_gu", [P, KT * GU]), ("w_dn", [P, IT * D]), ("wo_hi", [P, KT, D]), ("wo_lo", [P, KT, D])):
            keep[name] = sb(name, shape, F32R)
        phase_b(nc, io, keep)
        phase_c(nc, io, keep)


def kernel(L0_attn_x, L0_attn_w_qkv, L0_attn_b_qkv, L0_attn_w_out, L0_attn_b_out, L0_ffn_gate_up_packed,
           L0_ffn_gate_up_scales, L0_ffn_down_packed, L0_ffn_down_scales, L0_c, L0_wmod):
    import numpy as np
    from concourse import bacc
    from concourse.bass_utils import run_bass_kernel_spmd

    def nibble_order(n):
        return np.arange(n).reshape(n // P, WG, NIB).transpose(0, 2, 1).reshape(n)

    fo, ho = nibble_order(D), nibble_order(NI)
    gu_order = np.concatenate([ho, NI + ho])
    a = {k: np.asarray(v) for k, v in locals().items() if k.startswith("L0_")}
    gu = a["L0_ffn_gate_up_packed"][gu_order].T.reshape(KT, WG, GU)
    dn = a["L0_ffn_down_packed"][fo].T.reshape(IT, WG, D).transpose(1, 0, 2).reshape(WG, NG, DN).transpose(1, 0, 2)
    gus = a["L0_ffn_gate_up_scales"][:, gu_order].reshape(KT, GU // P, P).transpose(2, 1, 0).reshape(P, -1)
    arrays = {
        "x": a["L0_attn_x"].reshape(S, D)[:, fo],
        "c": a["L0_c"].reshape(D),
        "wmod": a["L0_wmod"].T.reshape(6, D, D)[:, fo].reshape(6, KT, P, D),
        "w_qkv": a["L0_attn_w_qkv"][fo].reshape(KT, P, 3 * D),
        "bias_qk": a["L0_attn_b_qkv"][:2 * D].reshape(2 * KT, P).T,
        "bias_v": a["L0_attn_b_qkv"][2 * D:],
        "w_out": a["L0_attn_w_out"][:, fo].reshape(KT, P, D),
        "b_out": a["L0_attn_b_out"][fo],
        "minus_unit": np.full((1, HG, S), -M_UNIT, np.float16),
        "packed": np.tile(np.concatenate([gu, dn], axis=2), (1, NIB, 1)),
        "scales": gus,
        "down_scales": a["L0_ffn_down_scales"][:, fo].reshape(-1),
        "shifts": (28 - 4 * (np.arange(P) // WG)).astype(np.int32).reshape(P, 1),
    }
    arrays = {k: np.ascontiguousarray(v) for k, v in arrays.items()}
    nc = bacc.Bacc("TRN2", target_bir_lowering=False, num_devices=1)
    io = {k: nc.dram_tensor(f"in_{k}", v.shape, mybir.dt.from_np(v.dtype), kind="ExternalInput").ap()
          for k, v in arrays.items()}
    io["out"] = nc.dram_tensor("out_0", (S, D), F32, kind="ExternalOutput").ap()
    adaln_layer(nc, io)
    r = run_bass_kernel_spmd(nc, [{f"in_{k}": v for k, v in arrays.items()}], core_ids=[0])
    out = np.empty((1, S, D), np.float32)
    out[0][:, fo] = r.results[0]["out_0"].reshape(S, D)
    return out
```
